# Optimizing a Trainium2 kernel written in Bass

```python
import numpy as np
import jax
import jax.numpy as jnp

def _softmax(x, axis=-1):
    return jax.nn.softmax(x, axis=axis)

def _gelu(x):
    return jax.nn.gelu(x, approximate=True)

def _silu(x):
    return jax.nn.silu(x)

def _sigmoid(x):
    return jax.nn.sigmoid(x)

def _layernorm(x, axis=-1, eps=1e-05):
    m = jnp.mean(x, axis=axis, keepdims=True)
    v = jnp.var(x, axis=axis, keepdims=True)
    return (x - m) / jnp.sqrt(v + eps)

def _scatter_add(tgt, idx, src, axis=0):
    return tgt.at[idx].add(src)

def _segment_sum(src, seg, n):
    return jax.ops.segment_sum(src, seg, n)
kernel_name = 'mk_audio_tower_d1_tok_audfeat1024_r4_acee5c'

def setup_inputs(seed: int=0):
    np.random.seed(seed)
    _w = jnp.asarray

    def _rec_inputs():
        import jax
        import jax.numpy as jnp
        _rk = jax.random.key(seed)
        x = -0.000125008 + 0.999885 * jax.random.normal(jax.random.fold_in(_rk, 1), (128, 125, 256), jnp.float32)
        return x
    x = _rec_inputs()

    def _L0_tok_setup():
        import jax, jax.numpy as jnp
        import numpy as np
        H = 32
        DECAY = 0.9
        key = jax.random.key(seed)
        ks = jax.random.split(key, 6)
        B, T, D = (8, 1024, 256)
        x = jax.random.normal(ks[0], (B, T, D), dtype=jnp.float32)
        s = 1.0 / np.sqrt(D)
        Wv = jax.random.normal(ks[1], (D, D), dtype=jnp.float32) * s
        bv = jax.random.normal(ks[2], (D,), dtype=jnp.float32) * s
        Wo = jax.random.normal(ks[3], (D, D), dtype=jnp.float32) * s
        bo = jax.random.normal(ks[4], (D,), dtype=jnp.float32) * s
        w = jnp.asarray(DECAY ** np.arange(H), dtype=jnp.float32)
        decay_w = w / jnp.sum(w)
        return {'x': x, 'Wv': Wv, 'bv': bv, 'Wo': Wo, 'bo': bo, 'decay_w': decay_w}
    _L0_tok_all = _L0_tok_setup()
    _L0_tok_in = {k: v for k, v in _L0_tok_all.items() if k in ('Wv', 'bv', 'Wo', 'bo', 'decay_w')}
    del _L0_tok_all

    def _L0_attn_setup():
        import jax, jax.numpy as jnp
        import numpy as np
        import math
        H = 256
        NHALF = 32
        B = 4
        L = 1024
        DT_MIN, DT_MAX = (0.001, 0.1)

        def _kernel(log_dt, log_A_real, A_imag, C, L_len):
            dt = jnp.exp(log_dt)
            A = -jnp.exp(log_A_real) + 1j * A_imag
            Cc = C[..., 0] + 1j * C[..., 1]
            dtA = A * dt[:, None]
            Cw = Cc * (jnp.exp(dtA) - 1.0) / A
            l = jnp.arange(L_len)
            vand = jnp.exp(dtA[..., None] * l)
            K = 2.0 * jnp.einsum('hn,hnl->hl', Cw, vand).real
            return K
        key = jax.random.key(seed)
        k_x, k_dt, k_c, k_d = jax.random.split(key, 4)
        x = jax.random.normal(k_x, (B, L, H), dtype=jnp.float32)
        log_dt = jax.random.uniform(k_dt, (H,), dtype=jnp.float32) * (math.log(DT_MAX) - math.log(DT_MIN)) + math.log(DT_MIN)
        log_A_real = jnp.log(0.5 * jnp.ones((H, NHALF), dtype=jnp.float32))
        A_imag = math.pi * jnp.broadcast_to(jnp.arange(NHALF, dtype=jnp.float32), (H, NHALF))
        C = jax.random.normal(k_c, (H, NHALF, 2), dtype=jnp.float32) / math.sqrt(NHALF)
        D = jax.random.normal(k_d, (H,), dtype=jnp.float32)
        return {'x': x, 'log_dt': log_dt, 'log_A_real': log_A_real, 'A_imag': A_imag, 'C': C, 'D': D}
    _L0_attn_all = _L0_attn_setup()
    _L0_attn_in = {k: v for k, v in _L0_attn_all.items() if k in ('log_dt', 'log_A_real', 'A_imag', 'C', 'D')}
    del _L0_attn_all

    def _L0_ffn_setup():
        import jax, jax.numpy as jnp
        import numpy as np
        N_EMBD = 256
        N_EXPERTS = 8
        TOP_K = 2
        CAPACITY_FACTOR = 1.25
        key = jax.random.key(seed)
        ks = jax.random.split(key, 8)
        B, T, C, E, H = (8, 512, N_EMBD, N_EXPERTS, 4 * N_EMBD)
        w = lambda k, shape: jax.random.normal(k, shape, jnp.float32) * 0.02
        return {'x': jax.random.normal(ks[0], (B, T, C), jnp.float32), 'rW1': w(ks[1], (C, H)), 'rb1': jnp.zeros((H,), jnp.float32), 'rW2': w(ks[2], (H, H)), 'rb2': jnp.zeros((H,), jnp.float32), 'rW3': w(ks[3], (H, E)), 'rb3': jnp.zeros((E,), jnp.float32), 'eW1': w(ks[4], (E, C, H)), 'eb1': jnp.zeros((E, H), jnp.float32), 'eW2': w(ks[5], (E, H, C)), 'eb2': jnp.zeros((E, C), jnp.float32)}
    _L0_ffn_all = _L0_ffn_setup()
    _L0_ffn_in = {k: v for k, v in _L0_ffn_all.items() if k in ('rW1', 'rb1', 'rW2', 'rb2', 'rW3', 'rb3', 'eW1', 'eb1', 'eW2', 'eb2')}
    del _L0_ffn_all
    return {'x': x, 'L0_tok_Wv': _L0_tok_in['Wv'], 'L0_tok_bv': _L0_tok_in['bv'], 'L0_tok_Wo': _L0_tok_in['Wo'], 'L0_tok_bo': _L0_tok_in['bo'], 'L0_tok_decay_w': _L0_tok_in['decay_w'], 'L0_attn_log_dt': _L0_attn_in['log_dt'], 'L0_attn_log_A_real': _L0_attn_in['log_A_real'], 'L0_attn_A_imag': _L0_attn_in['A_imag'], 'L0_attn_C': _L0_attn_in['C'], 'L0_attn_D': _L0_attn_in['D'], 'L0_ffn_rW1': _L0_ffn_in['rW1'], 'L0_ffn_rb1': _L0_ffn_in['rb1'], 'L0_ffn_rW2': _L0_ffn_in['rW2'], 'L0_ffn_rb2': _L0_ffn_in['rb2'], 'L0_ffn_rW3': _L0_ffn_in['rW3'], 'L0_ffn_rb3': _L0_ffn_in['rb3'], 'L0_ffn_eW1': _L0_ffn_in['eW1'], 'L0_ffn_eb1': _L0_ffn_in['eb1'], 'L0_ffn_eW2': _L0_ffn_in['eW2'], 'L0_ffn_eb2': _L0_ffn_in['eb2']}

def reference(x, L0_tok_Wv, L0_tok_bv, L0_tok_Wo, L0_tok_bo, L0_tok_decay_w, L0_attn_log_dt, L0_attn_log_A_real, L0_attn_A_imag, L0_attn_C, L0_attn_D, L0_ffn_rW1, L0_ffn_rb1, L0_ffn_rW2, L0_ffn_rb2, L0_ffn_rW3, L0_ffn_rb3, L0_ffn_eW1, L0_ffn_eb1, L0_ffn_eW2, L0_ffn_eb2):
    import jax
    import jax.numpy as jnp

    def _L0_tok_ref(x, Wv, bv, Wo, bo, decay_w):
        import jax, jax.numpy as jnp
        import numpy as np
        H = 32
        DECAY = 0.9
        B, T, D = x.shape
        Hlen = decay_w.shape[0]
        x_pad = jnp.pad(x, ((0, 0), (Hlen, 0), (0, 0)))
        kernel = jnp.broadcast_to(decay_w[:, None, None], (Hlen, 1, D))
        s = jax.lax.conv_general_dilated(x_pad, kernel, window_strides=(1,), padding='VALID', dimension_numbers=('NWC', 'WIO', 'NWC'), feature_group_count=D)
        attended = s @ Wv.T + bv * jnp.sum(decay_w)
        return attended @ Wo.T + bo

    def _L0_attn_ref(x, log_dt, log_A_real, A_imag, C, D):
        import jax, jax.numpy as jnp
        import numpy as np
        import math
        H = 256
        NHALF = 32
        B = 4
        L = 1024
        DT_MIN, DT_MAX = (0.001, 0.1)

        def _kernel(log_dt, log_A_real, A_imag, C, L_len):
            dt = jnp.exp(log_dt)
            A = -jnp.exp(log_A_real) + 1j * A_imag
            Cc = C[..., 0] + 1j * C[..., 1]
            dtA = A * dt[:, None]
            Cw = Cc * (jnp.exp(dtA) - 1.0) / A
            l = jnp.arange(L_len)
            vand = jnp.exp(dtA[..., None] * l)
            K = 2.0 * jnp.einsum('hn,hnl->hl', Cw, vand).real
            return K
        xt = jnp.swapaxes(x, -1, -2)
        Lc = xt.shape[-1]
        K = _kernel(log_dt, log_A_real, A_imag, C, Lc)
        n = 2 * Lc
        Kf = jnp.fft.rfft(K.astype(jnp.float32), n=n)
        xf = jnp.fft.rfft(xt.astype(jnp.float32), n=n)
        y = jnp.fft.irfft(xf * Kf, n=n)[..., :Lc]
        y = y + xt * D[:, None]
        return jnp.swapaxes(y, -1, -2).astype(x.dtype)

    def _L0_ffn_ref(x, rW1, rb1, rW2, rb2, rW3, rb3, eW1, eb1, eW2, eb2):
        import jax, jax.numpy as jnp
        import numpy as np
        N_EMBD = 256
        N_EXPERTS = 8
        TOP_K = 2
        CAPACITY_FACTOR = 1.25
        B, T, C = x.shape
        E = rb3.shape[0]
        k = TOP_K
        capacity = int(T / E * CAPACITY_FACTOR)
        h = jax.nn.relu(x @ rW1 + rb1)
        h = jax.nn.relu(h @ rW2 + rb2)
        scales = jax.nn.softmax(h @ rW3 + rb3, axis=-1)
        topk_scales, topk_experts = jax.lax.top_k(scales, k)
        e_flat = topk_experts.reshape(B, T * k)
        onehot = jax.nn.one_hot(e_flat, E, dtype=jnp.int32)
        pos_excl = jnp.cumsum(onehot, axis=1) - onehot
        pos = jnp.take_along_axis(pos_excl, e_flat[..., None], axis=-1)[..., 0]
        keep = pos < capacity
        pos_c = jnp.where(keep, pos, capacity)
        b_idx = jnp.broadcast_to(jnp.arange(B)[:, None], (B, T * k))
        x_rep = jnp.repeat(x, k, axis=1)
        dispatched = jnp.zeros((E, B, capacity, C), x.dtype)
        dispatched = dispatched.at[e_flat, b_idx, pos_c].set(jnp.where(keep[..., None], x_rep, 0.0), mode='drop')
        hh = jax.nn.relu(jnp.einsum('ebnc,ech->ebnh', dispatched, eW1) + eb1[:, None, None, :])
        eout = jnp.einsum('ebnh,ehc->ebnc', hh, eW2) + eb2[:, None, None, :]
        gathered = eout[e_flat, b_idx, pos_c]
        gathered = jnp.where(keep[..., None], gathered, 0.0).reshape(B, T, k, C)
        out = jnp.sum(topk_scales[..., None] * gathered, axis=2)
        return out
    h = _L0_tok_ref(x, L0_tok_Wv, L0_tok_bv, L0_tok_Wo, L0_tok_bo, L0_tok_decay_w)
    h = h + _L0_attn_ref(_layernorm(h, axis=-1), L0_attn_log_dt, L0_attn_log_A_real, L0_attn_A_imag, L0_attn_C, L0_attn_D)
    h = h + _L0_ffn_ref(_layernorm(h, axis=-1), L0_ffn_rW1, L0_ffn_rb1, L0_ffn_rW2, L0_ffn_rb2, L0_ffn_rW3, L0_ffn_rb3, L0_ffn_eW1, L0_ffn_eb1, L0_ffn_eW2, L0_ffn_eb2)
    return h

_drawn_inputs = setup_inputs


def setup_inputs(seed=0):
    import zlib

    import numpy as np

    out = dict(_drawn_inputs(seed))
    spreads = {'L0_attn_log_A_real': (-0.6931471824645996, 0.6),
     'L0_ffn_rb1': (0.0, 0.601),
     'L0_ffn_rb2': (0.0, 0.441),
     'L0_ffn_rb3': (0.0, 0.49),
     'L0_ffn_eb1': (0.0, 0.8),
     'L0_ffn_eb2': (0.0, 0.703)}
    factors = {'L0_ffn_rW1': 3.397,
     'L0_ffn_rW2': 3.206,
     'L0_ffn_rW3': 3.06,
     'L0_ffn_eW1': 4.029,
     'L0_ffn_eW2': 3.139}
    for name, (base, spread) in spreads.items():
        noise = np.random.default_rng([zlib.crc32(name.encode()), seed]).standard_normal(out[name].shape)
        drawn = base * np.exp(spread * noise) if base else spread * noise
        out[name] = jnp.asarray(drawn.astype(out[name].dtype))
    for name, factor in factors.items():
        out[name] = (out[name] * factor).astype(out[name].dtype)
    return out
```

```python
from contextlib import ExitStack

import concourse.bass as bass
from concourse import mybir

F32 = mybir.dt.float32
F32R = mybir.dt.float32r
BF16 = mybir.dt.bfloat16
I32 = mybir.dt.int32
ALU = mybir.AluOpType
ACT = mybir.ActivationFunctionType
AX = mybir.AxisListType.X

P = 128
B, TIN, C = 128, 125, 256
T = TIN + 1
TAPS = 32
NM = 32
CC = C // P
HID = 1024
HC = HID // P
E = 8
CAP = int(T / E * 1.25)
SL = E * CAP
HSL = SL // 2
EPS = 1e-5

GB = 4
NG = B // GB
GT = GB * T
PAIRS = B // 2
STEP = 4
TURNS = PAIRS // STEP
LPAD = 256

LOG2E = 1.4426950408889634
LN2_HI = 0.693145751953125
LN2_LO = 1.4286068203094172e-06
ROUND = 12582912.0
TWO_PI = 6.283185307179586
PI2_A = 6.28125
PI2_B = 0.0019350051879882812
PI2_C = 3.019915981956753e-07
PI_BELOW = 3.1415925


def wait(eng, sem, value):
    if isinstance(value, int) and value <= 0:
        return
    eng.wait_ge(sem, value)


def wait_apart(eng, sem, value, passed):
    wait(eng, sem, value)
    if not isinstance(value, int):
        eng.sem_inc(passed, 1)


class Chain:

    def __init__(self, eng, sem, base=0):
        self.eng, self.sem, self.base, self.n = eng, sem, base, 0

    def step(self, ins):
        ins.then_inc(self.sem, 1)
        self.n += 1
        self.eng.wait_ge(self.sem, self.base + self.n)


def split(chain, eng, hi, lo, src):
    chain.step(eng.tensor_copy(hi, src))
    chain.step(eng.tensor_tensor(lo, src, hi.bitcast(F32), ALU.subtract))


def matmul3(pe, out, w_hi, w_lo, x_hi, x_lo, start, stop):
    pe.matmul(out, w_hi, x_hi, start=start, stop=False)
    pe.matmul(out, w_hi, x_lo, start=False, stop=False)
    return pe.matmul(out, w_lo, x_hi, start=False, stop=stop)


def exp_steps(ch, dve, x, t, k, r, p, scale_bits):
    ch.step(dve.tensor_scalar(t, x, LOG2E, ROUND, ALU.mult, ALU.add))
    ch.step(dve.tensor_scalar(k, t, -ROUND, None, ALU.add))
    ch.step(dve.tensor_scalar(k, k, 127.0, -126.0, ALU.min, ALU.max))
    ch.step(dve.scalar_tensor_tensor(r, k, -LN2_HI, x, ALU.mult, ALU.add))
    ch.step(dve.scalar_tensor_tensor(r, k, -LN2_LO, r, ALU.mult, ALU.add))
    ch.step(dve.tensor_scalar(p, r, 1.0 / 5040.0, None, ALU.mult))
    for fact in (720.0, 120.0, 24.0, 6.0, 2.0, 1.0):
        ch.step(dve.scalar_tensor_tensor(p, p, 1.0 / fact, r, ALU.add, ALU.mult))
    ch.step(dve.tensor_scalar(scale_bits, k, 127.0, 8388608.0, ALU.add, ALU.mult))
    ch.step(dve.scalar_tensor_tensor(p, p, 1.0, scale_bits.bitcast(F32), ALU.add, ALU.mult))


def rstd_steps(ch, dve, var_in, var, y, t):
    ch.step(dve.tensor_scalar(var, var_in, EPS, None, ALU.add))
    ch.step(dve.tensor_scalar(y.bitcast(I32), var.bitcast(I32), -0.5, 1597463007.0, ALU.mult, ALU.add))
    for _ in range(3):
        ch.step(dve.tensor_tensor(t, y, y, ALU.mult))
        ch.step(dve.scalar_tensor_tensor(t, t, -0.5, var, ALU.mult, ALU.mult))
        ch.step(dve.scalar_tensor_tensor(y, t, 1.5, y, ALU.add, ALU.mult))


RSTD_STEPS = 2 + 3 * 3


def phase_tokens(nc, A, scratch, xn):
    h1_dram, kern_dram, taps_dram = scratch["h1"], scratch["kern"], scratch["taps"]
    with ExitStack() as ctx:
        def sb(name, shape, dt=F32):
            return ctx.enter_context(nc.sbuf_tensor(name, shape, dt))

        def sem(name):
            return ctx.enter_context(nc.semaphore(name))

        ident = sb("a_ident", [P, P])
        ones = sb("a_ones", [P, P])
        tap_row = sb("tap_row", [1, LPAD])
        tap_all = sb("tap_all", [P, TAPS])
        tap_sum = sb("tap_sum", [P, 1])
        conv_rev = sb("conv_rev", [TIN, T])
        conv = sb("conv", [TIN, T])
        wv = sb("wv", [P, CC, C])
        wo = sb("wo", [P, CC, C])
        woT = sb("woT", [P, CC, C])
        bv = sb("bv", [P, CC])
        bv_sum = sb("bv_sum", [P, CC])
        bv_rows = sb("bv_rows", [P, CC, T])
        bo_row = sb("bo_row", [1, C])
        bias1 = sb("bias1", [T, C])
        w_hi = sb("w_hi", [P, CC, C], F32R)
        w_lo = sb("w_lo", [P, CC, C], F32R)

        x_in = sb("x_in", [TIN, STEP, 2, C])
        s_hi = sb("s_hi", [P, STEP, 2 * CC * T], F32R)
        s_lo = sb("s_lo", [P, STEP, 2 * CC * T], F32R)
        h1 = sb("h1", [T, STEP, 2, C])
        stats = sb("stats", [T, 2 * STEP, 6])
        mv = sb("mv", [T, 2 * STEP, 2])
        var = sb("var", [T, 2 * STEP])
        rstd = sb("rstd", [T, 2 * STEP])
        newton = sb("newton", [T, 2 * STEP])
        shift = sb("shift", [T, 2 * STEP])

        logs = sb("logs", [P, 2 + CC * NM])
        exps = sb("exps", [P, 2 + CC * NM])
        a_im = sb("a_im", [P, CC, NM])
        c_in = sb("c_in", [P, CC, NM, 2])
        d_skip = sb("d_skip", [P, CC])
        s0 = sb("s0", [P, 2 + CC * NM])
        s1 = sb("s1", [P, 2 + CC * NM])
        s2 = sb("s2", [P, 2 + CC * NM])
        s3 = sb("s3", [P, 2 + CC * NM], I32)
        g = {n: sb("g_" + n, [P, CC, NM]) for n in
             ("are", "xr", "yi", "mag", "sin", "cos", "zr", "zi", "den", "ir", "ii", "cr", "ci", "t", "u")}
        NA, NB = 8, 16
        vr = sb("vr", [P, CC, NB, NM])
        vi = sb("vi", [P, CC, NB, NM])
        ur = sb("ur", [P, CC, NA, NM])
        ui = sb("ui", [P, CC, NA, NM])
        pr = [sb(f"pr{n}", [P, CC, NM]) for n in range(2)]
        pi = [sb(f"pi{n}", [P, CC, NM]) for n in range(2)]
        q0 = sb("q0", [P, CC, NB // 2, NM])
        AH = NA // 4
        prod = sb("prod", [P, AH, NB, NM])
        prod2 = sb("prod2", [P, AH, NB, NM])
        kern = sb("kern", [P, CC, LPAD])

        ps_s = [ctx.enter_context(nc.psum_tensor(f"ps_s{n}", [P, 512], F32)) for n in range(2)]
        ps_h = [ctx.enter_context(nc.psum_tensor(f"ps_h{n}", [P, 512], F32)) for n in range(2)]
        ps_w = [ctx.enter_context(nc.psum_tensor(f"ps_w{n}", [P, 512], F32)) for n in range(2)]
        ps_b = ctx.enter_context(nc.psum_tensor("ps_b", [P, 512], F32))

        consts_made = sem("consts_made")
        taps_in = sem("taps_in")
        taps_out = sem("taps_out")
        conv_in = sem("conv_in")
        weights_in = sem("weights_in")
        modes_in = sem("modes_in")
        woT_done = sem("woT_done")
        woT_copied = sem("woT_copied")
        w_done = sem("w_done")
        setup = sem("a_setup")
        setup_pool = sem("a_setup_pool")
        weights_ready = sem("weights_ready")
        angles_ready = sem("angles_ready")
        sines_ready = sem("sines_ready")
        modes_ready = sem("modes_ready")
        kern_ready = sem("kern_ready")
        kern_out = sem("kern_out")
        x_loaded = [sem(f"x_loaded{k}") for k in range(STEP)]
        h1_stored = [sem(f"h1_stored{k}") for k in range(STEP)]
        conv_done = sem("conv_done")
        s_hi_ready = sem("s_hi_ready")
        s_lo_ready = sem("s_lo_ready")
        proj_done = sem("proj_done")
        h1_ready = sem("h1_ready")
        stats_done = sem("stats_done")
        aggr_done = sem("aggr_done")
        rstd_chain = sem("rstd_chain")
        norm_ready = sem("norm_ready")
        norm_done = sem("norm_done")
        passed_act = sem("a_passed_act")
        passed_dve = sem("a_passed_dve")

        def load_x(sp, u, k):
            sp.dma_start(x_in[:, k], A["x"][bass.ds(2 * u, 2)].rearrange("b t c -> t b c"))\
              .then_inc(x_loaded[k], 16)

        block = ctx.enter_context(nc.Block())

        @block.sync
        def _(sp):
            sp.wait_ge(consts_made, 1)
            sp.dma_start(tap_row[0:1, TIN - TAPS:TIN], A["L0_tok_decay_w"].rearrange("(a n) -> a n", a=1))\
              .then_inc(taps_in, 16)
            for k in range(STEP):
                load_x(sp, k, k)
            sp.dma_start(wv[:], A["L0_tok_Wv"].rearrange("(k p) n -> p k n", p=P)).then_inc(weights_in, 16)
            sp.dma_start(wo[:], A["L0_tok_Wo"].rearrange("(k p) n -> p k n", p=P)).then_inc(weights_in, 16)
            sp.wait_ge(taps_in, 16)
            sp.dma_start(taps_dram, tap_row[:]).then_inc(taps_out, 16)
            sp.dma_start(bo_row[:], A["L0_tok_bo"].rearrange("(a n) -> a n", a=1)).then_inc(weights_in, 16)
            sp.dma_start(tap_all[:], bass.AP(A["L0_tok_decay_w"].tensor, 0, [[0, P], [1, TAPS]]))\
              .then_inc(weights_in, 16)
            sp.wait_ge(taps_out, 16)
            sp.dma_start(conv_rev[:], bass.AP(taps_dram.tensor, 0, [[1, TIN], [1, T]])).then_inc(conv_in, 16)

            def turn(i, load=True, store=True):
                for k in range(STEP):
                    if store:
                        v = (i - 1) * STEP + k
                        wait(sp, h1_ready, v + 1)
                        sp.dma_start(h1_dram[:, bass.ds(2 * v, 2), :], h1[:, k]).then_inc(h1_stored[k], 16)
                    if load:
                        wait(sp, conv_done, i * STEP + k + 1)
                        load_x(sp, (i + 1) * STEP + k, k)

            turn(0, store=False)
            with sp.Fori(1, TURNS - 1) as i:
                turn(i)
            turn(TURNS - 1, load=False)
            turn(TURNS, load=False)
            for k in range(STEP):
                sp.wait_ge(h1_stored[k], 16 * TURNS)
            sp.wait_ge(kern_out, 16)

        @block.gpsimd
        def _(pool):
            pool.memset(tap_row[:], 0.0).then_inc(consts_made, 1)
            pool.memset(ident[:], 0.0).then_inc(setup_pool, 1)
            pool.memset(ones[:], 1.0).then_inc(consts_made, 1)
            pool.wait_ge(setup_pool, 1)
            pool.affine_select(out=ident[:], in_=ident[:], compare_op=ALU.not_equal, fill=1.0, base=0,
                               pattern=[[-1, P]], channel_multiplier=1).then_inc(consts_made, 1)
            pool.memset(kern[:], 0.0).then_inc(setup_pool, 1)
            ch = Chain(pool, setup_pool, 2)
            pool.wait_ge(setup_pool, 2)
            pool.wait_ge(modes_ready, 1)

            def cmul(outr, outi, xr, xi, yr, yi, tmp):
                ch.step(pool.tensor_tensor(outr, xr, yr, ALU.mult))
                ch.step(pool.tensor_tensor(tmp, xi, yi, ALU.mult))
                ch.step(pool.tensor_tensor(outr, outr, tmp, ALU.subtract))
                ch.step(pool.tensor_tensor(outi, xr, yi, ALU.mult))
                ch.step(pool.tensor_tensor(tmp, xi, yr, ALU.mult))
                ch.step(pool.tensor_tensor(outi, outi, tmp, ALU.add))

            def wide(x, m):
                return x[:].rearrange("p g (o n) -> p g o n", o=1).to_broadcast((P, CC, m, NM))

            ch.step(pool.memset(vr[:, :, NB - 1, :], 1.0))
            ch.step(pool.memset(vi[:, :, NB - 1, :], 0.0))
            zr, zi = g["zr"], g["zi"]
            m, at = 1, 0
            while m < NB:
                lo, mid = NB - 2 * m, NB - m
                if m == 1:
                    ch.step(pool.tensor_copy(vr[:, :, lo, :], zr[:]))
                    ch.step(pool.tensor_copy(vi[:, :, lo, :], zi[:]))
                else:
                    cmul(vr[:, :, lo:mid, :], vi[:, :, lo:mid, :], vr[:, :, mid:NB, :], vi[:, :, mid:NB, :],
                         wide(zr, m), wide(zi, m), q0[:, :, 0:m, :])
                cmul(pr[at][:], pi[at][:], zr[:], zi[:], zr[:], zi[:], q0[:, :, 0, :])
                zr, zi, at, m = pr[at], pi[at], 1 - at, 2 * m
            ch.step(pool.tensor_copy(ur[:, :, NA - 1, :], g["cr"][:]))
            ch.step(pool.tensor_copy(ui[:, :, NA - 1, :], g["ci"][:]))
            m = 1
            while m < NA:
                lo, mid = NA - 2 * m, NA - m
                cmul(ur[:, :, lo:mid, :], ui[:, :, lo:mid, :], ur[:, :, mid:NA, :], ui[:, :, mid:NA, :],
                     wide(zr, m), wide(zi, m), q0[:, :, 0:m, :])
                if 2 * m < NA:
                    cmul(pr[at][:], pi[at][:], zr[:], zi[:], zr[:], zi[:], q0[:, :, 0, :])
                    zr, zi, at = pr[at], pi[at], 1 - at
                m *= 2
            for c in range(CC):
                for a in range(0, NA, AH):
                    def u_of(x):
                        return x[:, c, a:a + AH, :].rearrange("p a (o n) -> p a o n", o=1)\
                                                   .to_broadcast((P, AH, NB, NM))

                    def v_of(x):
                        return x[:, c, :, :].rearrange("p (o b) n -> p o b n", o=1).to_broadcast((P, AH, NB, NM))

                    ch.step(pool.tensor_tensor(prod[:], u_of(ur), v_of(vr), ALU.mult))
                    ch.step(pool.tensor_tensor(prod2[:], u_of(ui), v_of(vi), ALU.mult))
                    ch.step(pool.tensor_tensor(prod[:], prod[:], prod2[:], ALU.subtract))
                    n = NM // 2
                    while n > 1:
                        ch.step(pool.tensor_tensor(prod[:, :, :, 0:n], prod[:, :, :, 0:n], prod[:, :, :, n:2 * n],
                                                   ALU.add))
                        n //= 2
                    ch.step(pool.tensor_tensor(
                        kern[:, c, NB * a:NB * (a + AH)].rearrange("p (a b) -> p a b", a=AH),
                        prod[:, :, :, 0], prod[:, :, :, 1], ALU.add))
            for c in range(CC):
                last = pool.tensor_tensor(kern[:, c, 127:128], kern[:, c, 127:128], d_skip[:, c:c + 1], ALU.add)
                ch.step(last)
            pool.dma_start(kern_dram.rearrange("(c p) l -> p c l", p=P)[:, :, 0:2 * T],
                           kern[:, :, P - T:P + T]).then_inc(kern_out, 16)

        @block.scalar
        def _(act):
            act.dma_start(logs[:, 0:2], A["L0_attn_log_dt"].rearrange("(c p) -> p c", p=P),
                          allow_slow_non_contiguous=True).then_inc(modes_in, 16)
            act.dma_start(logs[:, 2:2 + CC * NM].rearrange("p (c n) -> p c n", c=CC),
                          A["L0_attn_log_A_real"].rearrange("(c p) n -> p c n", p=P)).then_inc(modes_in, 16)
            act.dma_start(a_im[:], A["L0_attn_A_imag"].rearrange("(c p) n -> p c n", p=P)).then_inc(modes_in, 16)
            act.dma_start(c_in[:], A["L0_attn_C"].rearrange("(c p) n r -> p c n r", p=P)).then_inc(modes_in, 16)
            act.dma_start(d_skip[:], A["L0_attn_D"].rearrange("(c p) -> p c", p=P),
                          allow_slow_non_contiguous=True).then_inc(modes_in, 16)
            act.dma_start(bv[:], A["L0_tok_bv"].rearrange("(c p) -> p c", p=P),
                          allow_slow_non_contiguous=True).then_inc(weights_in, 16)
            act.wait_ge(angles_ready, 1)
            act.activation(g["sin"][:], g["yi"][:], ACT.Sin).then_inc(sines_ready, 1)
            act.activation(g["cos"][:], g["t"][:], ACT.Sin).then_inc(sines_ready, 1)

            def turn(i, conv=True, norm=True):
                for k in range(STEP):
                    if conv:
                        u = i * STEP + k
                        act.wait_ge(conv_done, u + 1)
                        wait(act, proj_done, u - STEP + 1)
                        act.activation(s_hi[:, k], ps_s[k % 2][:, 0:2 * CC * T], ACT.Copy).then_inc(s_hi_ready, 1)
                    if norm:
                        v = (i - 2) * STEP + k
                        wait_apart(act, norm_ready, i - 1, passed_act)
                        for j in range(2):
                            n = 2 * k + j
                            act.activation(xn[:, bass.ds(2 * v + j, 1), :].rearrange("p o c -> p (o c)"), h1[:, k, j], ACT.Identity,
                                           bias=shift[:, n:n + 1], scale=rstd[:, n:n + 1]).then_inc(norm_done, 1)

            turn(0, norm=False)
            turn(1, norm=False)
            with act.Fori(2, TURNS) as i:
                turn(i)
            turn(TURNS, conv=False)
            turn(TURNS + 1, conv=False)

        @block.vector
        def _(dve):
            ch = Chain(dve, setup)
            dve.wait_ge(weights_in, 80)
            ch.step(dve.reduce_sum(tap_sum[:], tap_all[:], AX))
            ch.step(dve.tensor_scalar(bv_sum[:], bv[:], tap_sum[:, 0:1], None, ALU.mult))
            dve.wait_ge(consts_made, 3)
            for c in range(CC):
                ch.step(dve.tensor_scalar(bv_rows[:, c, :], ones[:, 0:T], bv_sum[:, c:c + 1], None, ALU.mult))
            dve.wait_ge(woT_done, 1)
            for c in range(CC):
                dve.tensor_copy(woT[:, c, :], ps_w[c][:, 0:C]).then_inc(woT_copied, 1)
            dve.wait_ge(conv_in, 16)
            dve.tensor_copy(conv[:], conv_rev[:, ::-1]).then_inc(weights_ready, 1)
            dve.wait_ge(w_done, 1)
            for c in range(CC):
                split(ch, dve, w_hi[:, c, :], w_lo[:, c, :], ps_w[c][:, 0:C])
            dve.tensor_copy(bias1[:], ps_b[0:T, 0:C]).then_inc(weights_ready, 1)

            dve.wait_ge(modes_in, 80)
            exp_steps(ch, dve, logs[:], s0[:], s1[:], s2[:], exps[:], s3[:])
            m = {n: x[:].rearrange("p c n -> p (c n)") for n, x in g.items()}
            for c in range(CC):
                ch.step(dve.tensor_scalar(g["are"][:, c, :], exps[:, 2 + c * NM:2 + (c + 1) * NM], -1.0, None, ALU.mult))
                ch.step(dve.tensor_scalar(g["xr"][:, c, :], g["are"][:, c, :], exps[:, c:c + 1], None, ALU.mult))
                ch.step(dve.tensor_scalar(g["yi"][:, c, :], a_im[:, c, :], exps[:, c:c + 1], None, ALU.mult))
            n = CC * NM
            ch.step(dve.tensor_scalar(m["t"], m["yi"], 1.0 / TWO_PI, ROUND, ALU.mult, ALU.add))
            ch.step(dve.tensor_scalar(m["t"], m["t"], -ROUND, None, ALU.add))
            for part in (PI2_A, PI2_B, PI2_C):
                ch.step(dve.scalar_tensor_tensor(m["yi"], m["t"], -part, m["yi"], ALU.mult, ALU.add))
            ch.step(dve.tensor_scalar(m["yi"], m["yi"], PI_BELOW, -PI_BELOW, ALU.min, ALU.max))
            ch.step(dve.tensor_scalar(m["u"], m["yi"], -1.0, None, ALU.mult))
            ch.step(dve.tensor_tensor(m["u"], m["u"], m["yi"], ALU.max))
            ch.step(dve.tensor_scalar(m["t"], m["u"], -1.0, TWO_PI / 4, ALU.mult, ALU.add))
            ch.step(dve.tensor_copy(m["u"], m["t"]))
            dve.sem_inc(angles_ready, 1)
            exp_steps(ch, dve, m["xr"], s0[:, 0:n], s1[:, 0:n], s2[:, 0:n], m["mag"], s3[:, 0:n])
            im = a_im[:].rearrange("p c n -> p (c n)")
            ch.step(dve.tensor_tensor(m["den"], m["are"], m["are"], ALU.mult))
            ch.step(dve.tensor_tensor(m["u"], im, im, ALU.mult))
            ch.step(dve.tensor_tensor(m["den"], m["den"], m["u"], ALU.add))
            ch.step(dve.reciprocal(m["u"], m["den"]))
            ch.step(dve.tensor_tensor(m["ir"], m["are"], m["u"], ALU.mult))
            ch.step(dve.scalar_tensor_tensor(m["ii"], im, -1.0, m["u"], ALU.mult, ALU.mult))
            dve.wait_ge(sines_ready, 2)
            ch.step(dve.tensor_tensor(m["zr"], m["mag"], m["cos"], ALU.mult))
            ch.step(dve.tensor_tensor(m["zi"], m["mag"], m["sin"], ALU.mult))
            ch.step(dve.tensor_scalar(m["mag"], m["zr"], -1.0, None, ALU.add))
            ch.step(dve.tensor_tensor(m["den"], m["mag"], m["ir"], ALU.mult))
            ch.step(dve.tensor_tensor(m["t"], m["zi"], m["ii"], ALU.mult))
            ch.step(dve.tensor_tensor(m["den"], m["den"], m["t"], ALU.subtract))
            ch.step(dve.tensor_tensor(m["u"], m["mag"], m["ii"], ALU.mult))
            ch.step(dve.tensor_tensor(m["t"], m["zi"], m["ir"], ALU.mult))
            ch.step(dve.tensor_tensor(m["u"], m["u"], m["t"], ALU.add))
            c_re = c_in[:].rearrange("p c n r -> p (c n) r")[:, :, 0]
            c_im = c_in[:].rearrange("p c n r -> p (c n) r")[:, :, 1]
            ch.step(dve.tensor_tensor(m["cr"], m["den"], c_re, ALU.mult))
            ch.step(dve.tensor_tensor(m["t"], m["u"], c_im, ALU.mult))
            ch.step(dve.tensor_tensor(m["cr"], m["cr"], m["t"], ALU.subtract))
            ch.step(dve.tensor_scalar(m["cr"], m["cr"], 2.0, None, ALU.mult))
            ch.step(dve.tensor_tensor(m["ci"], m["den"], c_im, ALU.mult))
            ch.step(dve.tensor_tensor(m["t"], m["u"], c_re, ALU.mult))
            ch.step(dve.tensor_tensor(m["ci"], m["ci"], m["t"], ALU.add))
            dve.tensor_scalar(m["ci"], m["ci"], 2.0, None, ALU.mult).then_inc(modes_ready, 1)

            def turn(i, conv=True, proj=True):
                for k in range(STEP):
                    if conv:
                        u = i * STEP + k
                        dve.wait_ge(s_hi_ready, u + 1)
                        dve.tensor_tensor(s_lo[:, k], ps_s[k % 2][:, 0:2 * CC * T], s_hi[:, k].bitcast(F32),
                                          ALU.subtract).then_inc(s_lo_ready, 1)
                    if proj:
                        v = (i - 1) * STEP + k
                        dve.wait_ge(proj_done, v + 1)
                        wait(dve, norm_done, 2 * (v - STEP + 1))
                        wait(dve, h1_stored[k], 16 * (i - 1))
                        bias = bias1[:].rearrange("p (o c) -> p o c", o=1).to_broadcast((T, 2, C))
                        dve.tensor_tensor(h1[:, k], ps_h[k % 2][0:T, :].rearrange("p (b c) -> p b c", b=2), bias,
                                          ALU.add).then_inc(h1_ready, 1)
                        dve.wait_ge(h1_ready, v + 1)
                        for j in range(2):
                            dve.bn_stats(stats[:, 2 * k + j, :], h1[:, k, j]).then_inc(stats_done, 1)
                        wait_apart(dve, stats_done, 2 * v + 2, passed_dve)
                        for j in range(2):
                            dve.bn_aggr(mv[:, 2 * k + j, :], stats[:, 2 * k + j, :]).then_inc(aggr_done, 1)
                if proj:
                    v = (i - 1) * STEP
                    dve.wait_ge(aggr_done, 2 * (v + STEP))
                    ch = Chain(dve, rstd_chain, (i - 1) * RSTD_STEPS)
                    rstd_steps(ch, dve, mv[:, :, 1], var[:], rstd[:], newton[:])
                    dve.scalar_tensor_tensor(shift[:], mv[:, :, 0], -1.0, rstd[:], ALU.mult, ALU.mult)\
                       .then_inc(norm_ready, 1)

            turn(0, proj=False)
            turn(1)
            with dve.Fori(2, TURNS) as i:
                turn(i)
            turn(TURNS, conv=False)

        @block.tensor
        def _(pe):
            pe.wait_ge(consts_made, 3)
            pe.wait_ge(weights_in, 80)
            for m in range(CC):
                for e in range(CC):
                    last = pe.transpose(ps_w[m][:, e * P:(e + 1) * P], wo[:, e, m * P:(m + 1) * P], ident[:])
            last.then_inc(woT_done, 1)
            pe.wait_ge(woT_copied, 2)
            for m in range(CC):
                pe.matmul(ps_b[0:T, 0:C], bv_rows[:, m, :], woT[:, m, :], start=(m == 0), stop=False)
            pe.matmul(ps_b[0:T, 0:C], ones[0:1, 0:T], bo_row[:], start=False, stop=True)
            for d in range(CC):
                for m in range(CC):
                    last = pe.matmul(ps_w[d][:, 0:C], wv[:, m, d * P:(d + 1) * P], woT[:, m, :],
                                     start=(m == 0), stop=(m == CC - 1))
            last.then_inc(w_done, 1)
            pe.wait_ge(weights_ready, 2)

            def turn(i, conv_=True, proj=True):
                for k in range(STEP):
                    if conv_:
                        u = i * STEP + k
                        pe.wait_ge(x_loaded[k], 16 * (i + 1))
                        wait(pe, s_lo_ready, u - 1)
                        for j in range(2):
                            for c in range(CC):
                                n = (j * CC + c) * T
                                last = pe.matmul(ps_s[k % 2][:, n:n + T], x_in[:, k, j, c * P:(c + 1) * P], conv[:],
                                                 start=True, stop=True)
                        last.then_inc(conv_done, 1)
                    if proj:
                        v = (i - 1) * STEP + k
                        wait(pe, s_lo_ready, v + 1)
                        wait(pe, h1_ready, v - 1)
                        for j in range(2):
                            for c in range(CC):
                                n = (j * CC + c) * T
                                last = matmul3(pe, ps_h[k % 2][0:T, j * C:(j + 1) * C], s_hi[:, k, n:n + T],
                                               s_lo[:, k, n:n + T], w_hi[:, c, :], w_lo[:, c, :], c == 0, c == CC - 1)
                        last.then_inc(proj_done, 1)

            turn(0, proj=False)
            turn(1)
            with pe.Fori(2, TURNS) as i:
                turn(i)
            turn(TURNS, conv_=False)


def phase_states(nc, scratch, xn):
    CH = 4
    UNITS = 8
    TURNS_B = C // (CH * UNITS)
    LD = 2
    SLOTS = UNITS // LD
    kern_dram, y_dram = scratch["kern"], scratch["y"]
    with ExitStack() as ctx:
        rows_in = ctx.enter_context(nc.sbuf_tensor("rows_in", [T, UNITS * CH, T], F32))
        toep = ctx.enter_context(nc.sbuf_tensor("toep", [T, UNITS * CH, T], F32))
        ps = [ctx.enter_context(nc.psum_tensor(f"ps_y{n}", [P, CH, P], F32)) for n in range(UNITS)]
        toep_loaded = [ctx.enter_context(nc.semaphore(f"toep_loaded{n}")) for n in range(SLOTS)]
        toep_ready = ctx.enter_context(nc.semaphore("toep_ready"))
        y_done = ctx.enter_context(nc.semaphore("y_done"))
        y_even = ctx.enter_context(nc.semaphore("y_even"))
        y_odd = ctx.enter_context(nc.semaphore("y_odd"))
        y_stored = ctx.enter_context(nc.semaphore("y_stored"))
        passed_pool = ctx.enter_context(nc.semaphore("b_passed_pool"))
        block = ctx.enter_context(nc.Block())

        def copy_out(eng, op, i, n, done):
            h = (i * UNITS + n) * CH
            eng.wait_ge(y_done, i * UNITS + n + 1)
            op(xn[:, :, bass.ds(h, CH)], ps[n][0:T].rearrange("p h b -> p b h")).then_inc(done, 1)

        @block.sync
        def _(sp):
            def turn(i):
                for s in range(SLOTS):
                    wait(sp, toep_ready, (i - 1) * SLOTS + s + 1)
                    h = (i * UNITS + s * LD) * CH
                    rows = bass.AP(kern_dram.tensor, h * LPAD, [[1, T], [LPAD, LD * CH], [1, T]])
                    sp.dma_start(rows_in[:, s * LD * CH:(s + 1) * LD * CH, :], rows)\
                      .then_inc(toep_loaded[s], 16)

            turn(0)
            with sp.Fori(1, TURNS_B) as i:
                turn(i)
            sp.wait_ge(y_even, C // CH // 2)
            sp.wait_ge(y_odd, C // CH // 2)
            for n in range(4):
                b = slice(n * B // 4, (n + 1) * B // 4)
                sp.dma_start(y_dram[:, b, :], xn[:, b, :]).then_inc(y_stored, 16)
            sp.wait_ge(y_stored, 64)

        @block.gpsimd
        def _(pool):
            def turn(i):
                for s in range(SLOTS):
                    pool.wait_ge(toep_loaded[s], 16 * (i + 1))
                    wait_apart(pool, y_done, (i - 1) * UNITS + (s + 1) * LD, passed_pool)
                    h = slice(s * LD * CH, (s + 1) * LD * CH)
                    pool.tensor_copy(toep[:, h, :], rows_in[:, h, ::-1]).then_inc(toep_ready, 1)

            turn(0)
            with pool.Fori(1, TURNS_B) as i:
                turn(i)

        @block.tensor
        def _(pe):
            def turn(i):
                for n in range(UNITS):
                    if n % LD == 0:
                        pe.wait_ge(toep_ready, i * SLOTS + n // LD + 1)
                    wait(pe, y_odd if n % 2 else y_even, (i - 1) * (UNITS // 2) + n // 2 + 1)
                    for c in range(CH):
                        h = (i * UNITS + n) * CH + c
                        last = pe.matmul(ps[n][0:T, c, :], toep[:, n * CH + c, :], xn[:, :, bass.ds(h, 1)].rearrange("p b o -> p (b o)"),
                                         start=True, stop=True)
                    last.then_inc(y_done, 1)

            turn(0)
            with pe.Fori(1, TURNS_B) as i:
                turn(i)

        @block.vector
        def _(dve):
            def turn(i):
                for n in range(0, UNITS, 2):
                    copy_out(dve, dve.tensor_copy, i, n, y_even)

            turn(0)
            with dve.Fori(1, TURNS_B) as i:
                turn(i)

        @block.scalar
        def _(act):
            def turn(i):
                for n in range(1, UNITS, 2):
                    copy_out(act, act.copy, i, n, y_odd)

            turn(0)
            with act.Fori(1, TURNS_B) as i:
                turn(i)


def phase_router_weights(nc, A, w):
    with ExitStack() as ctx:
        raw1 = ctx.enter_context(nc.sbuf_tensor("raw1", [P, CC, HID], F32))
        raw2 = ctx.enter_context(nc.sbuf_tensor("raw2", [P, HC, HID], F32))
        raw3 = ctx.enter_context(nc.sbuf_tensor("raw3", [P, HC, E], F32))
        small_in = ctx.enter_context(nc.semaphore("small_in"))
        raw1_in = ctx.enter_context(nc.semaphore("raw1_in"))
        raw2_in = [ctx.enter_context(nc.semaphore(f"raw2_in{k}")) for k in range(HC)]
        hi_done = ctx.enter_context(nc.semaphore("router_hi_done"))
        made = ctx.enter_context(nc.semaphore("router_consts"))
        block = ctx.enter_context(nc.Block())

        @block.sync
        def _(sp):
            sp.dma_start(raw1[:], A["L0_ffn_rW1"].rearrange("(k p) n -> p k n", p=P)).then_inc(raw1_in, 16)
            for k in range(HC):
                sp.dma_start(raw2[:, k], A["L0_ffn_rW2"][k * P:(k + 1) * P]).then_inc(raw2_in[k], 16)
            sp.dma_start(raw3[:], A["L0_ffn_rW3"].rearrange("(k p) n -> p k n", p=P)).then_inc(small_in, 16)
            for name, dst in (("L0_ffn_rb1", w["rb1"]), ("L0_ffn_rb2", w["rb2"])):
                sp.dma_start(dst[:], A[name].rearrange("(k p) -> p k", p=P),
                             allow_slow_non_contiguous=True).then_inc(small_in, 16)
            sp.dma_start(w["rb3"][:], bass.AP(A["L0_ffn_rb3"].tensor, 0, [[0, P], [1, E]])).then_inc(small_in, 16)

        @block.scalar
        def _(act):
            act.wait_ge(raw1_in, 16)
            act.copy(w["w1_hi"][:], raw1[:]).then_inc(hi_done, 1)
            for k in range(HC):
                act.wait_ge(raw2_in[k], 16)
                act.copy(w["w2_hi"][:, k], raw2[:, k]).then_inc(hi_done, 1)
            act.wait_ge(small_in, 64)
            act.copy(w["w3"][:, :, 0:E], raw3[:]).then_inc(hi_done, 1)

        @block.vector
        def _(dve):
            dve.wait_ge(hi_done, 1)
            dve.tensor_tensor(w["w1_lo"][:], raw1[:], w["w1_hi"][:].bitcast(F32), ALU.subtract)
            for k in range(HC):
                dve.wait_ge(hi_done, k + 2)
                dve.tensor_tensor(w["w2_lo"][:, k], raw2[:, k], w["w2_hi"][:, k].bitcast(F32), ALU.subtract)
            dve.wait_ge(hi_done, HC + 2)
            dve.tensor_tensor(w["w3"][:, :, E:2 * E], raw3[:], w["w3"][:, :, 0:E].bitcast(F32), ALU.subtract)

        @block.gpsimd
        def _(pool):
            pool.memset(w["ident"][:], 0.0).then_inc(made, 1)
            pool.memset(w["earlier"][:], 1.0).then_inc(made, 1)
            pool.wait_ge(made, 2)
            pool.affine_select(out=w["ident"][:], in_=w["ident"][:], compare_op=ALU.not_equal, fill=1.0, base=0,
                               pattern=[[-1, P]], channel_multiplier=1)
            pool.affine_select(out=w["earlier"][:], in_=w["earlier"][:], compare_op=ALU.is_gt, fill=0.0, base=0,
                               pattern=[[1, T]], channel_multiplier=-1)
            pool.iota(w["slot_no"][:], pattern=[[0, GB * E], [1, CAP]], base=0, channel_multiplier=0,
                      allow_small_or_imprecise_dtypes=True)
            pool.iota(w["rank"][:], pattern=[[0, GB], [-1, E]], base=E, channel_multiplier=0,
                      allow_small_or_imprecise_dtypes=True)


def phase_router(nc, scratch, w, place, gate):
    h1_dram, y_dram, h2_dram, rows_dram = scratch["h1"], scratch["y"], scratch["h2"], scratch["rows"]
    NT = HC
    RELU = 4
    MM = 4
    with ExitStack() as ctx:
        def sb(name, shape, dt=F32):
            return ctx.enter_context(nc.sbuf_tensor(name, shape, dt))

        def sem(name):
            return ctx.enter_context(nc.semaphore(name))

        h1 = sb("c_h1", [T, GB, C])
        y = sb("c_y", [T, GB, C])
        h2 = sb("c_h2", [T, GB, C])
        x2 = sb("c_x2", [T, GB, C])
        x2_part = [sb(f"x2_part{n}", [T, GB, C], BF16) for n in range(3)]
        x2_rest = sb("x2_rest", [T, GB, C])
        stats = sb("c_stats", [T, GB, 6])
        mv = sb("c_mv", [T, GB, 2])
        var = sb("c_var", [T, GB])
        rstd = sb("c_rstd", [T, GB])
        newton = sb("c_newton", [T, GB])
        shift = sb("c_shift", [T, GB])
        xT_hi = sb("xT_hi", [P, CC, GT], F32R)
        xT_lo = sb("xT_lo", [P, CC, GT], F32R)
        relu = sb("relu", [P, RELU, GT])
        a1_hi = sb("a1_hi", [P, HC, GT], F32R)
        a1_lo = sb("a1_lo", [P, HC, GT], F32R)
        a2_hi = sb("a2_hi", [P, HC, GT], F32R)
        a2_lo = sb("a2_lo", [P, HC, GT], F32R)
        logT = sb("logT", [2 * E, GT])
        logit = sb("logit", [T, GB, E])
        ex = sb("ex", [T, GB, E])
        prob = sb("prob", [T, GB, E])
        key = sb("key", [T, GB, E])
        first = sb("first", [T, GB, E])
        rest = sb("rest", [T, GB, E])
        chosen = sb("chosen", [T, GB, E])
        chosen_bf = sb("chosen_bf", [T, GB * E], BF16)
        m1 = sb("m1", [T, GB])
        m2 = sb("m2", [T, GB])
        onehot = sb("onehot", [T, GB * E, CAP], BF16)
        rows = sb("rows", [P, CC, E, GB, CAP])

        ps_m = [ctx.enter_context(nc.psum_tensor(f"ps_m{n}", [P, 512], F32)) for n in range(MM)]
        ps_x = [ctx.enter_context(nc.psum_tensor(f"ps_x{n}", [P, 512], F32)) for n in range(3)]
        ps_l = ps_x[2]
        ps_r = ctx.enter_context(nc.psum_tensor("ps_r", [P, 512], F32))
        logit_ps = ps_r[0:T, 0:GB * 2 * E].rearrange("p (b e) -> p b e", b=GB)
        pos_ps = ps_r[0:T, GB * 2 * E:GB * 3 * E]

        h1_in = sem("c_h1_in")
        y_in = sem("c_y_in")
        h2_ready = sem("c_h2_ready")
        h2_stored = sem("c_h2_stored")
        stats_done = sem("c_stats_done")
        aggr_done = sem("c_aggr_done")
        prep_chain = sem("prep_chain")
        norm_ready = sem("c_norm_ready")
        norm_done = sem("c_norm_done")
        part0_ready = sem("part0_ready")
        rest_ready = sem("rest_ready")
        part1_ready = sem("part1_ready")
        part2_ready = sem("part2_ready")
        xT_done = sem("xT_done")
        xT_hi_ready = sem("xT_hi_ready")
        xT_ready = sem("xT_ready")
        tile_done = sem("tile_done")
        relu_done = sem("relu_done")
        hi_ready = sem("hi_ready")
        lo_ready = sem("lo_ready")
        logT_done = sem("logT_done")
        logT_copied = sem("logT_copied")
        logit_done = sem("logit_done")
        route_chain = sem("route_chain")
        exp_ready = sem("exp_ready")
        exp_done = sem("exp_done")
        chosen_ready = sem("chosen_ready")
        place_ready = sem("place_ready")
        pos_done = sem("pos_done")
        onehot_ready = sem("onehot_ready")
        rows_done = sem("rows_done")
        rows_copied = sem("rows_copied")
        rows_stored = sem("rows_stored")
        passed_dve = sem("c_passed_dve")
        passed_pe = sem("c_passed_pe")
        block = ctx.enter_context(nc.Block())

        TILES = 2 * NT
        ROUTE_STEPS = 19
        PIECES = GB * CC

        def bank_of(piece):
            n = piece % 3 * SL
            return ps_x[piece // 3][:, n:n + SL]

        def groups(eng, turn, before, after):
            before()
            turn(0, route=False)
            turn(1)
            with eng.Fori(2, NG - 1) as g:
                turn(g)
            turn(NG - 1, prep=False)
            after()

        @block.sync
        def _(sp):
            def load(g):
                wait(sp, h2_ready, g)
                sp.dma_start(h1[:], h1_dram[:, bass.ds(g * GB, GB), :]).then_inc(h1_in, 16)
                sp.dma_start(y[:], y_dram[:, bass.ds(g * GB, GB), :]).then_inc(y_in, 16)

            def store_h2(g):
                wait(sp, h2_ready, g + 1)
                sp.dma_start(h2_dram[:, bass.ds(g * GB, GB), :], h2[:]).then_inc(h2_stored, 16)

            def store_rows(g):
                wait(sp, rows_copied, PIECES * (g + 1))
                sp.dma_start(rows_dram[:, :, bass.ds(g * GB * CAP, GB * CAP)],
                             rows[:].rearrange("p c e b s -> p (c e) (b s)")).then_inc(rows_stored, 16)

            load(0)
            store_h2(0)
            load(1)
            store_h2(1)
            load(2)

            def turn(g):
                store_rows(g - 1)
                store_h2(g + 1)
                load(g + 2)

            turn(1)
            with sp.Fori(2, NG - 2) as g:
                turn(g)
            store_rows(NG - 3)
            store_h2(NG - 1)
            store_rows(NG - 2)
            store_rows(NG - 1)
            sp.wait_ge(h2_stored, 16 * NG)
            sp.wait_ge(rows_stored, 16 * NG)

        @block.scalar
        def _(act):
            def norm(g):
                wait(act, norm_ready, g + 1)
                wait(act, rest_ready, g)
                wait(act, xT_done, g)
                for b in range(GB):
                    act.activation(x2[:, b], h2[:, b], ACT.Identity, bias=shift[:, b:b + 1], scale=rstd[:, b:b + 1])\
                       .then_inc(norm_done, 1)

            def copy_xT(g):
                wait(act, xT_done, g + 1)
                for c in range(CC):
                    act.copy(xT_hi[:, c], ps_x[c][:, 0:GT]).then_inc(xT_hi_ready, 1)

            def relus(g, layer, tiles):
                bias = w["rb1"] if layer == 0 else w["rb2"]
                for t in tiles:
                    n = g * TILES + layer * NT + t
                    act.wait_ge(tile_done, n + 1)
                    wait(act, lo_ready, n - RELU + 1)
                    act.activation(relu[:, t % RELU], ps_m[t % MM][:, 0:GT], ACT.Relu,
                                   bias=bias[:, t:t + 1]).then_inc(relu_done, 1)

            def copy_logT(g):
                wait(act, logT_done, g + 1)
                act.copy(logT[:], ps_l[0:2 * E, 0:GT]).then_inc(logT_copied, 1)

            def exps(g):
                wait(act, exp_ready, g + 1)
                act.activation(ex[:], logit[:], ACT.Exp).then_inc(exp_done, 1)

            def copy_rows(g):
                wait(act, rows_done, g + 1)
                wait(act, rows_stored, 16 * g)
                for n in range(PIECES):
                    act.copy(rows[:, n // GB, :, n % GB, :], bank_of(n).rearrange("p (e s) -> p e s", e=E))\
                       .then_inc(rows_copied, 1)

            def part0(g):
                wait(act, rows_done, g)
                wait(act, norm_done, GB * (g + 1))
                act.copy(x2_part[0][:], x2[:]).then_inc(part0_ready, 1)

            def part1(g):
                wait(act, rest_ready, g + 1)
                act.copy(x2_part[1][:], x2_rest[:]).then_inc(part1_ready, 1)

            def turn(g, route=True, prep=True):
                relus(g, 0, range(NT))
                if route:
                    copy_logT(g - 1)
                relus(g, 1, [0])
                if route:
                    exps(g - 1)
                relus(g, 1, [1, 2, 3])
                if route:
                    copy_rows(g - 1)
                part0(g)
                relus(g, 1, [4])
                if prep:
                    norm(g + 1)
                part1(g)
                relus(g, 1, [5])
                if prep:
                    copy_xT(g + 1)
                relus(g, 1, [6, 7])

            def before():
                norm(0)
                copy_xT(0)

            def after():
                copy_logT(NG - 1)
                exps(NG - 1)
                copy_rows(NG - 1)

            groups(act, turn, before, after)

        @block.vector
        def _(dve):
            def stats_of(g):
                wait(dve, h1_in, 16 * (g + 1))
                wait(dve, y_in, 16 * (g + 1))
                wait(dve, h2_stored, 16 * g)
                wait(dve, norm_done, GB * g)
                dve.tensor_tensor(h2[:], h1[:], y[:], ALU.add).then_inc(h2_ready, 1)
                wait(dve, h2_ready, g + 1)
                for b in range(GB):
                    dve.bn_stats(stats[:, b, :], h2[:, b]).then_inc(stats_done, 1)
                wait_apart(dve, stats_done, GB * (g + 1), passed_dve)
                for b in range(GB):
                    dve.bn_aggr(mv[:, b, :], stats[:, b, :]).then_inc(aggr_done, 1)
                wait(dve, aggr_done, GB * (g + 1))
                ch = Chain(dve, prep_chain, g * RSTD_STEPS)
                rstd_steps(ch, dve, mv[:, :, 1], var[:], rstd[:], newton[:])
                dve.scalar_tensor_tensor(shift[:], mv[:, :, 0], -1.0, rstd[:], ALU.mult, ALU.mult)\
                   .then_inc(norm_ready, 1)

            def split_xT(g):
                wait(dve, xT_hi_ready, CC * (g + 1))
                for c in range(CC):
                    dve.tensor_tensor(xT_lo[:, c], ps_x[c][:, 0:GT], xT_hi[:, c].bitcast(F32), ALU.subtract)\
                       .then_inc(xT_ready, 1)

            def splits(g, layer, tiles):
                hi, lo = (a1_hi, a1_lo) if layer == 0 else (a2_hi, a2_lo)
                for t in tiles:
                    n = g * TILES + layer * NT + t
                    dve.wait_ge(relu_done, n + 1)
                    if layer == 1 and t == 0:
                        wait(dve, logT_done, g)
                    dve.tensor_copy(hi[:, t], relu[:, t % RELU]).then_inc(hi_ready, 1)
                    dve.wait_ge(hi_ready, n + 1)
                    dve.tensor_tensor(lo[:, t], relu[:, t % RELU], hi[:, t].bitcast(F32), ALU.subtract)\
                       .then_inc(lo_ready, 1)

            def rest_of_x2(g):
                wait(dve, part0_ready, g + 1)
                wait(dve, part2_ready, g)
                dve.tensor_tensor(x2_rest[:], x2[:], x2_part[0][:], ALU.subtract).then_inc(rest_ready, 1)

            def part2(g):
                wait(dve, part1_ready, g + 1)
                dve.tensor_tensor(x2_part[2][:], x2_rest[:], x2_part[1][:], ALU.subtract).then_inc(part2_ready, 1)

            def over_e(x):
                return x[:].rearrange("p (b o) -> p b o", o=1).to_broadcast((T, GB, E))

            def best(ch, scores, mask):
                ch.step(dve.tensor_reduce(m1[:], scores, AX, ALU.max))
                ch.step(dve.tensor_tensor(key[:], scores, over_e(m1), ALU.is_equal))
                ch.step(dve.tensor_tensor(key[:], key[:], w["rank"][0:T], ALU.mult))
                ch.step(dve.tensor_reduce(m2[:], key[:], AX, ALU.max))
                ch.step(dve.tensor_tensor(mask, key[:], over_e(m2), ALU.is_equal))

            def choose(g):
                ch = Chain(dve, route_chain, g * ROUTE_STEPS)
                wait(dve, logit_done, g + 1)
                bias = w["rb3"][0:T, :].rearrange("p (o e) -> p o e", o=1).to_broadcast((T, GB, E))
                ch.step(dve.tensor_tensor(logit[:], logit_ps[:, :, 0:E], bias, ALU.add))
                ch.step(dve.tensor_tensor(logit[:], logit_ps[:, :, E:2 * E], logit[:], ALU.add))
                ch.step(dve.tensor_reduce(m1[:], logit[:], AX, ALU.max))
                dve.tensor_tensor(logit[:], logit[:], over_e(m1), ALU.subtract).then_inc(exp_ready, 1)
                wait(dve, exp_done, g + 1)
                ch.step(dve.reduce_sum(m2[:], ex[:], AX))
                ch.step(dve.reciprocal(m1[:], m2[:]))
                ch.step(dve.tensor_tensor(prob[:], ex[:], over_e(m1), ALU.mult))
                best(ch, prob[:], first[:])
                ch.step(dve.scalar_tensor_tensor(rest[:], first[:], -2.0, prob[:], ALU.mult, ALU.add))
                best(ch, rest[:], chosen[:])
                ch.step(dve.tensor_tensor(chosen[:], chosen[:], first[:], ALU.add))
                dve.tensor_copy(chosen_bf[:], chosen[:].rearrange("p b e -> p (b e)")).then_inc(chosen_ready, 1)
                dve.tensor_tensor(gate[:, bass.ds(g * GB * E, GB * E)].rearrange("p (b e) -> p b e", b=GB),
                                  prob[:], chosen[:], ALU.mult)
                assert ch.n == ROUTE_STEPS - 1

            def slots(g):
                at = place[:, bass.ds(g * GB * E, GB * E)]
                wait(dve, pos_done, g + 1)
                dve.tensor_scalar(key[:], chosen[:], -1000.0, 1000.0, ALU.mult, ALU.add).then_inc(route_chain, 1)
                dve.wait_ge(route_chain, (g + 1) * ROUTE_STEPS)
                dve.tensor_tensor(at, pos_ps, key[:].rearrange("p b e -> p (b e)"), ALU.add)\
                   .then_inc(place_ready, 1)
                wait(dve, place_ready, g + 1)
                wait(dve, rows_done, g)
                dve.tensor_tensor(onehot[:], w["slot_no"][0:T],
                                  at.rearrange("p (n o) -> p n o", o=1).to_broadcast((T, GB * E, CAP)),
                                  ALU.is_equal).then_inc(onehot_ready, 1)

            def turn(g, route=True, prep=True):
                splits(g, 0, range(NT))
                splits(g, 1, [0])
                if route:
                    choose(g - 1)
                splits(g, 1, [1])
                if prep:
                    stats_of(g + 1)
                splits(g, 1, [2])
                if route:
                    slots(g - 1)
                splits(g, 1, [3])
                rest_of_x2(g)
                splits(g, 1, [4])
                part2(g)
                splits(g, 1, [5])
                if prep:
                    split_xT(g + 1)
                splits(g, 1, [6, 7])

            def before():
                stats_of(0)
                split_xT(0)

            def after():
                choose(NG - 1)
                slots(NG - 1)

            groups(dve, turn, before, after)

        @block.tensor
        def _(pe):
            def transpose_x2(g):
                wait(pe, norm_done, GB * (g + 1))
                wait(pe, rows_copied, PIECES * (g - 1))
                wait(pe, xT_ready, CC * g)
                for c in range(CC):
                    for b in range(GB):
                        last = pe.transpose(ps_x[c][:, b * T:(b + 1) * T], x2[:, b, c * P:(c + 1) * P],
                                            w["ident"][0:T, 0:T])
                last.then_inc(xT_done, 1)

            def layer(g, n_layer, tiles):
                w_hi, w_lo = (w["w1_hi"], w["w1_lo"]) if n_layer == 0 else (w["w2_hi"], w["w2_lo"])
                x_hi, x_lo = (xT_hi, xT_lo) if n_layer == 0 else (a1_hi, a1_lo)
                chunks = CC if n_layer == 0 else HC
                for t in tiles:
                    n = g * TILES + n_layer * NT + t
                    if n_layer == 0 and t == 0:
                        wait(pe, xT_ready, CC * (g + 1))
                    wait(pe, relu_done, n - MM + 1)
                    for k in range(chunks):
                        if n_layer == 1 and t == 0:
                            wait(pe, lo_ready, g * TILES + k + 1)
                        o = slice(t * P, (t + 1) * P)
                        last = matmul3(pe, ps_m[t % MM][:, 0:GT], w_hi[:, k, o], w_lo[:, k, o], x_hi[:, k], x_lo[:, k],
                                       k == 0, k == chunks - 1)
                    last.then_inc(tile_done, 1)

            def logits(g):
                wait(pe, lo_ready, (g + 1) * TILES)
                wait(pe, rows_copied, PIECES * g)
                for k in range(HC):
                    pe.matmul(ps_l[0:2 * E, 0:GT], w["w3"][:, k, :], a2_hi[:, k], start=(k == 0), stop=False)
                    last = pe.matmul(ps_l[0:E, 0:GT], w["w3"][:, k, 0:E], a2_lo[:, k], start=False, stop=(k == HC - 1))
                last.then_inc(logT_done, 1)

            def transpose_logits(g):
                wait(pe, logT_copied, g + 1)
                wait_apart(pe, onehot_ready, g, passed_pe)
                for b in range(GB):
                    last = pe.transpose(ps_r[0:T, b * 2 * E:(b + 1) * 2 * E], logT[:, b * T:(b + 1) * T],
                                        w["ident"][0:2 * E, 0:2 * E])
                last.then_inc(logit_done, 1)

            def positions(g):
                wait(pe, chosen_ready, g + 1)
                pe.matmul(pos_ps, w["earlier"][:], chosen_bf[:], start=True, stop=True).then_inc(pos_done, 1)

            def gather(g):
                wait(pe, onehot_ready, g + 1)
                wait(pe, part2_ready, g + 1)
                for n in range(PIECES):
                    c, b = n // GB, n % GB
                    hot = onehot[:, b * E:(b + 1) * E, :].rearrange("p e s -> p (e s)")
                    for part in range(3):
                        last = pe.matmul(bank_of(n), x2_part[part][:, b, c * P:(c + 1) * P], hot, start=(part == 0),
                                         stop=(part == 2))
                last.then_inc(rows_done, 1)

            def turn(g, route=True, prep=True):
                layer(g, 0, range(NT))
                if route:
                    logits(g - 1)
                layer(g, 1, [0])
                if route:
                    transpose_logits(g - 1)
                layer(g, 1, [1, 2])
                if route:
                    positions(g - 1)
                layer(g, 1, [3])
                if route:
                    gather(g - 1)
                layer(g, 1, [4, 5])
                if prep:
                    transpose_x2(g + 1)
                layer(g, 1, [6, 7])

            def before():
                transpose_x2(0)

            def after():
                logits(NG - 1)
                transpose_logits(NG - 1)
                positions(NG - 1)
                gather(NG - 1)

            groups(pe, turn, before, after)


def phase_experts(nc, A, scratch, w):
    rows_dram, out_dram = scratch["rows"], scratch["slots"]
    SPT = 4
    TPE = -(-CAP // SPT)
    MM = 4
    RELU = 4
    N = SPT * B
    assert B == P and N == 512

    def slots_of(j):
        return min(SPT, CAP - j * SPT)

    with ExitStack() as ctx:
        def sb(name, shape, dt=F32):
            return ctx.enter_context(nc.sbuf_tensor(name, shape, dt))

        def sem(name):
            return ctx.enter_context(nc.semaphore(name))

        w1_raw = sb("w1_raw", [P, CC, HID])
        w2_raw = sb("w2_raw", [P, HC, C])
        w1_hi = [sb(f"d_w1_hi{n}", [P, CC, HID], F32R) for n in range(2)]
        w1_lo = [sb(f"d_w1_lo{n}", [P, CC, HID], F32R) for n in range(2)]
        w2_hi = [sb(f"d_w2_hi{n}", [P, HC, C], F32R) for n in range(2)]
        w2_lo = [sb(f"d_w2_lo{n}", [P, HC, C], F32R) for n in range(2)]
        rows = sb("d_rows", [P, CC, B * CAP])
        x_hi = [sb(f"d_x_hi{n}", [P, CC, N], F32R) for n in range(2)]
        x_lo = [sb(f"d_x_lo{n}", [P, CC, N], F32R) for n in range(2)]
        a_hi = [sb(f"d_a_hi{n}", [P, HC, N], F32R) for n in range(2)]
        a_lo = [sb(f"d_a_lo{n}", [P, HC, N], F32R) for n in range(2)]
        relu = sb("d_relu", [P, RELU, N])
        out = sb("d_out", [P, SPT, C])
        b1_rows = sb("b1_rows", [E * HC, P])
        b1 = sb("d_b1", [P, E * HC])
        b2 = sb("d_b2", [P, 2, C])
        ps_m = [ctx.enter_context(nc.psum_tensor(f"ps_d{n}", [P, 512], F32)) for n in range(MM)]
        ps_o = [ctx.enter_context(nc.psum_tensor(f"ps_o{n}", [P, 512], F32)) for n in range(SPT)]

        b1_in = sem("b1_in")
        b1_done = sem("b1_done")
        b1_ready = sem("b1_ready")
        w_in = sem("d_w_in")
        b2_in = [sem(f"b2_in{n}") for n in range(2)]
        rows_in = sem("d_rows_in")
        w_hi_done = sem("w_hi_done")
        w_ready = sem("d_w_ready")
        x_hi_done = sem("x_hi_done")
        x_ready = sem("d_x_ready")
        tile_done = sem("d_tile_done")
        relu_done = sem("d_relu_done")
        hi_ready = sem("d_hi_ready")
        lo_ready = sem("d_lo_ready")
        out_done = sem("d_out_done")
        out_ready = sem("d_out_ready")
        passed_act = sem("d_passed_act")
        passed_pool = sem("d_passed_pool")
        out_stored = [sem(f"d_out_stored{n}") for n in range(SPT)]
        block = ctx.enter_context(nc.Block())

        def in_turns(eng, turn):
            turn(0, first=True)
            with eng.Fori(1, E // 2 - 1) as i:
                turn(i)
            turn(E // 2 - 1, last=True)

        def before(e, j):
            return (e, j - 1) if j else (e - 1, TPE - 1)

        @block.sync
        def _(sp):
            def load_w(e):
                wait(sp, w_ready, 2 * e)
                sp.dma_start(w1_raw[:], A["L0_ffn_eW1"][bass.ds(e, 1)].rearrange("e (k p) n -> p (e k) n", p=P))\
                  .then_inc(w_in, 16)
                sp.dma_start(w2_raw[:], A["L0_ffn_eW2"][bass.ds(e, 1)].rearrange("e (k p) n -> p (e k) n", p=P))\
                  .then_inc(w_in, 16)

            def load_b2(e, q):
                sp.dma_start(b2[:, q], A["L0_ffn_eb2"][bass.ds(e, 1)].to_broadcast((P, C))).then_inc(b2_in[q], 16)

            def load_rows(e):
                wait(sp, x_ready, TPE * e)
                sp.dma_start(rows[:], rows_dram.rearrange("p (c e) n -> p c e n", c=CC)[:, :, bass.ds(e, 1), :]
                             .rearrange("p c o n -> p c (o n)")).then_inc(rows_in, 16)

            def store(e, j):
                for r in range(slots_of(j)):
                    wait(sp, out_ready, e * CAP + j * SPT + r + 1)
                    sp.dma_start(out_dram[bass.ds(e * CAP + j * SPT + r, 1)].rearrange("o b c -> b (o c)"), out[:, r])\
                      .then_inc(out_stored[r], 16)

            sp.dma_start(b1_rows[:], A["L0_ffn_eb1"].rearrange("e (k p) -> (e k) p", p=P)).then_inc(b1_in, 16)
            load_w(0)
            load_rows(0)

            def turn(i, first=False, last=False):
                for q in range(2):
                    e = 2 * i + q
                    for j in range(TPE):
                        if j == 0:
                            wait(sp, out_ready, (e - 1) * CAP)
                            load_b2(e, q)
                            if not (last and q == 1):
                                load_w(e + 1)
                        if not (first and q == 0 and j == 0):
                            store(*before(e, j))
                        if j == 3 and not (last and q == 1):
                            load_rows(e + 1)

            in_turns(sp, turn)
            store(E - 1, TPE - 1)
            for r in range(SPT):
                sp.wait_ge(out_stored[r], 16 * E * (TPE if r < slots_of(TPE - 1) else TPE - 1))

        @block.gpsimd
        def _(pool):
            def split_w(e, q):
                wait(pool, w_in, 32 * (e + 1))
                wait_apart(pool, out_done, (e - 1) * CAP, passed_pool)
                pool.tensor_copy(w1_hi[q][:], w1_raw[:]).then_inc(w_hi_done, 1)
                pool.tensor_copy(w2_hi[q][:], w2_raw[:]).then_inc(w_hi_done, 1)
                wait(pool, w_hi_done, 2 * (e + 1))
                pool.tensor_tensor(w1_lo[q][:], w1_raw[:], w1_hi[q][:].bitcast(F32), ALU.subtract).then_inc(w_ready, 1)
                pool.tensor_tensor(w2_lo[q][:], w2_raw[:], w2_hi[q][:].bitcast(F32), ALU.subtract).then_inc(w_ready, 1)

            def split_x(e, j, q):
                n = slots_of(j)
                if j == 0:
                    wait(pool, rows_in, 16 * (e + 1))
                wait_apart(pool, tile_done, HC * (e * TPE + j - 1), passed_pool)
                s = (q * TPE + j) % 2
                for c in range(CC):
                    src = rows[:, c].rearrange("p (b s) -> p s b", s=CAP)[:, j * SPT:j * SPT + n, :]
                    hi = x_hi[s][:, c, 0:n * B].rearrange("p (s b) -> p s b", s=n)
                    pool.tensor_copy(hi, src).then_inc(x_hi_done, 1)
                wait(pool, x_hi_done, CC * (e * TPE + j + 1))
                for c in range(CC):
                    src = rows[:, c].rearrange("p (b s) -> p s b", s=CAP)[:, j * SPT:j * SPT + n, :]
                    hi = x_hi[s][:, c, 0:n * B].rearrange("p (s b) -> p s b", s=n)
                    lo = x_lo[s][:, c, 0:n * B].rearrange("p (s b) -> p s b", s=n)
                    ins = pool.tensor_tensor(lo, src, hi.bitcast(F32), ALU.subtract)
                ins.then_inc(x_ready, 1)

            split_w(0, 0)

            def turn(i, first=False, last=False):
                for q in range(2):
                    for j in range(TPE):
                        split_x(2 * i + q, j, q)
                        if j == 2 and not (last and q == 1):
                            split_w(2 * i + q + 1, 1 - q)

            in_turns(pool, turn)

        @block.scalar
        def _(act):
            act.wait_ge(b1_done, 1)
            act.copy(b1[:], ps_m[0][:, 0:E * HC]).then_inc(b1_ready, 1)
            act.wait_ge(b1_ready, 1)

            def turn(i, first=False, last=False):
                for q in range(2):
                    for j in range(TPE):
                        e, n = 2 * i + q, slots_of(j) * B
                        for t in range(HC):
                            m = (e * TPE + j) * HC + t
                            act.wait_ge(tile_done, m + 1)
                            wait_apart(act, lo_ready, m - RELU + 1, passed_act)
                            act.activation(relu[:, t % RELU, 0:n], ps_m[t % MM][:, 0:n], ACT.Relu,
                                           bias=b1[:, bass.ds(e * HC + t, 1)]).then_inc(relu_done, 1)

            in_turns(act, turn)

        @block.vector
        def _(dve):
            def splits(e, j, q):
                n, s = slots_of(j) * B, (q * TPE + j) % 2
                for t in range(HC):
                    m = (e * TPE + j) * HC + t
                    dve.wait_ge(relu_done, m + 1)
                    dve.tensor_copy(a_hi[s][:, t, 0:n], relu[:, t % RELU, 0:n]).then_inc(hi_ready, 1)
                    dve.wait_ge(hi_ready, m + 1)
                    dve.tensor_tensor(a_lo[s][:, t, 0:n], relu[:, t % RELU, 0:n], a_hi[s][:, t, 0:n].bitcast(F32),
                                      ALU.subtract).then_inc(lo_ready, 1)

            def add_bias(e, j, q):
                if j == 0:
                    wait(dve, b2_in[q], 16 * (e // 2 + 1) if isinstance(e, int) else 8 * (e - q) + 16)
                for r in range(slots_of(j)):
                    wait(dve, out_done, e * CAP + j * SPT + r + 1)
                    wait(dve, out_stored[r], 16 * (e * (TPE if r < slots_of(TPE - 1) else TPE - 1) + j))
                    dve.tensor_tensor(out[:, r], ps_o[r][:, 0:C], b2[:, q], ALU.add).then_inc(out_ready, 1)

            def turn(i, first=False, last=False):
                for q in range(2):
                    for j in range(TPE):
                        e = 2 * i + q
                        splits(e, j, q)
                        if not (first and q == 0 and j == 0):
                            add_bias(*before(e, j), q if j else 1 - q)

            in_turns(dve, turn)
            add_bias(E - 1, TPE - 1, 1)

        @block.tensor
        def _(pe):
            pe.wait_ge(b1_in, 16)
            pe.transpose(ps_m[0][:, 0:E * HC], b1_rows[:], w["ident"][0:E * HC, 0:E * HC]).then_inc(b1_done, 1)
            pe.wait_ge(b1_ready, 1)

            def layer1(e, j, q):
                n, s = slots_of(j) * B, (q * TPE + j) % 2
                wait(pe, x_ready, e * TPE + j + 1)
                if j == 0:
                    wait(pe, w_ready, 2 * (e + 1))
                for t in range(HC):
                    m = (e * TPE + j) * HC + t
                    wait(pe, relu_done, m - MM + 1)
                    for k in range(CC):
                        o = slice(t * P, (t + 1) * P)
                        last = matmul3(pe, ps_m[t % MM][:, 0:n], w1_hi[q][:, k, o], w1_lo[q][:, k, o],
                                       x_hi[s][:, k, 0:n], x_lo[s][:, k, 0:n], k == 0, k == CC - 1)
                    last.then_inc(tile_done, 1)

            def layer2(e, j, q):
                s = (q * TPE + j) % 2
                wait(pe, lo_ready, (e * TPE + j + 1) * HC)
                for r in range(slots_of(j)):
                    here = e * CAP + j * SPT + r
                    past = here - SPT if j or r >= slots_of(TPE - 1) else here - slots_of(TPE - 1)
                    if j == 0 and r >= slots_of(TPE - 1):
                        past = here - slots_of(TPE - 1) - SPT
                    wait(pe, out_ready, past + 1)
                    rows_at = slice(r * B, (r + 1) * B)
                    for k in range(HC):
                        last = matmul3(pe, ps_o[r][:, 0:C], a_hi[s][:, k, rows_at], a_lo[s][:, k, rows_at],
                                       w2_hi[q][:, k], w2_lo[q][:, k], k == 0, k == HC - 1)
                    last.then_inc(out_done, 1)

            def turn(i, first=False, last=False):
                for q in range(2):
                    for j in range(TPE):
                        e = 2 * i + q
                        layer1(e, j, q)
                        if not (first and q == 0 and j == 0):
                            layer2(*before(e, j), q if j else 1 - q)

            in_turns(pe, turn)
            layer2(E - 1, TPE - 1, 1)


def phase_combine(nc, scratch, w, place, gate, result):
    h2_dram, slots_dram = scratch["h2"], scratch["slots"]
    STEP_E = 4
    TURNS_E = NG // STEP_E
    with ExitStack() as ctx:
        def sb(name, shape, dt=F32):
            return ctx.enter_context(nc.sbuf_tensor(name, shape, dt))

        def sem(name):
            return ctx.enter_context(nc.semaphore(name))

        hot = sb("e_hot", [T, STEP_E, GB * E, CAP])
        mix = sb("e_mix", [T, STEP_E, GB * E, CAP])
        mixT = sb("e_mixT", [HSL, STEP_E, 2, GT])
        slots = sb("e_slots", [HSL, STEP_E, 2, GB * C])
        h2 = sb("e_h2", [T, STEP_E, GB, C])
        out = sb("e_out", [T, STEP_E, GB, C])
        ps_t = [[ctx.enter_context(nc.psum_tensor(f"ps_t{n}{h}", [P, 512], F32)) for h in range(2)] for n in range(2)]
        ps_c = [[ctx.enter_context(nc.psum_tensor(f"ps_c{n}{h}", [P, 512], F32)) for h in range(2)] for n in range(2)]
        slots_in = [sem(f"slots_in{n}") for n in range(STEP_E)]
        h2_in = [sem(f"e_h2_in{n}") for n in range(STEP_E)]
        out_stored = [sem(f"e_out_stored{n}") for n in range(STEP_E)]
        hot_done = sem("hot_done")
        mix_ready = sem("mix_ready")
        mixT_done = sem("mixT_done")
        mixT_ready = sem("mixT_ready")
        sum_done = sem("sum_done")
        out_ready = sem("e_out_ready")
        block = ctx.enter_context(nc.Block())

        def in_turns(eng, turn):
            turn(0, mixing=False)
            turn(1)
            with eng.Fori(2, TURNS_E) as i:
                turn(i)
            turn(TURNS_E, mix=False)

        @block.sync
        def _(sp):
            def load(g, k):
                for h in range(2):
                    rows = slots_dram[h * HSL:(h + 1) * HSL, bass.ds(g * GB, GB), :].rearrange("s b c -> s (b c)")
                    sp.dma_start(slots[:, k, h], rows).then_inc(slots_in[k], 16)
                sp.dma_start(h2[:, k], h2_dram[:, bass.ds(g * GB, GB), :]).then_inc(h2_in[k], 16)

            for k in range(STEP_E):
                load(k, k)

            def turn(i, load_next=True):
                for k in range(STEP_E):
                    g = i * STEP_E + k
                    wait(sp, out_ready, 2 * (g + 1))
                    sp.dma_start(result[bass.ds(g * GB, GB)].rearrange("b t c -> t b c"), out[:, k])\
                      .then_inc(out_stored[k], 16)
                    if load_next:
                        load(g + STEP_E, k)

            with sp.Fori(0, TURNS_E - 1) as i:
                turn(i)
            turn(TURNS_E - 1, load_next=False)
            for k in range(STEP_E):
                sp.wait_ge(out_stored[k], 16 * TURNS_E)

        @block.gpsimd
        def _(pool):
            def turn(i):
                for k in range(STEP_E):
                    g = i * STEP_E + k
                    span = bass.ds(g * GB * E, GB * E)
                    wait(pool, mixT_done, g - STEP_E + 1)
                    over = (T, GB * E, CAP)
                    wait(pool, hot_done, g + 1)
                    pool.tensor_tensor(mix[:, k], hot[:, k],
                                       gate[:, span].rearrange("p (n o) -> p n o", o=1).to_broadcast(over),
                                       ALU.mult).then_inc(mix_ready, 1)

            turn(0)
            with pool.Fori(1, TURNS_E) as i:
                turn(i)

        @block.tensor
        def _(pe):
            def turn(i, mix=True, mixing=True):
                for k in range(STEP_E):
                    if mix:
                        g = i * STEP_E + k
                        wait(pe, mix_ready, g + 1)
                        wait(pe, mixT_ready, 2 * (g - 1))
                        for h in range(2):
                            for b in range(GB):
                                at = mix_at(k, b, h)
                                last = pe.transpose(ps_t[k % 2][h][0:HSL, b * T:(b + 1) * T], at, w["ident"][0:T, 0:T])
                        last.then_inc(mixT_done, 1)
                    if mixing:
                        g = (i - 1) * STEP_E + k
                        wait(pe, mixT_ready, 2 * (g + 1))
                        wait(pe, slots_in[k], 32 * i)
                        wait(pe, out_ready, 2 * (g - 1))
                        for b in range(GB):
                            for h in range(2):
                                last = pe.matmul(ps_c[k % 2][b // 2][0:T, b % 2 * C:(b % 2 + 1) * C],
                                                 mixT[:, k, h, b * T:(b + 1) * T], slots[:, k, h, b * C:(b + 1) * C],
                                                 start=(h == 0), stop=(h == 1))
                        last.then_inc(sum_done, 1)

            def mix_at(k, b, h):
                return mix[:, k, b * E + h * E // 2:b * E + (h + 1) * E // 2, :].rearrange("p e s -> p (e s)")

            in_turns(pe, turn)

        @block.scalar
        def _(act):
            def turn(i):
                for k in range(STEP_E):
                    g = i * STEP_E + k
                    wait(act, mixT_done, g + 1)
                    wait(act, sum_done, g - STEP_E + 1)
                    for h in range(2):
                        act.copy(mixT[:, k, h], ps_t[k % 2][h][0:HSL, 0:GT]).then_inc(mixT_ready, 1)

            turn(0)
            with act.Fori(1, TURNS_E) as i:
                turn(i)

        @block.vector
        def _(dve):
            def hot_of(g, k):
                wait(dve, mix_ready, g - STEP_E + 1)
                at = place[:, bass.ds(g * GB * E, GB * E)].rearrange("p (n o) -> p n o", o=1)
                dve.tensor_tensor(hot[:, k], w["slot_no"][0:T], at.to_broadcast((T, GB * E, CAP)),
                                  ALU.is_equal).then_inc(hot_done, 1)

            def turn(i, mix=True, mixing=True, ahead=True):
                for k in range(STEP_E):
                    if mix and (ahead or k + 2 < STEP_E):
                        hot_of(i * STEP_E + k + 2, (k + 2) % STEP_E)
                    if mixing:
                        g = (i - 1) * STEP_E + k
                        dve.wait_ge(sum_done, g + 1)
                        wait(dve, h2_in[k], 16 * i)
                        wait(dve, out_stored[k], 16 * (i - 1))
                        for n in range(2):
                            dve.tensor_tensor(out[:, k, 2 * n:2 * n + 2],
                                              ps_c[k % 2][n][0:T, :].rearrange("p (b c) -> p b c", b=2),
                                              h2[:, k, 2 * n:2 * n + 2], ALU.add).then_inc(out_ready, 1)

            hot_of(0, 0)
            hot_of(1, 1)
            turn(0, mixing=False)
            turn(1)
            with dve.Fori(2, TURNS_E - 1) as i:
                turn(i)
            turn(TURNS_E - 1, ahead=False)
            turn(TURNS_E, mix=False)


def build(nc, A, result):
    scratch = {
        "taps": nc.dram_tensor("taps_scratch", (1, LPAD), F32).ap(),
        "kern": nc.dram_tensor("kern_scratch", (C, LPAD), F32).ap(),
        "h1": nc.dram_tensor("h1_scratch", (T, B, C), F32).ap(),
        "y": nc.dram_tensor("y_scratch", (T, B, C), F32).ap(),
        "h2": nc.dram_tensor("h2_scratch", (T, B, C), F32).ap(),
        "rows": nc.dram_tensor("rows_scratch", (P, CC * E, B * CAP), F32).ap(),
        "slots": nc.dram_tensor("slots_scratch", (SL, B, C), F32).ap(),
    }
    with nc.sbuf_tensor("xn", [T, B, C], F32) as xn:
        phase_tokens(nc, A, scratch, xn)
        phase_states(nc, scratch, xn)
    with ExitStack() as ctx:
        def sb(name, shape, dt=F32):
            return ctx.enter_context(nc.sbuf_tensor(name, shape, dt))

        place = sb("place", [T, B * E])
        gate = sb("gate", [T, B * E])
        w = {"ident": sb("ident", [P, P]), "earlier": sb("earlier", [T, T], BF16),
             "slot_no": sb("slot_no", [P, GB * E, CAP]), "rank": sb("rank", [P, GB, E])}
        with ExitStack() as router:
            def rsb(name, shape, dt=F32R):
                return router.enter_context(nc.sbuf_tensor(name, shape, dt))

            w |= {"w1_hi": rsb("w1_hi", [P, CC, HID]), "w1_lo": rsb("w1_lo", [P, CC, HID]),
                  "w2_hi": rsb("w2_hi", [P, HC, HID]), "w2_lo": rsb("w2_lo", [P, HC, HID]),
                  "w3": rsb("w3", [P, HC, 2 * E]),
                  "rb1": rsb("rb1", [P, HC], F32), "rb2": rsb("rb2", [P, HC], F32), "rb3": rsb("rb3", [P, E], F32)}
            phase_router_weights(nc, A, w)
            phase_router(nc, scratch, w, place, gate)
        phase_experts(nc, A, scratch, w)
        phase_combine(nc, scratch, w, place, gate, result)


_INS = ["x", "L0_tok_Wv", "L0_tok_bv", "L0_tok_Wo", "L0_tok_bo", "L0_tok_decay_w", "L0_attn_log_dt",
        "L0_attn_log_A_real", "L0_attn_A_imag", "L0_attn_C", "L0_attn_D", "L0_ffn_rW1", "L0_ffn_rb1", "L0_ffn_rW2",
        "L0_ffn_rb2", "L0_ffn_rW3", "L0_ffn_rb3", "L0_ffn_eW1", "L0_ffn_eb1", "L0_ffn_eW2", "L0_ffn_eb2"]


def kernel(**inputs):
    import numpy as _np
    import concourse.bacc as _bacc
    from concourse.bass_utils import run_bass_kernel_spmd as _run

    nc = _bacc.Bacc("TRN2", target_bir_lowering=False, num_devices=1)
    arrays, args = {}, {}
    for name in _INS:
        a = _np.ascontiguousarray(inputs[name])
        arrays[f"in_{name}"] = a
        args[name] = nc.dram_tensor(f"in_{name}", a.shape, mybir.dt.from_np(a.dtype), kind="ExternalInput").ap()
    result = nc.dram_tensor("result", (B, T, C), F32, kind="ExternalOutput").ap()
    build(nc, args, result)
    r = _run(nc, [arrays], core_ids=[0])
    return r.results[0]["result"]
```

```python
from contextlib import ExitStack

import concourse.bass as bass
from concourse import mybir

F32 = mybir.dt.float32
F32R = mybir.dt.float32r
BF16 = mybir.dt.bfloat16
I32 = mybir.dt.int32
ALU = mybir.AluOpType
ACT = mybir.ActivationFunctionType
AX = mybir.AxisListType.X

P = 128
B, TIN, C = 128, 125, 256
T = TIN + 1
TAPS = 32
NM = 32
CC = C // P
HID = 1024
HC = HID // P
E = 8
CAP = int(T / E * 1.25)
SL = E * CAP
HSL = SL // 2
EPS = 1e-5

GB = 4
NG = B // GB
GT = GB * T
PAIRS = B // 2
STEP = 4
TURNS = PAIRS // STEP
LPAD = 256

LOG2E = 1.4426950408889634
LN2_HI = 0.693145751953125
LN2_LO = 1.4286068203094172e-06
ROUND = 12582912.0
TWO_PI = 6.283185307179586
PI2_A = 6.28125
PI2_B = 0.0019350051879882812
PI2_C = 3.019915981956753e-07
PI_BELOW = 3.1415925


def wait(eng, sem, value):
    if isinstance(value, int) and value <= 0:
        return
    eng.wait_ge(sem, value)


def wait_apart(eng, sem, value, passed):
    wait(eng, sem, value)
    if not isinstance(value, int):
        eng.sem_inc(passed, 1)


class Chain:

    def __init__(self, eng, sem, base=0):
        self.eng, self.sem, self.base, self.n = eng, sem, base, 0

    def step(self, ins):
        ins.then_inc(self.sem, 1)
        self.n += 1
        self.eng.wait_ge(self.sem, self.base + self.n)


def split(chain, eng, hi, lo, src):
    chain.step(eng.tensor_copy(hi, src))
    chain.step(eng.tensor_tensor(lo, src, hi.bitcast(F32), ALU.subtract))


def matmul3(pe, out, w_hi, w_lo, x_hi, x_lo, start, stop):
    pe.matmul(out, w_hi, x_hi, start=start, stop=False)
    pe.matmul(out, w_hi, x_lo, start=False, stop=False)
    return pe.matmul(out, w_lo, x_hi, start=False, stop=stop)


def exp_steps(ch, dve, x, t, k, r, p, scale_bits):
    ch.step(dve.tensor_scalar(t, x, LOG2E, ROUND, ALU.mult, ALU.add))
    ch.step(dve.tensor_scalar(k, t, -ROUND, None, ALU.add))
    ch.step(dve.tensor_scalar(k, k, 127.0, -126.0, ALU.min, ALU.max))
    ch.step(dve.scalar_tensor_tensor(r, k, -LN2_HI, x, ALU.mult, ALU.add))
    ch.step(dve.scalar_tensor_tensor(r, k, -LN2_LO, r, ALU.mult, ALU.add))
    ch.step(dve.tensor_scalar(p, r, 1.0 / 5040.0, None, ALU.mult))
    for fact in (720.0, 120.0, 24.0, 6.0, 2.0, 1.0):
        ch.step(dve.scalar_tensor_tensor(p, p, 1.0 / fact, r, ALU.add, ALU.mult))
    ch.step(dve.tensor_scalar(scale_bits, k, 127.0, 8388608.0, ALU.add, ALU.mult))
    ch.step(dve.scalar_tensor_tensor(p, p, 1.0, scale_bits.bitcast(F32), ALU.add, ALU.mult))


def rstd_steps(ch, dve, var_in, var, y, t):
    ch.step(dve.tensor_scalar(var, var_in, EPS, None, ALU.add))
    ch.step(dve.tensor_scalar(y.bitcast(I32), var.bitcast(I32), -0.5, 1597463007.0, ALU.mult, ALU.add))
    for _ in range(3):
        ch.step(dve.tensor_tensor(t, y, y, ALU.mult))
        ch.step(dve.scalar_tensor_tensor(t, t, -0.5, var, ALU.mult, ALU.mult))
        ch.step(dve.scalar_tensor_tensor(y, t, 1.5, y, ALU.add, ALU.mult))


RSTD_STEPS = 2 + 3 * 3


def phase_tokens(nc, A, scratch, xn):
    h1_dram, kern_dram, taps_dram = scratch["h1"], scratch["kern"], scratch["taps"]
    with ExitStack() as ctx:
        def sb(name, shape, dt=F32):
            return ctx.enter_context(nc.sbuf_tensor(name, shape, dt))

        def sem(name):
            return ctx.enter_context(nc.semaphore(name))

        ident = sb("a_ident", [P, P])
        ones = sb("a_ones", [P, P])
        tap_row = sb("tap_row", [1, LPAD])
        tap_all = sb("tap_all", [P, TAPS])
        tap_sum = sb("tap_sum", [P, 1])
        conv_rev = sb("conv_rev", [TIN, T])
        conv = sb("conv", [TIN, T])
        wv = sb("wv", [P, CC, C])
        wo = sb("wo", [P, CC, C])
        woT = sb("woT", [P, CC, C])
        bv = sb("bv", [P, CC])
        bv_sum = sb("bv_sum", [P, CC])
        bv_rows = sb("bv_rows", [P, CC, T])
        bo_row = sb("bo_row", [1, C])
        PART = 32
        sel_f32 = sb("sel_f32", [2 * PART, T])
        sel = sb("sel", [2 * PART, T], F32R)
        bias = sb("bias", [2 * PART, 2, C], F32R)
        w_hi = sb("w_hi", [P, CC, C], F32R)
        w_lo = sb("w_lo", [P, CC, C], F32R)

        x_in = sb("x_in", [TIN, STEP, 2, C])
        s_hi = sb("s_hi", [P, STEP, 2 * CC * T], F32R)
        s_lo = sb("s_lo", [P, STEP, 2 * CC * T], F32R)
        h1 = sb("h1", [T, STEP, 2, C])
        stats = sb("stats", [T, 2 * STEP, 6])
        mv = sb("mv", [T, 2 * STEP, 2])
        var = sb("var", [T, 2 * STEP])
        rstd = sb("rstd", [T, 2 * STEP])
        newton = sb("newton", [T, 2 * STEP])
        shift = sb("shift", [T, 2 * STEP])

        logs = sb("logs", [P, 2 + CC * NM])
        exps = sb("exps", [P, 2 + CC * NM])
        a_im = sb("a_im", [P, CC, NM])
        c_in = sb("c_in", [P, CC, NM, 2])
        d_skip = sb("d_skip", [P, CC])
        s0 = sb("s0", [P, 2 + CC * NM])
        s1 = sb("s1", [P, 2 + CC * NM])
        s2 = sb("s2", [P, 2 + CC * NM])
        s3 = sb("s3", [P, 2 + CC * NM], I32)
        g = {n: sb("g_" + n, [P, CC, NM]) for n in
             ("are", "xr", "yi", "mag", "sin", "cos", "zr", "zi", "den", "ir", "ii", "cr", "ci", "t", "u")}
        NA, NB = 8, 16
        vr = sb("vr", [P, CC, NB, NM])
        vi = sb("vi", [P, CC, NB, NM])
        ur = sb("ur", [P, CC, NA, NM])
        ui = sb("ui", [P, CC, NA, NM])
        pr = [sb(f"pr{n}", [P, CC, NM]) for n in range(2)]
        pi = [sb(f"pi{n}", [P, CC, NM]) for n in range(2)]
        q0 = sb("q0", [P, CC, NB // 2, NM])
        AH = NA // 4
        prod = sb("prod", [P, AH, NB, NM])
        prod2 = sb("prod2", [P, AH, NB, NM])
        kern = wo

        ps_s = [ctx.enter_context(nc.psum_tensor(f"ps_s{n}", [P, 512], F32)) for n in range(STEP)]
        ps_h = [ctx.enter_context(nc.psum_tensor(f"ps_h{n}", [P, 512], F32)) for n in range(STEP)]
        ps_w, ps_b = ps_h[0:CC], ps_h[CC]

        consts_made = sem("consts_made")
        taps_in = sem("taps_in")
        taps_out = sem("taps_out")
        conv_in = sem("conv_in")
        weights_in = sem("weights_in")
        modes_in = sem("modes_in")
        woT_done = sem("woT_done")
        woT_copied = sem("woT_copied")
        w_done = sem("w_done")
        setup = sem("a_setup")
        setup_pool = sem("a_setup_pool")
        weights_ready = sem("weights_ready")
        angles_ready = sem("angles_ready")
        sines_ready = sem("sines_ready")
        modes_ready = sem("modes_ready")
        kern_ready = sem("kern_ready")
        kern_out = sem("kern_out")
        x_loaded = [sem(f"x_loaded{k}") for k in range(STEP)]
        h1_stored = [sem(f"h1_stored{k}") for k in range(STEP)]
        conv_done = sem("conv_done")
        s_hi_ready = sem("s_hi_ready")
        s_lo_ready = sem("s_lo_ready")
        proj_done = sem("proj_done")
        h1_ready = sem("h1_ready")
        stats_done = sem("stats_done")
        aggr_done = sem("aggr_done")
        rstd_chain = sem("rstd_chain")
        norm_ready = sem("norm_ready")
        norm_done = sem("norm_done")
        sel_made = sem("sel_made")
        passed_act = sem("a_passed_act")
        passed_dve = sem("a_passed_dve")

        def load_x(sp, u, k):
            for t in (slice(0, 112), slice(112, TIN)):
                sp.dma_start(x_in[t, k], A["x"][bass.ds(2 * u, 2), t].rearrange("b t c -> t b c"))\
                  .then_inc(x_loaded[k], 16)

        block = ctx.enter_context(nc.Block())

        @block.sync
        def _(sp):
            sp.dma_start(wo[:], A["L0_tok_Wo"].rearrange("(k p) n -> p k n", p=P)).then_inc(weights_in, 16)
            sp.dma_start(wv[:], A["L0_tok_Wv"].rearrange("(k p) n -> p k n", p=P)).then_inc(weights_in, 16)
            sp.dma_start(bo_row[:], A["L0_tok_bo"].rearrange("(a n) -> a n", a=1)).then_inc(weights_in, 16)
            sp.dma_start(tap_all[:], bass.AP(A["L0_tok_decay_w"].tensor, 0, [[0, P], [1, TAPS]]))\
              .then_inc(weights_in, 16)
            for k in range(STEP):
                load_x(sp, k, k)

            def turn(i, load=True, store=True):
                if load:
                    for k in range(STEP):
                        wait(sp, conv_done, i * STEP + k + 1)
                        load_x(sp, (i + 1) * STEP + k, k)
                if store:
                    for k in range(STEP):
                        v = (i - 1) * STEP + k
                        wait(sp, h1_ready, v + 1)
                        sp.dma_start(h1_dram[:, bass.ds(2 * v, 2), :], h1[:, k]).then_inc(h1_stored[k], 16)

            turn(0, store=False)
            with sp.Fori(1, TURNS - 1) as i:
                turn(i)
            turn(TURNS - 1, load=False)
            turn(TURNS, load=False)
            for k in range(STEP):
                sp.wait_ge(h1_stored[k], 16 * TURNS)
            sp.wait_ge(kern_out, 16)

        @block.gpsimd
        def _(pool):
            pool.memset(tap_row[:], 0.0).then_inc(consts_made, 1)
            pool.memset(ident[:], 0.0).then_inc(setup_pool, 1)
            pool.memset(ones[:], 1.0).then_inc(consts_made, 1)
            pool.memset(sel_f32[:], 0.0).then_inc(sel_made, 1)
            pool.wait_ge(setup_pool, 1)
            pool.affine_select(out=ident[:], in_=ident[:], compare_op=ALU.not_equal, fill=1.0, base=0,
                               pattern=[[-1, P]], channel_multiplier=1).then_inc(consts_made, 1)
            pool.wait_ge(consts_made, 3)
            for n in range(2):
                pool.wait_ge(sel_made, n + 1)
                pool.memset(sel_f32[PART * n:PART * n + 1, :], 1.0).then_inc(sel_made, 1)
            pool.wait_ge(sel_made, 3)
            pool.wait_ge(woT_done, 1)
            pool.memset(kern[:], 0.0).then_inc(setup_pool, 1)
            ch = Chain(pool, setup_pool, 2)
            pool.wait_ge(setup_pool, 2)
            pool.wait_ge(modes_ready, 1)

            def cmul(outr, outi, xr, xi, yr, yi, tmp):
                ch.step(pool.tensor_tensor(outr, xr, yr, ALU.mult))
                ch.step(pool.tensor_tensor(tmp, xi, yi, ALU.mult))
                ch.step(pool.tensor_tensor(outr, outr, tmp, ALU.subtract))
                ch.step(pool.tensor_tensor(outi, xr, yi, ALU.mult))
                ch.step(pool.tensor_tensor(tmp, xi, yr, ALU.mult))
                ch.step(pool.tensor_tensor(outi, outi, tmp, ALU.add))

            def wide(x, m):
                return x[:].rearrange("p g (o n) -> p g o n", o=1).to_broadcast((P, CC, m, NM))

            ch.step(pool.memset(vr[:, :, NB - 1, :], 1.0))
            ch.step(pool.memset(vi[:, :, NB - 1, :], 0.0))
            zr, zi = g["zr"], g["zi"]
            m, at = 1, 0
            while m < NB:
                lo, mid = NB - 2 * m, NB - m
                if m == 1:
                    ch.step(pool.tensor_copy(vr[:, :, lo, :], zr[:]))
                    ch.step(pool.tensor_copy(vi[:, :, lo, :], zi[:]))
                else:
                    cmul(vr[:, :, lo:mid, :], vi[:, :, lo:mid, :], vr[:, :, mid:NB, :], vi[:, :, mid:NB, :],
                         wide(zr, m), wide(zi, m), q0[:, :, 0:m, :])
                cmul(pr[at][:], pi[at][:], zr[:], zi[:], zr[:], zi[:], q0[:, :, 0, :])
                zr, zi, at, m = pr[at], pi[at], 1 - at, 2 * m
            ch.step(pool.tensor_copy(ur[:, :, NA - 1, :], g["cr"][:]))
            ch.step(pool.tensor_copy(ui[:, :, NA - 1, :], g["ci"][:]))
            m = 1
            while m < NA:
                lo, mid = NA - 2 * m, NA - m
                cmul(ur[:, :, lo:mid, :], ui[:, :, lo:mid, :], ur[:, :, mid:NA, :], ui[:, :, mid:NA, :],
                     wide(zr, m), wide(zi, m), q0[:, :, 0:m, :])
                if 2 * m < NA:
                    cmul(pr[at][:], pi[at][:], zr[:], zi[:], zr[:], zi[:], q0[:, :, 0, :])
                    zr, zi, at = pr[at], pi[at], 1 - at
                m *= 2
            for c in range(CC):
                for a in range(0, NA, AH):
                    def u_of(x):
                        return x[:, c, a:a + AH, :].rearrange("p a (o n) -> p a o n", o=1)\
                                                   .to_broadcast((P, AH, NB, NM))

                    def v_of(x):
                        return x[:, c, :, :].rearrange("p (o b) n -> p o b n", o=1).to_broadcast((P, AH, NB, NM))

                    ch.step(pool.tensor_tensor(prod[:], u_of(ur), v_of(vr), ALU.mult))
                    ch.step(pool.tensor_tensor(prod2[:], u_of(ui), v_of(vi), ALU.mult))
                    ch.step(pool.tensor_tensor(prod[:], prod[:], prod2[:], ALU.subtract))
                    n = NM // 2
                    while n > 1:
                        ch.step(pool.tensor_tensor(prod[:, :, :, 0:n], prod[:, :, :, 0:n], prod[:, :, :, n:2 * n],
                                                   ALU.add))
                        n //= 2
                    ch.step(pool.tensor_tensor(
                        kern[:, c, NB * a:NB * (a + AH)].rearrange("p (a b) -> p a b", a=AH),
                        prod[:, :, :, 0], prod[:, :, :, 1], ALU.add))
            for c in range(CC):
                last = pool.tensor_tensor(kern[:, c, 127:128], kern[:, c, 127:128], d_skip[:, c:c + 1], ALU.add)
                ch.step(last)
            pool.dma_start(kern_dram.rearrange("(c p) l -> p c l", p=P)[:, :, 0:T + P],
                           kern[:, :, P - T:2 * P]).then_inc(kern_out, 16)

        @block.scalar
        def _(act):
            act.dma_start(bv[:], A["L0_tok_bv"].rearrange("(c p) -> p c", p=P),
                          allow_slow_non_contiguous=True).then_inc(weights_in, 16)
            act.wait_ge(consts_made, 1)
            act.dma_start(tap_row[0:1, TIN - TAPS:TIN], A["L0_tok_decay_w"].rearrange("(a n) -> a n", a=1))\
               .then_inc(taps_in, 16)
            act.wait_ge(taps_in, 16)
            act.dma_start(taps_dram, tap_row[:]).then_inc(taps_out, 16)
            act.wait_ge(taps_out, 16)
            act.dma_start(conv_rev[:], bass.AP(taps_dram.tensor, 0, [[1, TIN], [1, T]])).then_inc(conv_in, 16)
            act.dma_start(logs[:, 0:2], A["L0_attn_log_dt"].rearrange("(c p) -> p c", p=P),
                          allow_slow_non_contiguous=True).then_inc(modes_in, 16)
            act.dma_start(logs[:, 2:2 + CC * NM].rearrange("p (c n) -> p c n", c=CC),
                          A["L0_attn_log_A_real"].rearrange("(c p) n -> p c n", p=P)).then_inc(modes_in, 16)
            act.dma_start(a_im[:], A["L0_attn_A_imag"].rearrange("(c p) n -> p c n", p=P)).then_inc(modes_in, 16)
            act.dma_start(c_in[:], A["L0_attn_C"].rearrange("(c p) n r -> p c n r", p=P)).then_inc(modes_in, 16)
            act.dma_start(d_skip[:], A["L0_attn_D"].rearrange("(c p) -> p c", p=P),
                          allow_slow_non_contiguous=True).then_inc(modes_in, 16)

            def turn(i, conv=True, proj=True, norm=True):
                if conv:
                    for k in range(STEP):
                        u = i * STEP + k
                        act.wait_ge(conv_done, u + 1)
                        wait(act, proj_done, u - STEP + 1)
                        act.activation(s_hi[:, k], ps_s[k][:, 0:2 * CC * T], ACT.Copy).then_inc(s_hi_ready, 1)
                for k in range(STEP):
                    if norm:
                        v = (i - 2) * STEP + k
                        wait_apart(act, norm_ready, i - 1, passed_act)
                        for j in range(2):
                            n = 2 * k + j
                            act.activation(xn[:, bass.ds(2 * v + j, 1), :].rearrange("p o c -> p (o c)"), h1[:, k, j],
                                           ACT.Identity, bias=shift[:, n:n + 1], scale=rstd[:, n:n + 1])\
                               .then_inc(norm_done, 1)
                    if proj:
                        v = (i - 1) * STEP + k
                        act.wait_ge(proj_done, v + 1)
                        wait(act, norm_done, 2 * (v - STEP + 1))
                        wait(act, h1_stored[k], 16 * (i - 1))
                        act.copy(h1[:, k], ps_h[k][0:T, :].rearrange("p (b c) -> p b c", b=2)).then_inc(h1_ready, 1)

            turn(0, proj=False, norm=False)
            act.wait_ge(angles_ready, 1)
            act.activation(g["sin"][:], g["yi"][:], ACT.Sin).then_inc(sines_ready, 1)
            act.activation(g["cos"][:], g["t"][:], ACT.Sin).then_inc(sines_ready, 1)
            turn(1, norm=False)
            with act.Fori(2, TURNS) as i:
                turn(i)
            turn(TURNS, conv=False)
            turn(TURNS + 1, conv=False, proj=False)

        @block.vector
        def _(dve):
            ch = Chain(dve, setup)
            dve.wait_ge(weights_in, 80)
            ch.step(dve.reduce_sum(tap_sum[:], tap_all[:], AX))
            ch.step(dve.tensor_scalar(bv_sum[:], bv[:], tap_sum[:, 0:1], None, ALU.mult))
            dve.wait_ge(consts_made, 3)
            for c in range(CC):
                ch.step(dve.tensor_scalar(bv_rows[:, c, :], ones[:, 0:T], bv_sum[:, c:c + 1], None, ALU.mult))
            dve.wait_ge(woT_done, 1)
            for c in range(CC):
                dve.tensor_copy(woT[:, c, :], ps_w[c][:, 0:C]).then_inc(woT_copied, 1)
            dve.wait_ge(conv_in, 16)
            dve.tensor_copy(conv[:], conv_rev[:, ::-1]).then_inc(weights_ready, 1)
            dve.wait_ge(w_done, 1)
            for c in range(CC):
                split(ch, dve, w_hi[:, c, :], w_lo[:, c, :], ps_w[c][:, 0:C])
            dve.wait_ge(sel_made, 3)
            dve.tensor_copy(sel[:], sel_f32[:])
            for j in range(2):
                ch.step(dve.tensor_copy(bias[:, j], ps_b[0:2 * PART, 0:C]))
            for j in range(2):
                low = slice(PART, 2 * PART)
                ins = dve.tensor_tensor(bias[low, j], ps_b[low, 0:C], bias[low, j].bitcast(F32), ALU.subtract)
            ins.then_inc(weights_ready, 1)
            def modes():
                dve.wait_ge(modes_in, 80)
                exp_steps(ch, dve, logs[:], s0[:], s1[:], s2[:], exps[:], s3[:])
                m = {n: x[:].rearrange("p c n -> p (c n)") for n, x in g.items()}
                for c in range(CC):
                    ch.step(dve.tensor_scalar(g["are"][:, c, :], exps[:, 2 + c * NM:2 + (c + 1) * NM], -1.0, None, ALU.mult))
                    ch.step(dve.tensor_scalar(g["xr"][:, c, :], g["are"][:, c, :], exps[:, c:c + 1], None, ALU.mult))
                    ch.step(dve.tensor_scalar(g["yi"][:, c, :], a_im[:, c, :], exps[:, c:c + 1], None, ALU.mult))
                n = CC * NM
                ch.step(dve.tensor_scalar(m["t"], m["yi"], 1.0 / TWO_PI, ROUND, ALU.mult, ALU.add))
                ch.step(dve.tensor_scalar(m["t"], m["t"], -ROUND, None, ALU.add))
                for part in (PI2_A, PI2_B, PI2_C):
                    ch.step(dve.scalar_tensor_tensor(m["yi"], m["t"], -part, m["yi"], ALU.mult, ALU.add))
                ch.step(dve.tensor_scalar(m["yi"], m["yi"], PI_BELOW, -PI_BELOW, ALU.min, ALU.max))
                ch.step(dve.tensor_scalar(m["u"], m["yi"], -1.0, None, ALU.mult))
                ch.step(dve.tensor_tensor(m["u"], m["u"], m["yi"], ALU.max))
                ch.step(dve.tensor_scalar(m["t"], m["u"], -1.0, TWO_PI / 4, ALU.mult, ALU.add))
                ch.step(dve.tensor_copy(m["u"], m["t"]))
                dve.sem_inc(angles_ready, 1)
                exp_steps(ch, dve, m["xr"], s0[:, 0:n], s1[:, 0:n], s2[:, 0:n], m["mag"], s3[:, 0:n])
                im = a_im[:].rearrange("p c n -> p (c n)")
                ch.step(dve.tensor_tensor(m["den"], m["are"], m["are"], ALU.mult))
                ch.step(dve.tensor_tensor(m["u"], im, im, ALU.mult))
                ch.step(dve.tensor_tensor(m["den"], m["den"], m["u"], ALU.add))
                ch.step(dve.reciprocal(m["u"], m["den"]))
                ch.step(dve.tensor_tensor(m["ir"], m["are"], m["u"], ALU.mult))
                ch.step(dve.scalar_tensor_tensor(m["ii"], im, -1.0, m["u"], ALU.mult, ALU.mult))
                dve.wait_ge(sines_ready, 2)
                ch.step(dve.tensor_tensor(m["zr"], m["mag"], m["cos"], ALU.mult))
                ch.step(dve.tensor_tensor(m["zi"], m["mag"], m["sin"], ALU.mult))
                ch.step(dve.tensor_scalar(m["mag"], m["zr"], -1.0, None, ALU.add))
                ch.step(dve.tensor_tensor(m["den"], m["mag"], m["ir"], ALU.mult))
                ch.step(dve.tensor_tensor(m["t"], m["zi"], m["ii"], ALU.mult))
                ch.step(dve.tensor_tensor(m["den"], m["den"], m["t"], ALU.subtract))
                ch.step(dve.tensor_tensor(m["u"], m["mag"], m["ii"], ALU.mult))
                ch.step(dve.tensor_tensor(m["t"], m["zi"], m["ir"], ALU.mult))
                ch.step(dve.tensor_tensor(m["u"], m["u"], m["t"], ALU.add))
                c_re = c_in[:].rearrange("p c n r -> p (c n) r")[:, :, 0]
                c_im = c_in[:].rearrange("p c n r -> p (c n) r")[:, :, 1]
                ch.step(dve.tensor_tensor(m["cr"], m["den"], c_re, ALU.mult))
                ch.step(dve.tensor_tensor(m["t"], m["u"], c_im, ALU.mult))
                ch.step(dve.tensor_tensor(m["cr"], m["cr"], m["t"], ALU.subtract))
                ch.step(dve.tensor_scalar(m["cr"], m["cr"], 2.0, None, ALU.mult))
                ch.step(dve.tensor_tensor(m["ci"], m["den"], c_im, ALU.mult))
                ch.step(dve.tensor_tensor(m["t"], m["u"], c_re, ALU.mult))
                ch.step(dve.tensor_tensor(m["ci"], m["ci"], m["t"], ALU.add))
                dve.tensor_scalar(m["ci"], m["ci"], 2.0, None, ALU.mult).then_inc(modes_ready, 1)

            def turn(i, conv=True, proj=True):
                if conv:
                    for k in range(STEP):
                        u = i * STEP + k
                        dve.wait_ge(s_hi_ready, u + 1)
                        dve.tensor_tensor(s_lo[:, k], ps_s[k][:, 0:2 * CC * T], s_hi[:, k].bitcast(F32),
                                          ALU.subtract).then_inc(s_lo_ready, 1)
                if proj:
                    for k in range(STEP):
                        v = (i - 1) * STEP + k
                        dve.wait_ge(h1_ready, v + 1)
                        for j in range(2):
                            dve.bn_stats(stats[:, 2 * k + j, :], h1[:, k, j]).then_inc(stats_done, 1)
                    v = (i - 1) * STEP
                    wait_apart(dve, stats_done, 2 * (v + STEP), passed_dve)
                    for n in range(2 * STEP):
                        dve.bn_aggr(mv[:, n, :], stats[:, n, :]).then_inc(aggr_done, 1)
                    dve.wait_ge(aggr_done, 2 * (v + STEP))
                    wait(dve, norm_done, 2 * v)
                    ch = Chain(dve, rstd_chain, (i - 1) * RSTD_STEPS)
                    rstd_steps(ch, dve, mv[:, :, 1], var[:], rstd[:], newton[:])
                    dve.scalar_tensor_tensor(shift[:], mv[:, :, 0], -1.0, rstd[:], ALU.mult, ALU.mult)\
                       .then_inc(norm_ready, 1)

            turn(0, proj=False)
            modes()
            turn(1)
            with dve.Fori(2, TURNS) as i:
                turn(i)
            turn(TURNS, conv=False)

        @block.tensor
        def _(pe):
            pe.wait_ge(consts_made, 3)
            pe.wait_ge(weights_in, 80)
            for m in range(CC):
                for e in range(CC):
                    last = pe.transpose(ps_w[m][:, e * P:(e + 1) * P], wo[:, e, m * P:(m + 1) * P], ident[:])
            last.then_inc(woT_done, 1)
            pe.wait_ge(woT_copied, 2)
            for m in range(CC):
                pe.matmul(ps_b[0:T, 0:C], bv_rows[:, m, :], woT[:, m, :], start=(m == 0), stop=False)
            pe.matmul(ps_b[0:T, 0:C], ones[0:1, 0:T], bo_row[:], start=False, stop=True)
            for d in range(CC):
                for m in range(CC):
                    last = pe.matmul(ps_w[d][:, 0:C], wv[:, m, d * P:(d + 1) * P], woT[:, m, :],
                                     start=(m == 0), stop=(m == CC - 1))
            last.then_inc(w_done, 1)
            pe.wait_ge(weights_ready, 2)

            def turn(i, conv_=True, proj=True):
                if conv_:
                    for k in range(STEP):
                        u = i * STEP + k
                        pe.wait_ge(x_loaded[k], 32 * (i + 1))
                        wait(pe, s_lo_ready, u - STEP + 1)
                        for j in range(2):
                            for c in range(CC):
                                n = (j * CC + c) * T
                                last = pe.matmul(ps_s[k][:, n:n + T], x_in[:, k, j, c * P:(c + 1) * P], conv[:],
                                                 start=True, stop=True)
                        last.then_inc(conv_done, 1)
                if proj:
                    for k in range(STEP):
                        v = (i - 1) * STEP + k
                        wait(pe, s_lo_ready, v + 1)
                        wait(pe, h1_ready, v - STEP + 1)
                        pe.matmul(ps_h[k][0:T, :], sel[:], bias[:].rearrange("p b c -> p (b c)"), start=True, stop=False)
                        for j in range(2):
                            for c in range(CC):
                                n = (j * CC + c) * T
                                last = matmul3(pe, ps_h[k][0:T, j * C:(j + 1) * C], s_hi[:, k, n:n + T],
                                               s_lo[:, k, n:n + T], w_hi[:, c, :], w_lo[:, c, :], False,
                                               j == 1 and c == CC - 1)
                        last.then_inc(proj_done, 1)

            turn(0, proj=False)
            turn(1)
            with pe.Fori(2, TURNS) as i:
                turn(i)
            turn(TURNS, conv_=False)


def phase_states(nc, A, scratch, xn, raw):
    CH = 4
    UNITS = 8
    TURNS_B = C // (CH * UNITS)
    LD = 2
    SLOTS = UNITS // LD
    kern_dram, y_dram = scratch["kern"], scratch["y"]
    with ExitStack() as ctx:
        rows_in = ctx.enter_context(nc.sbuf_tensor("rows_in", [T, UNITS * CH, P], F32))
        toep = ctx.enter_context(nc.sbuf_tensor("toep", [T, UNITS * CH, T], F32))
        ps = [ctx.enter_context(nc.psum_tensor(f"ps_y{n}", [P, CH, P], F32)) for n in range(UNITS)]
        toep_loaded = [ctx.enter_context(nc.semaphore(f"toep_loaded{n}")) for n in range(SLOTS)]
        toep_ready = ctx.enter_context(nc.semaphore("toep_ready"))
        y_done = ctx.enter_context(nc.semaphore("y_done"))
        y_ready = ctx.enter_context(nc.semaphore("y_ready"))
        y_stored = ctx.enter_context(nc.semaphore("y_stored"))
        raw_in = ctx.enter_context(nc.semaphore("raw_in"))
        passed_dve = ctx.enter_context(nc.semaphore("b_passed_dve"))
        block = ctx.enter_context(nc.Block())

        def store_y(eng, half):
            c = slice(half * P, (half + 1) * P)
            for n in range(4):
                b = slice(n * B // 4, (n + 1) * B // 4)
                eng.dma_start(y_dram[:, b, c], xn[:, b, c]).then_inc(y_stored, 16)

        @block.sync
        def _(sp):
            def turn(i):
                for s in range(SLOTS):
                    wait(sp, toep_ready, (i - 1) * SLOTS + s + 1)
                    h = (i * UNITS + s * LD) * CH
                    rows = bass.AP(kern_dram.tensor, h * LPAD, [[1, T], [LPAD, LD * CH], [1, P]])
                    sp.dma_start(rows_in[:, s * LD * CH:(s + 1) * LD * CH, :], rows)\
                      .then_inc(toep_loaded[s], 16)

            turn(0)
            with sp.Fori(1, TURNS_B) as i:
                turn(i)
            sp.dma_start(raw["w1"][:], A["L0_ffn_rW1"].rearrange("(k p) n -> p k n", p=P)).then_inc(raw_in, 16)
            sp.dma_start(raw["w2"][:], A["L0_ffn_rW2"].rearrange("(k p) n -> p k n", p=P)).then_inc(raw_in, 16)
            sp.wait_ge(y_ready, C // CH)
            store_y(sp, 1)
            sp.wait_ge(raw_in, 32)
            sp.wait_ge(y_stored, 128)

        @block.vector
        def _(dve):
            def turn(i):
                for s in range(SLOTS):
                    dve.wait_ge(toep_loaded[s], 16 * (i + 1))
                    wait_apart(dve, y_done, (i - 1) * UNITS + (s + 1) * LD, passed_dve)
                    h = slice(s * LD * CH, (s + 1) * LD * CH)
                    dve.tensor_copy(toep[:, h, :], rows_in[:, h, T - 1::-1]).then_inc(toep_ready, 1)

            turn(0)
            with dve.Fori(1, TURNS_B) as i:
                turn(i)

        @block.tensor
        def _(pe):
            def turn(i):
                for n in range(UNITS):
                    if n % LD == 0:
                        pe.wait_ge(toep_ready, i * SLOTS + n // LD + 1)
                    wait(pe, y_ready, (i - 1) * UNITS + n + 1)
                    for c in range(CH):
                        h = (i * UNITS + n) * CH + c
                        last = pe.matmul(ps[n][0:T, c, :], toep[:, n * CH + c, :], xn[:, :, bass.ds(h, 1)].rearrange("p b o -> p (b o)"),
                                         start=True, stop=True)
                    last.then_inc(y_done, 1)

            turn(0)
            with pe.Fori(1, TURNS_B) as i:
                turn(i)

        @block.scalar
        def _(act):
            def turn(i):
                for n in range(UNITS):
                    h = (i * UNITS + n) * CH
                    act.wait_ge(y_done, i * UNITS + n + 1)
                    act.copy(xn[:, :, bass.ds(h, CH)], ps[n][0:T].rearrange("p h b -> p b h")).then_inc(y_ready, 1)

            turn(0)
            with act.Fori(1, TURNS_B // 2) as i:
                turn(i)
            act.wait_ge(y_ready, C // CH // 2)
            store_y(act, 0)
            with act.Fori(TURNS_B // 2, TURNS_B) as i:
                turn(i)


def phase_router(nc, A, scratch, w, raw, place, gate):
    h1_dram, y_dram, h2_dram, rows_dram = scratch["h1"], scratch["y"], scratch["h2"], scratch["rows"]
    NT = HC
    RELU = 4
    MM = 4
    with ExitStack() as ctx:
        def sb(name, shape, dt=F32, side="left"):
            return ctx.enter_context(nc.sbuf_tensor(name, shape, dt, side=side))

        def sem(name):
            return ctx.enter_context(nc.semaphore(name))

        h1 = sb("c_h1", [T, GB, C])
        y = sb("c_y", [T, GB, C])
        h2 = sb("c_h2", [T, GB, C])
        x2 = sb("c_x2", [T, GB, C])
        x2_part = [sb(f"x2_part{n}", [T, GB, C], BF16) for n in range(3)]
        x2_rest = sb("x2_rest", [T, GB, C])
        stats = sb("c_stats", [T, GB, 6])
        mv = sb("c_mv", [T, GB, 2])
        var = sb("c_var", [T, GB])
        rstd = sb("c_rstd", [T, GB])
        newton = sb("c_newton", [T, GB])
        shift = sb("c_shift", [T, GB])
        xT_hi = sb("xT_hi", [P, CC, GT], F32R)
        xT_lo = sb("xT_lo", [P, CC, GT], F32R)
        a1_hi = sb("a1_hi", [P, HC, GT], F32R)
        a1_lo = sb("a1_lo", [P, HC, GT], F32R)
        relu = sb("relu", [P, RELU, GT], side="right")
        a2_hi = sb("a2_hi", [P, HC, GT], F32R, side="right")
        a2_lo = sb("a2_lo", [P, HC, GT], F32R, side="right")
        raw3 = sb("raw3", [P, HC, E])
        logT = sb("logT", [2 * E, GT])
        logit = sb("logit", [T, GB, E])
        ex = sb("ex", [T, GB, E])
        prob = sb("prob", [T, GB, E])
        key = sb("key", [T, GB, E])
        first = sb("first", [T, GB, E])
        rest = sb("rest", [T, GB, E])
        chosen = sb("chosen", [T, GB, E])
        chosen_bf = sb("chosen_bf", [T, GB * E], BF16)
        m1 = sb("m1", [T, GB])
        m2 = sb("m2", [T, GB])
        onehot = sb("onehot", [T, GB * E, CAP], BF16)
        rows = sb("rows", [P, CC, E, GB, CAP])

        ps_m = [ctx.enter_context(nc.psum_tensor(f"ps_m{n}", [P, 512], F32)) for n in range(MM)]
        ps_x = [ctx.enter_context(nc.psum_tensor(f"ps_x{n}", [P, 512], F32)) for n in range(3)]
        ps_l = ps_x[2]
        ps_r = ctx.enter_context(nc.psum_tensor("ps_r", [P, 512], F32))
        logit_ps = ps_r[0:T, 0:GB * 2 * E].rearrange("p (b e) -> p b e", b=GB)
        pos_ps = ps_r[0:T, GB * 2 * E:GB * 3 * E]

        h1_in = sem("c_h1_in")
        y_in = sem("c_y_in")
        h2_ready = sem("c_h2_ready")
        h2_stored = sem("c_h2_stored")
        stats_done = sem("c_stats_done")
        aggr_done = sem("c_aggr_done")
        prep_chain = sem("prep_chain")
        norm_ready = sem("c_norm_ready")
        norm_done = sem("c_norm_done")
        part0_ready = sem("part0_ready")
        rest_ready = sem("rest_ready")
        part1_ready = sem("part1_ready")
        part2_ready = sem("part2_ready")
        xT_done = sem("xT_done")
        xT_hi_ready = sem("xT_hi_ready")
        xT_ready = sem("xT_ready")
        tile_done = sem("tile_done")
        relu_done = sem("relu_done")
        hi_ready = sem("hi_ready")
        lo_ready = sem("lo_ready")
        logT_done = sem("logT_done")
        logT_copied = sem("logT_copied")
        logit_done = sem("logit_done")
        route_chain = sem("route_chain")
        exp_ready = sem("exp_ready")
        exp_done = sem("exp_done")
        chosen_ready = sem("chosen_ready")
        place_ready = sem("place_ready")
        pos_done = sem("pos_done")
        onehot_ready = sem("onehot_ready")
        rows_done = sem("rows_done")
        rows_copied = sem("rows_copied")
        rows_stored = sem("rows_stored")
        passed_dve = sem("c_passed_dve")
        passed_pe = sem("c_passed_pe")
        small_in = sem("small_in")
        hi_done = sem("router_hi_done")
        w1_ready = sem("w1_ready")
        w2_ready = sem("w2_ready")
        w3_ready = sem("w3_ready")
        made = sem("router_consts")
        consts_ready = sem("router_consts_ready")
        block = ctx.enter_context(nc.Block())

        TILES = 2 * NT
        ROUTE_STEPS = 19
        PIECES = GB * CC

        def bank_of(piece):
            n = piece % 3 * SL
            return ps_x[piece // 3][:, n:n + SL]

        def w2_low(eng, k):
            eng.wait_ge(hi_done, k + 2)
            eng.tensor_tensor(w["w2_lo"][:, k], raw["w2"][:, k], w["w2_hi"][:, k].bitcast(F32), ALU.subtract)\
               .then_inc(w2_ready, 1)

        def groups(eng, turn, before, after):
            before()
            turn(0, route=False)
            turn(1)
            with eng.Fori(2, NG - 1) as g:
                turn(g)
            turn(NG - 1, prep=False)
            after()

        @block.sync
        def _(sp):
            def load(g):
                wait(sp, h2_ready, g)
                sp.dma_start(h1[:], h1_dram[:, bass.ds(g * GB, GB), :]).then_inc(h1_in, 16)
                sp.dma_start(y[:], y_dram[:, bass.ds(g * GB, GB), :]).then_inc(y_in, 16)

            def store_h2(g):
                wait(sp, h2_ready, g + 1)
                sp.dma_start(h2_dram[:, bass.ds(g * GB, GB), :], h2[:]).then_inc(h2_stored, 16)

            def store_rows(g):
                wait(sp, rows_copied, PIECES * (g + 1))
                sp.dma_start(rows_dram[:, :, bass.ds(g * GB * CAP, GB * CAP)],
                             rows[:].rearrange("p c e b s -> p (c e) (b s)")).then_inc(rows_stored, 16)

            load(0)
            sp.dma_start(raw3[:], A["L0_ffn_rW3"].rearrange("(k p) n -> p k n", p=P)).then_inc(small_in, 16)
            for name, dst in (("L0_ffn_rb1", w["rb1"]), ("L0_ffn_rb2", w["rb2"])):
                sp.dma_start(dst[:], A[name].rearrange("(k p) -> p k", p=P),
                             allow_slow_non_contiguous=True).then_inc(small_in, 16)
            sp.dma_start(w["rb3"][:], bass.AP(A["L0_ffn_rb3"].tensor, 0, [[0, P], [1, E]])).then_inc(small_in, 16)
            store_h2(0)
            load(1)
            store_h2(1)
            load(2)

            def turn(g):
                store_rows(g - 1)
                store_h2(g + 1)
                load(g + 2)

            turn(1)
            with sp.Fori(2, NG - 2) as g:
                turn(g)
            store_rows(NG - 3)
            store_h2(NG - 1)
            store_rows(NG - 2)
            store_rows(NG - 1)
            sp.wait_ge(h2_stored, 16 * NG)
            sp.wait_ge(rows_stored, 16 * NG)

        @block.gpsimd
        def _(pool):
            pool.memset(w["ident"][:], 0.0).then_inc(made, 1)
            pool.memset(w["earlier"][:], 1.0).then_inc(made, 1)
            pool.wait_ge(made, 1)
            pool.affine_select(out=w["ident"][:], in_=w["ident"][:], compare_op=ALU.not_equal, fill=1.0, base=0,
                               pattern=[[-1, P]], channel_multiplier=1).then_inc(consts_ready, 1)
            pool.wait_ge(made, 2)
            pool.affine_select(out=w["earlier"][:], in_=w["earlier"][:], compare_op=ALU.is_gt, fill=0.0, base=0,
                               pattern=[[1, T]], channel_multiplier=-1).then_inc(consts_ready, 1)
            pool.iota(w["rank"][:], pattern=[[0, GB], [-1, E]], base=E, channel_multiplier=0,
                      allow_small_or_imprecise_dtypes=True).then_inc(consts_ready, 1)
            pool.iota(w["slot_no"][:], pattern=[[0, GB * E], [1, CAP]], base=0, channel_multiplier=0,
                      allow_small_or_imprecise_dtypes=True).then_inc(consts_ready, 1)
            for k in range(3):
                w2_low(pool, k)

        @block.scalar
        def _(act):
            def norm(g):
                wait(act, norm_ready, g + 1)
                wait(act, rest_ready, g)
                wait(act, xT_done, g)
                for b in range(GB):
                    act.activation(x2[:, b], h2[:, b], ACT.Identity, bias=shift[:, b:b + 1], scale=rstd[:, b:b + 1])\
                       .then_inc(norm_done, 1)

            def copy_xT(g):
                wait(act, xT_done, g + 1)
                for c in range(CC):
                    act.copy(xT_hi[:, c], ps_x[c][:, 0:GT]).then_inc(xT_hi_ready, 1)

            def relus(g, layer, tiles):
                bias = w["rb1"] if layer == 0 else w["rb2"]
                for t in tiles:
                    n = g * TILES + layer * NT + t
                    act.wait_ge(tile_done, n + 1)
                    wait(act, lo_ready, n - RELU + 1)
                    act.activation(relu[:, t % RELU], ps_m[t % MM][:, 0:GT], ACT.Relu,
                                   bias=bias[:, t:t + 1]).then_inc(relu_done, 1)

            def copy_logT(g):
                wait(act, logT_done, g + 1)
                act.copy(logT[:], ps_l[0:2 * E, 0:GT]).then_inc(logT_copied, 1)

            def exps(g):
                wait(act, exp_ready, g + 1)
                act.activation(ex[:], logit[:], ACT.Exp).then_inc(exp_done, 1)

            def copy_rows(g):
                wait(act, rows_done, g + 1)
                wait(act, rows_stored, 16 * g)
                for n in range(PIECES):
                    act.copy(rows[:, n // GB, :, n % GB, :], bank_of(n).rearrange("p (e s) -> p e s", e=E))\
                       .then_inc(rows_copied, 1)

            def part0(g):
                wait(act, rows_done, g)
                wait(act, norm_done, GB * (g + 1))
                act.copy(x2_part[0][:], x2[:]).then_inc(part0_ready, 1)

            def part1(g):
                wait(act, rest_ready, g + 1)
                act.copy(x2_part[1][:], x2_rest[:]).then_inc(part1_ready, 1)

            def turn(g, route=True, prep=True):
                relus(g, 0, range(NT))
                if route:
                    copy_logT(g - 1)
                relus(g, 1, [0])
                if route:
                    exps(g - 1)
                relus(g, 1, [1, 2, 3])
                if route:
                    copy_rows(g - 1)
                part0(g)
                relus(g, 1, [4])
                if prep:
                    norm(g + 1)
                part1(g)
                relus(g, 1, [5])
                if prep:
                    copy_xT(g + 1)
                relus(g, 1, [6, 7])

            def before():
                act.copy(w["w1_hi"][:], raw["w1"][:]).then_inc(hi_done, 1)
                for k in range(HC):
                    act.copy(w["w2_hi"][:, k], raw["w2"][:, k]).then_inc(hi_done, 1)
                norm(0)
                copy_xT(0)
                act.wait_ge(small_in, 64)
                act.copy(w["w3"][:, :, 0:E], raw3[:]).then_inc(hi_done, 1)
                act.wait_ge(w1_ready, 1)

            def after():
                copy_logT(NG - 1)
                exps(NG - 1)
                copy_rows(NG - 1)

            groups(act, turn, before, after)

        @block.vector
        def _(dve):
            def stats_of(g):
                wait(dve, h1_in, 16 * (g + 1))
                wait(dve, y_in, 16 * (g + 1))
                wait(dve, h2_stored, 16 * g)
                wait(dve, norm_done, GB * g)
                dve.tensor_tensor(h2[:], h1[:], y[:], ALU.add).then_inc(h2_ready, 1)
                wait(dve, h2_ready, g + 1)
                for b in range(GB):
                    dve.bn_stats(stats[:, b, :], h2[:, b]).then_inc(stats_done, 1)
                wait_apart(dve, stats_done, GB * (g + 1), passed_dve)
                for b in range(GB):
                    dve.bn_aggr(mv[:, b, :], stats[:, b, :]).then_inc(aggr_done, 1)
                wait(dve, aggr_done, GB * (g + 1))
                ch = Chain(dve, prep_chain, g * RSTD_STEPS)
                rstd_steps(ch, dve, mv[:, :, 1], var[:], rstd[:], newton[:])
                dve.scalar_tensor_tensor(shift[:], mv[:, :, 0], -1.0, rstd[:], ALU.mult, ALU.mult)\
                   .then_inc(norm_ready, 1)

            def split_xT(g):
                wait(dve, xT_hi_ready, CC * (g + 1))
                for c in range(CC):
                    dve.tensor_tensor(xT_lo[:, c], ps_x[c][:, 0:GT], xT_hi[:, c].bitcast(F32), ALU.subtract)\
                       .then_inc(xT_ready, 1)

            def splits(g, layer, tiles):
                hi, lo = (a1_hi, a1_lo) if layer == 0 else (a2_hi, a2_lo)
                for t in tiles:
                    n = g * TILES + layer * NT + t
                    dve.wait_ge(relu_done, n + 1)
                    if layer == 1 and t == 0:
                        wait(dve, logT_done, g)
                    dve.tensor_copy(hi[:, t], relu[:, t % RELU]).then_inc(hi_ready, 1)
                    dve.wait_ge(hi_ready, n + 1)
                    dve.tensor_tensor(lo[:, t], relu[:, t % RELU], hi[:, t].bitcast(F32), ALU.subtract)\
                       .then_inc(lo_ready, 1)

            def rest_of_x2(g):
                wait(dve, part0_ready, g + 1)
                wait(dve, part2_ready, g)
                dve.tensor_tensor(x2_rest[:], x2[:], x2_part[0][:], ALU.subtract).then_inc(rest_ready, 1)

            def part2(g):
                wait(dve, part1_ready, g + 1)
                dve.tensor_tensor(x2_part[2][:], x2_rest[:], x2_part[1][:], ALU.subtract).then_inc(part2_ready, 1)

            def over_e(x):
                return x[:].rearrange("p (b o) -> p b o", o=1).to_broadcast((T, GB, E))

            def best(ch, scores, mask):
                ch.step(dve.tensor_reduce(m1[:], scores, AX, ALU.max))
                ch.step(dve.tensor_tensor(key[:], scores, over_e(m1), ALU.is_equal))
                ch.step(dve.tensor_tensor(key[:], key[:], w["rank"][0:T], ALU.mult))
                ch.step(dve.tensor_reduce(m2[:], key[:], AX, ALU.max))
                ch.step(dve.tensor_tensor(mask, key[:], over_e(m2), ALU.is_equal))

            def choose(g):
                ch = Chain(dve, route_chain, g * ROUTE_STEPS)
                wait(dve, logit_done, g + 1)
                bias = w["rb3"][0:T, :].rearrange("p (o e) -> p o e", o=1).to_broadcast((T, GB, E))
                ch.step(dve.tensor_tensor(logit[:], logit_ps[:, :, 0:E], bias, ALU.add))
                ch.step(dve.tensor_tensor(logit[:], logit_ps[:, :, E:2 * E], logit[:], ALU.add))
                ch.step(dve.tensor_reduce(m1[:], logit[:], AX, ALU.max))
                dve.tensor_tensor(logit[:], logit[:], over_e(m1), ALU.subtract).then_inc(exp_ready, 1)
                wait(dve, exp_done, g + 1)
                ch.step(dve.reduce_sum(m2[:], ex[:], AX))
                ch.step(dve.reciprocal(m1[:], m2[:]))
                ch.step(dve.tensor_tensor(prob[:], ex[:], over_e(m1), ALU.mult))
                best(ch, prob[:], first[:])
                ch.step(dve.scalar_tensor_tensor(rest[:], first[:], -2.0, prob[:], ALU.mult, ALU.add))
                best(ch, rest[:], chosen[:])
                ch.step(dve.tensor_tensor(chosen[:], chosen[:], first[:], ALU.add))
                dve.tensor_copy(chosen_bf[:], chosen[:].rearrange("p b e -> p (b e)")).then_inc(chosen_ready, 1)
                dve.tensor_tensor(gate[:, bass.ds(g * GB * E, GB * E)].rearrange("p (b e) -> p b e", b=GB),
                                  prob[:], chosen[:], ALU.mult)
                assert ch.n == ROUTE_STEPS - 1

            def slots(g):
                at = place[:, bass.ds(g * GB * E, GB * E)]
                wait(dve, pos_done, g + 1)
                dve.tensor_scalar(key[:], chosen[:], -1000.0, 1000.0, ALU.mult, ALU.add).then_inc(route_chain, 1)
                dve.wait_ge(route_chain, (g + 1) * ROUTE_STEPS)
                dve.tensor_tensor(at, pos_ps, key[:].rearrange("p b e -> p (b e)"), ALU.add)\
                   .then_inc(place_ready, 1)
                wait(dve, place_ready, g + 1)
                wait(dve, rows_done, g)
                dve.tensor_tensor(onehot[:], w["slot_no"][0:T],
                                  at.rearrange("p (n o) -> p n o", o=1).to_broadcast((T, GB * E, CAP)),
                                  ALU.is_equal).then_inc(onehot_ready, 1)

            def turn(g, route=True, prep=True):
                splits(g, 0, range(NT))
                splits(g, 1, [0])
                if route:
                    choose(g - 1)
                splits(g, 1, [1])
                if prep:
                    stats_of(g + 1)
                splits(g, 1, [2])
                if route:
                    slots(g - 1)
                splits(g, 1, [3])
                rest_of_x2(g)
                splits(g, 1, [4])
                part2(g)
                splits(g, 1, [5])
                if prep:
                    split_xT(g + 1)
                splits(g, 1, [6, 7])

            def before():
                dve.wait_ge(hi_done, 1)
                dve.tensor_tensor(w["w1_lo"][:], raw["w1"][:], w["w1_hi"][:].bitcast(F32), ALU.subtract)\
                   .then_inc(w1_ready, 1)
                stats_of(0)
                for k in range(3, 6):
                    w2_low(dve, k)
                split_xT(0)
                for k in range(6, HC):
                    w2_low(dve, k)
                dve.wait_ge(hi_done, HC + 2)
                dve.tensor_tensor(w["w3"][:, :, E:2 * E], raw3[:], w["w3"][:, :, 0:E].bitcast(F32), ALU.subtract)\
                   .then_inc(w3_ready, 1)
                dve.wait_ge(consts_ready, 4)

            def after():
                choose(NG - 1)
                slots(NG - 1)

            groups(dve, turn, before, after)

        @block.tensor
        def _(pe):
            def transpose_x2(g):
                wait(pe, norm_done, GB * (g + 1))
                wait(pe, rows_copied, PIECES * (g - 1))
                wait(pe, xT_ready, CC * g)
                for c in range(CC):
                    for b in range(GB):
                        last = pe.transpose(ps_x[c][:, b * T:(b + 1) * T], x2[:, b, c * P:(c + 1) * P],
                                            w["ident"][0:T, 0:T])
                last.then_inc(xT_done, 1)

            def layer(g, n_layer, tiles):
                w_hi, w_lo = (w["w1_hi"], w["w1_lo"]) if n_layer == 0 else (w["w2_hi"], w["w2_lo"])
                x_hi, x_lo = (xT_hi, xT_lo) if n_layer == 0 else (a1_hi, a1_lo)
                chunks = CC if n_layer == 0 else HC
                for t in tiles:
                    n = g * TILES + n_layer * NT + t
                    if n_layer == 0 and t == 0:
                        wait(pe, xT_ready, CC * (g + 1))
                    wait(pe, relu_done, n - MM + 1)
                    for k in range(chunks):
                        if n_layer == 1 and t == 0:
                            wait(pe, lo_ready, g * TILES + k + 1)
                        o = slice(t * P, (t + 1) * P)
                        last = matmul3(pe, ps_m[t % MM][:, 0:GT], w_hi[:, k, o], w_lo[:, k, o], x_hi[:, k], x_lo[:, k],
                                       k == 0, k == chunks - 1)
                    last.then_inc(tile_done, 1)

            def logits(g):
                wait(pe, lo_ready, (g + 1) * TILES)
                wait(pe, rows_copied, PIECES * g)
                for k in range(HC):
                    pe.matmul(ps_l[0:2 * E, 0:GT], w["w3"][:, k, :], a2_hi[:, k], start=(k == 0), stop=False)
                    last = pe.matmul(ps_l[0:E, 0:GT], w["w3"][:, k, 0:E], a2_lo[:, k], start=False, stop=(k == HC - 1))
                last.then_inc(logT_done, 1)

            def transpose_logits(g):
                wait(pe, logT_copied, g + 1)
                wait_apart(pe, onehot_ready, g, passed_pe)
                for b in range(GB):
                    last = pe.transpose(ps_r[0:T, b * 2 * E:(b + 1) * 2 * E], logT[:, b * T:(b + 1) * T],
                                        w["ident"][0:2 * E, 0:2 * E])
                last.then_inc(logit_done, 1)

            def positions(g):
                wait(pe, chosen_ready, g + 1)
                pe.matmul(pos_ps, w["earlier"][:], chosen_bf[:], start=True, stop=True).then_inc(pos_done, 1)

            def gather(g):
                wait(pe, onehot_ready, g + 1)
                wait(pe, part2_ready, g + 1)
                for n in range(PIECES):
                    c, b = n // GB, n % GB
                    hot = onehot[:, b * E:(b + 1) * E, :].rearrange("p e s -> p (e s)")
                    for part in range(3):
                        last = pe.matmul(bank_of(n), x2_part[part][:, b, c * P:(c + 1) * P], hot, start=(part == 0),
                                         stop=(part == 2))
                last.then_inc(rows_done, 1)

            def turn(g, route=True, prep=True):
                layer(g, 0, range(NT))
                if route:
                    logits(g - 1)
                else:
                    pe.wait_ge(w2_ready, HC)
                    pe.wait_ge(w3_ready, 1)
                    pe.wait_ge(consts_ready, 4)
                layer(g, 1, [0])
                if route:
                    transpose_logits(g - 1)
                layer(g, 1, [1, 2])
                if route:
                    positions(g - 1)
                layer(g, 1, [3])
                if route:
                    gather(g - 1)
                layer(g, 1, [4, 5])
                if prep:
                    transpose_x2(g + 1)
                layer(g, 1, [6, 7])

            def before():
                pe.wait_ge(consts_ready, 1)
                transpose_x2(0)
                pe.wait_ge(w1_ready, 1)

            def after():
                logits(NG - 1)
                transpose_logits(NG - 1)
                positions(NG - 1)
                gather(NG - 1)

            groups(pe, turn, before, after)


def phase_experts(nc, A, scratch, w):
    rows_dram, out_dram = scratch["rows"], scratch["slots"]
    SPT = 4
    TPE = -(-CAP // SPT)
    MM = 4
    RELU = 4
    N = SPT * B
    assert B == P and N == 512

    def slots_of(j):
        return min(SPT, CAP - j * SPT)

    with ExitStack() as ctx:
        def sb(name, shape, dt=F32):
            return ctx.enter_context(nc.sbuf_tensor(name, shape, dt))

        def sem(name):
            return ctx.enter_context(nc.semaphore(name))

        w1_raw = sb("w1_raw", [P, CC, HID])
        w2_raw = sb("w2_raw", [P, HC, C])
        w1_hi = [sb(f"d_w1_hi{n}", [P, CC, HID], F32R) for n in range(2)]
        w1_lo = [sb(f"d_w1_lo{n}", [P, CC, HID], F32R) for n in range(2)]
        w2_hi = [sb(f"d_w2_hi{n}", [P, HC, C], F32R) for n in range(2)]
        w2_lo = [sb(f"d_w2_lo{n}", [P, HC, C], F32R) for n in range(2)]
        rows = sb("d_rows", [P, CC, B * CAP])
        x_hi = [sb(f"d_x_hi{n}", [P, CC, N], F32R) for n in range(2)]
        x_lo = [sb(f"d_x_lo{n}", [P, CC, N], F32R) for n in range(2)]
        a_hi = [sb(f"d_a_hi{n}", [P, HC, N], F32R) for n in range(2)]
        a_lo = [sb(f"d_a_lo{n}", [P, HC, N], F32R) for n in range(2)]
        relu = sb("d_relu", [P, RELU, N])
        out = sb("d_out", [P, SPT, C])
        b1_rows = sb("b1_rows", [E * HC, P])
        b1 = sb("d_b1", [P, E * HC])
        b2 = sb("d_b2", [P, 2, C])
        ps_m = [ctx.enter_context(nc.psum_tensor(f"ps_d{n}", [P, 512], F32)) for n in range(MM)]
        ps_o = [ctx.enter_context(nc.psum_tensor(f"ps_o{n}", [P, 512], F32)) for n in range(SPT)]

        b1_in = sem("b1_in")
        b1_done = sem("b1_done")
        b1_ready = sem("b1_ready")
        w_in = sem("d_w_in")
        b2_in = [sem(f"b2_in{n}") for n in range(2)]
        rows_in = sem("d_rows_in")
        w_hi_done = sem("w_hi_done")
        w_ready = sem("d_w_ready")
        x_hi_done = sem("x_hi_done")
        x_ready = sem("d_x_ready")
        tile_done = sem("d_tile_done")
        relu_done = sem("d_relu_done")
        hi_ready = sem("d_hi_ready")
        lo_ready = sem("d_lo_ready")
        out_done = sem("d_out_done")
        out_ready = sem("d_out_ready")
        passed_act = sem("d_passed_act")
        passed_pool = sem("d_passed_pool")
        first_in = [sem(f"d_first_in{n}") for n in range(CC + 1)]
        first_hi = sem("d_first_hi")
        out_stored = [sem(f"d_out_stored{n}") for n in range(SPT)]
        block = ctx.enter_context(nc.Block())

        def in_turns(eng, turn):
            turn(0, first=True)
            with eng.Fori(1, E // 2 - 1) as i:
                turn(i)
            turn(E // 2 - 1, last=True)

        def first_tile(c):
            return rows[:, c].rearrange("p (b s) -> p s b", s=CAP)[:, 0:SPT, :]

        def before(e, j):
            return (e, j - 1) if j else (e - 1, TPE - 1)

        @block.sync
        def _(sp):
            def load_w(e):
                wait(sp, w_ready, 2 * e)
                sp.dma_start(w1_raw[:], A["L0_ffn_eW1"][bass.ds(e, 1)].rearrange("e (k p) n -> p (e k) n", p=P))\
                  .then_inc(w_in, 16)
                sp.dma_start(w2_raw[:], A["L0_ffn_eW2"][bass.ds(e, 1)].rearrange("e (k p) n -> p (e k) n", p=P))\
                  .then_inc(w_in, 16)

            def load_b2(e, q):
                sp.dma_start(b2[:, q], A["L0_ffn_eb2"][bass.ds(e, 1)].to_broadcast((P, C))).then_inc(b2_in[q], 16)

            def load_rows(e):
                wait(sp, x_ready, TPE * e)
                sp.dma_start(rows[:], rows_dram.rearrange("p (c e) n -> p c e n", c=CC)[:, :, bass.ds(e, 1), :]
                             .rearrange("p c o n -> p c (o n)")).then_inc(rows_in, 16)

            def store(e, j):
                for r in range(slots_of(j)):
                    wait(sp, out_ready, e * CAP + j * SPT + r + 1)
                    sp.dma_start(out_dram[bass.ds(e * CAP + j * SPT + r, 1)].rearrange("o b c -> b (o c)"), out[:, r])\
                      .then_inc(out_stored[r], 16)

            for c in range(CC):
                sp.dma_start(w1_raw[:, c], A["L0_ffn_eW1"][0, c * P:(c + 1) * P]).then_inc(first_in[c], 16)
            sp.dma_start(b1_rows[:], A["L0_ffn_eb1"].rearrange("e (k p) -> (e k) p", p=P)).then_inc(b1_in, 16)
            load_rows(0)
            sp.dma_start(w2_raw[:], A["L0_ffn_eW2"][0].rearrange("(k p) n -> p k n", p=P)).then_inc(first_in[CC], 16)

            def turn(i, first=False, last=False):
                for q in range(2):
                    e = 2 * i + q
                    for j in range(TPE):
                        if j == 0:
                            wait(sp, out_ready, (e - 1) * CAP)
                            load_b2(e, q)
                            if not (last and q == 1):
                                load_w(e + 1)
                        if not (first and q == 0 and j == 0):
                            store(*before(e, j))
                        if j == 3 and not (last and q == 1):
                            load_rows(e + 1)

            in_turns(sp, turn)
            store(E - 1, TPE - 1)
            for r in range(SPT):
                sp.wait_ge(out_stored[r], 16 * E * (TPE if r < slots_of(TPE - 1) else TPE - 1))

        @block.gpsimd
        def _(pool):
            def split_w(e, q):
                wait(pool, w_in, 32 * e)
                wait_apart(pool, out_done, (e - 1) * CAP, passed_pool)
                pool.tensor_copy(w1_hi[q][:], w1_raw[:]).then_inc(w_hi_done, 1)
                pool.tensor_copy(w2_hi[q][:], w2_raw[:]).then_inc(w_hi_done, 1)
                wait(pool, w_hi_done, 2 * e)
                pool.tensor_tensor(w1_lo[q][:], w1_raw[:], w1_hi[q][:].bitcast(F32), ALU.subtract).then_inc(w_ready, 1)
                pool.tensor_tensor(w2_lo[q][:], w2_raw[:], w2_hi[q][:].bitcast(F32), ALU.subtract).then_inc(w_ready, 1)

            def split_x(e, j, q):
                n = slots_of(j)
                if j == 0:
                    wait(pool, rows_in, 16 * (e + 1))
                elif isinstance(e, int) and e == 0 and j == 1:
                    pool.wait_ge(x_ready, 1)
                wait_apart(pool, tile_done, HC * (e * TPE + j - 1), passed_pool)
                s = (q * TPE + j) % 2
                for c in range(CC):
                    src = rows[:, c].rearrange("p (b s) -> p s b", s=CAP)[:, j * SPT:j * SPT + n, :]
                    hi = x_hi[s][:, c, 0:n * B].rearrange("p (s b) -> p s b", s=n)
                    pool.tensor_copy(hi, src).then_inc(x_hi_done, 1)
                wait(pool, x_hi_done, CC * (e * TPE + j))
                for c in range(CC):
                    src = rows[:, c].rearrange("p (b s) -> p s b", s=CAP)[:, j * SPT:j * SPT + n, :]
                    hi = x_hi[s][:, c, 0:n * B].rearrange("p (s b) -> p s b", s=n)
                    lo = x_lo[s][:, c, 0:n * B].rearrange("p (s b) -> p s b", s=n)
                    ins = pool.tensor_tensor(lo, src, hi.bitcast(F32), ALU.subtract)
                ins.then_inc(x_ready, 1)

            def turn(i, first=False, last=False):
                for q in range(2):
                    for j in range(TPE):
                        if not (first and q == 0 and j == 0):
                            split_x(2 * i + q, j, q)
                        if j == 2 and not (last and q == 1):
                            split_w(2 * i + q + 1, 1 - q)

            in_turns(pool, turn)

        @block.scalar
        def _(act):
            for c in range(CC):
                act.wait_ge(first_in[c], 16)
                act.copy(w1_hi[0][:, c], w1_raw[:, c]).then_inc(first_hi, 1)
            act.wait_ge(b1_done, 1)
            act.copy(b1[:], ps_m[0][:, 0:E * HC]).then_inc(b1_ready, 1)
            act.wait_ge(rows_in, 16)
            for c in range(CC):
                act.copy(x_hi[0][:, c].rearrange("p (s b) -> p s b", s=SPT), first_tile(c)).then_inc(first_hi, 1)
            act.wait_ge(first_in[CC], 16)
            act.copy(w2_hi[0][:], w2_raw[:]).then_inc(first_hi, 1)
            act.wait_ge(b1_ready, 1)

            def turn(i, first=False, last=False):
                for q in range(2):
                    for j in range(TPE):
                        e, n = 2 * i + q, slots_of(j) * B
                        for t in range(HC):
                            m = (e * TPE + j) * HC + t
                            act.wait_ge(tile_done, m + 1)
                            wait_apart(act, lo_ready, m - RELU + 1, passed_act)
                            act.activation(relu[:, t % RELU, 0:n], ps_m[t % MM][:, 0:n], ACT.Relu,
                                           bias=b1[:, bass.ds(e * HC + t, 1)]).then_inc(relu_done, 1)

            in_turns(act, turn)

        @block.vector
        def _(dve):
            def splits(e, j, q):
                n, s = slots_of(j) * B, (q * TPE + j) % 2
                for t in range(HC):
                    m = (e * TPE + j) * HC + t
                    dve.wait_ge(relu_done, m + 1)
                    dve.tensor_copy(a_hi[s][:, t, 0:n], relu[:, t % RELU, 0:n]).then_inc(hi_ready, 1)
                    dve.wait_ge(hi_ready, m + 1)
                    dve.tensor_tensor(a_lo[s][:, t, 0:n], relu[:, t % RELU, 0:n], a_hi[s][:, t, 0:n].bitcast(F32),
                                      ALU.subtract).then_inc(lo_ready, 1)

            def add_bias(e, j, q):
                if j == 0:
                    wait(dve, b2_in[q], 16 * (e // 2 + 1) if isinstance(e, int) else 8 * (e - q) + 16)
                for r in range(slots_of(j)):
                    wait(dve, out_done, e * CAP + j * SPT + r + 1)
                    wait(dve, out_stored[r], 16 * (e * (TPE if r < slots_of(TPE - 1) else TPE - 1) + j))
                    dve.tensor_tensor(out[:, r], ps_o[r][:, 0:C], b2[:, q], ALU.add).then_inc(out_ready, 1)

            def turn(i, first=False, last=False):
                for q in range(2):
                    for j in range(TPE):
                        e = 2 * i + q
                        splits(e, j, q)
                        if not (first and q == 0 and j == 0):
                            add_bias(*before(e, j), q if j else 1 - q)

            for c in range(CC):
                dve.wait_ge(first_hi, c + 1)
                ins = dve.tensor_tensor(w1_lo[0][:, c], w1_raw[:, c], w1_hi[0][:, c].bitcast(F32), ALU.subtract)
            ins.then_inc(w_ready, 1)
            for c in range(CC):
                dve.wait_ge(first_hi, CC + c + 1)
                ins = dve.tensor_tensor(x_lo[0][:, c].rearrange("p (s b) -> p s b", s=SPT), first_tile(c),
                                        x_hi[0][:, c].rearrange("p (s b) -> p s b", s=SPT).bitcast(F32), ALU.subtract)
            ins.then_inc(x_ready, 1)
            dve.wait_ge(first_hi, 2 * CC + 1)
            dve.tensor_tensor(w2_lo[0][:], w2_raw[:], w2_hi[0][:].bitcast(F32), ALU.subtract).then_inc(w_ready, 1)
            in_turns(dve, turn)
            add_bias(E - 1, TPE - 1, 1)

        @block.tensor
        def _(pe):
            pe.wait_ge(b1_in, 16)
            pe.transpose(ps_m[0][:, 0:E * HC], b1_rows[:], w["ident"][0:E * HC, 0:E * HC]).then_inc(b1_done, 1)
            pe.wait_ge(b1_ready, 1)

            def layer1(e, j, q):
                n, s = slots_of(j) * B, (q * TPE + j) % 2
                wait(pe, x_ready, e * TPE + j + 1)
                if j == 0:
                    wait(pe, w_ready, 1 if isinstance(e, int) and e == 0 else 2 * (e + 1))
                for t in range(HC):
                    m = (e * TPE + j) * HC + t
                    wait(pe, relu_done, m - MM + 1)
                    for k in range(CC):
                        o = slice(t * P, (t + 1) * P)
                        last = matmul3(pe, ps_m[t % MM][:, 0:n], w1_hi[q][:, k, o], w1_lo[q][:, k, o],
                                       x_hi[s][:, k, 0:n], x_lo[s][:, k, 0:n], k == 0, k == CC - 1)
                    last.then_inc(tile_done, 1)

            def layer2(e, j, q):
                s = (q * TPE + j) % 2
                wait(pe, lo_ready, (e * TPE + j + 1) * HC)
                if isinstance(e, int) and e == 0 and j == 0:
                    pe.wait_ge(w_ready, 2)
                for r in range(slots_of(j)):
                    here = e * CAP + j * SPT + r
                    past = here - SPT if j or r >= slots_of(TPE - 1) else here - slots_of(TPE - 1)
                    if j == 0 and r >= slots_of(TPE - 1):
                        past = here - slots_of(TPE - 1) - SPT
                    wait(pe, out_ready, past + 1)
                    rows_at = slice(r * B, (r + 1) * B)
                    for k in range(HC):
                        last = matmul3(pe, ps_o[r][:, 0:C], a_hi[s][:, k, rows_at], a_lo[s][:, k, rows_at],
                                       w2_hi[q][:, k], w2_lo[q][:, k], k == 0, k == HC - 1)
                    last.then_inc(out_done, 1)

            def turn(i, first=False, last=False):
                for q in range(2):
                    for j in range(TPE):
                        e = 2 * i + q
                        layer1(e, j, q)
                        if not (first and q == 0 and j == 0):
                            layer2(*before(e, j), q if j else 1 - q)

            in_turns(pe, turn)
            layer2(E - 1, TPE - 1, 1)


def phase_combine(nc, scratch, w, place, gate, result):
    h2_dram, slots_dram = scratch["h2"], scratch["slots"]
    STEP_E = 4
    TURNS_E = NG // STEP_E
    with ExitStack() as ctx:
        def sb(name, shape, dt=F32):
            return ctx.enter_context(nc.sbuf_tensor(name, shape, dt))

        def sem(name):
            return ctx.enter_context(nc.semaphore(name))

        hot = sb("e_hot", [T, STEP_E, GB * E, CAP])
        mix = sb("e_mix", [T, STEP_E, GB * E, CAP])
        mixT = sb("e_mixT", [HSL, STEP_E, 2, GT])
        slots = sb("e_slots", [HSL, STEP_E, 2, GB * C])
        h2 = sb("e_h2", [T, STEP_E, GB, C])
        out = sb("e_out", [T, STEP_E, GB, C])
        ps_t = [[ctx.enter_context(nc.psum_tensor(f"ps_t{n}{h}", [P, 512], F32)) for h in range(2)] for n in range(2)]
        ps_c = [[ctx.enter_context(nc.psum_tensor(f"ps_c{n}{h}", [P, 512], F32)) for h in range(2)] for n in range(2)]
        slots_in = [sem(f"slots_in{n}") for n in range(STEP_E)]
        h2_in = [sem(f"e_h2_in{n}") for n in range(STEP_E)]
        out_stored = [sem(f"e_out_stored{n}") for n in range(STEP_E)]
        hot_done = sem("hot_done")
        mix_ready = sem("mix_ready")
        mixT_done = sem("mixT_done")
        mixT_ready = sem("mixT_ready")
        sum_done = sem("sum_done")
        out_ready = sem("e_out_ready")
        block = ctx.enter_context(nc.Block())

        def in_turns(eng, turn):
            turn(0, mixing=False)
            turn(1)
            with eng.Fori(2, TURNS_E) as i:
                turn(i)
            turn(TURNS_E, mix=False)

        @block.sync
        def _(sp):
            def load(g, k):
                for h in range(2):
                    rows = slots_dram[h * HSL:(h + 1) * HSL, bass.ds(g * GB, GB), :].rearrange("s b c -> s (b c)")
                    sp.dma_start(slots[:, k, h], rows).then_inc(slots_in[k], 16)
                sp.dma_start(h2[:, k], h2_dram[:, bass.ds(g * GB, GB), :]).then_inc(h2_in[k], 16)

            for k in range(STEP_E):
                load(k, k)

            def turn(i, load_next=True):
                for k in range(STEP_E):
                    g = i * STEP_E + k
                    wait(sp, out_ready, 2 * (g + 1))
                    sp.dma_start(result[bass.ds(g * GB, GB)].rearrange("b t c -> t b c"), out[:, k])\
                      .then_inc(out_stored[k], 16)
                    if load_next:
                        load(g + STEP_E, k)

            with sp.Fori(0, TURNS_E - 1) as i:
                turn(i)
            turn(TURNS_E - 1, load_next=False)
            for k in range(STEP_E):
                sp.wait_ge(out_stored[k], 16 * TURNS_E)

        @block.gpsimd
        def _(pool):
            def turn(i):
                for k in range(STEP_E):
                    g = i * STEP_E + k
                    span = bass.ds(g * GB * E, GB * E)
                    wait(pool, mixT_done, g - STEP_E + 1)
                    over = (T, GB * E, CAP)
                    wait(pool, hot_done, g + 1)
                    pool.tensor_tensor(mix[:, k], hot[:, k],
                                       gate[:, span].rearrange("p (n o) -> p n o", o=1).to_broadcast(over),
                                       ALU.mult).then_inc(mix_ready, 1)

            turn(0)
            with pool.Fori(1, TURNS_E) as i:
                turn(i)

        @block.tensor
        def _(pe):
            def turn(i, mix=True, mixing=True):
                for k in range(STEP_E):
                    if mix:
                        g = i * STEP_E + k
                        wait(pe, mix_ready, g + 1)
                        wait(pe, mixT_ready, 2 * (g - 1))
                        for h in range(2):
                            for b in range(GB):
                                at = mix_at(k, b, h)
                                last = pe.transpose(ps_t[k % 2][h][0:HSL, b * T:(b + 1) * T], at, w["ident"][0:T, 0:T])
                        last.then_inc(mixT_done, 1)
                    if mixing:
                        g = (i - 1) * STEP_E + k
                        wait(pe, mixT_ready, 2 * (g + 1))
                        wait(pe, slots_in[k], 32 * i)
                        wait(pe, out_ready, 2 * (g - 1))
                        for b in range(GB):
                            for h in range(2):
                                last = pe.matmul(ps_c[k % 2][b // 2][0:T, b % 2 * C:(b % 2 + 1) * C],
                                                 mixT[:, k, h, b * T:(b + 1) * T], slots[:, k, h, b * C:(b + 1) * C],
                                                 start=(h == 0), stop=(h == 1))
                        last.then_inc(sum_done, 1)

            def mix_at(k, b, h):
                return mix[:, k, b * E + h * E // 2:b * E + (h + 1) * E // 2, :].rearrange("p e s -> p (e s)")

            in_turns(pe, turn)

        @block.scalar
        def _(act):
            def turn(i):
                for k in range(STEP_E):
                    g = i * STEP_E + k
                    wait(act, mixT_done, g + 1)
                    wait(act, sum_done, g - STEP_E + 1)
                    for h in range(2):
                        act.copy(mixT[:, k, h], ps_t[k % 2][h][0:HSL, 0:GT]).then_inc(mixT_ready, 1)

            turn(0)
            with act.Fori(1, TURNS_E) as i:
                turn(i)

        @block.vector
        def _(dve):
            def hot_of(g, k):
                wait(dve, mix_ready, g - STEP_E + 1)
                at = place[:, bass.ds(g * GB * E, GB * E)].rearrange("p (n o) -> p n o", o=1)
                dve.tensor_tensor(hot[:, k], w["slot_no"][0:T], at.to_broadcast((T, GB * E, CAP)),
                                  ALU.is_equal).then_inc(hot_done, 1)

            def turn(i, mix=True, mixing=True, ahead=True):
                for k in range(STEP_E):
                    if mix and (ahead or k + 2 < STEP_E):
                        hot_of(i * STEP_E + k + 2, (k + 2) % STEP_E)
                    if mixing:
                        g = (i - 1) * STEP_E + k
                        dve.wait_ge(sum_done, g + 1)
                        wait(dve, h2_in[k], 16 * i)
                        wait(dve, out_stored[k], 16 * (i - 1))
                        for n in range(2):
                            dve.tensor_tensor(out[:, k, 2 * n:2 * n + 2],
                                              ps_c[k % 2][n][0:T, :].rearrange("p (b c) -> p b c", b=2),
                                              h2[:, k, 2 * n:2 * n + 2], ALU.add).then_inc(out_ready, 1)

            hot_of(0, 0)
            hot_of(1, 1)
            turn(0, mixing=False)
            turn(1)
            with dve.Fori(2, TURNS_E - 1) as i:
                turn(i)
            turn(TURNS_E - 1, ahead=False)
            turn(TURNS_E, mix=False)


def build(nc, A, result):
    scratch = {
        "taps": nc.dram_tensor("taps_scratch", (1, LPAD), F32).ap(),
        "kern": nc.dram_tensor("kern_scratch", (C, LPAD), F32).ap(),
        "h1": nc.dram_tensor("h1_scratch", (T, B, C), F32).ap(),
        "y": nc.dram_tensor("y_scratch", (T, B, C), F32).ap(),
        "h2": nc.dram_tensor("h2_scratch", (T, B, C), F32).ap(),
        "rows": nc.dram_tensor("rows_scratch", (P, CC * E, B * CAP), F32).ap(),
        "slots": nc.dram_tensor("slots_scratch", (SL, B, C), F32).ap(),
    }
    with ExitStack() as ctx:
        def sb(name, shape, dt=F32):
            return ctx.enter_context(nc.sbuf_tensor(name, shape, dt))

        with nc.sbuf_tensor("xn", [T, B, C], F32) as xn:
            phase_tokens(nc, A, scratch, xn)
            raw_space = ExitStack()
            raw = {n: raw_space.enter_context(nc.sbuf_tensor(f"raw_{n}", shape, F32, side="right"))
                   for n, shape in (("w1", [P, CC, HID]), ("w2", [P, HC, HID]))}
            phase_states(nc, A, scratch, xn, raw)
        raw_space.close()
        place = sb("place", [T, B * E])
        gate = sb("gate", [T, B * E])
        w = {"ident": sb("ident", [P, P]), "earlier": sb("earlier", [T, T], BF16),
             "slot_no": sb("slot_no", [P, GB * E, CAP]), "rank": sb("rank", [P, GB, E])}
        with ExitStack() as router:
            def rsb(name, shape, dt=F32R):
                return router.enter_context(nc.sbuf_tensor(name, shape, dt))

            w |= {"w1_hi": rsb("w1_hi", [P, CC, HID]), "w1_lo": rsb("w1_lo", [P, CC, HID]),
                  "w2_hi": rsb("w2_hi", [P, HC, HID]), "w2_lo": rsb("w2_lo", [P, HC, HID]),
                  "w3": rsb("w3", [P, HC, 2 * E]),
                  "rb1": rsb("rb1", [P, HC], F32), "rb2": rsb("rb2", [P, HC], F32), "rb3": rsb("rb3", [P, E], F32)}
            phase_router(nc, A, scratch, w, raw, place, gate)
        phase_experts(nc, A, scratch, w)
        phase_combine(nc, scratch, w, place, gate, result)


_INS = ["x", "L0_tok_Wv", "L0_tok_bv", "L0_tok_Wo", "L0_tok_bo", "L0_tok_decay_w", "L0_attn_log_dt",
        "L0_attn_log_A_real", "L0_attn_A_imag", "L0_attn_C", "L0_attn_D", "L0_ffn_rW1", "L0_ffn_rb1", "L0_ffn_rW2",
        "L0_ffn_rb2", "L0_ffn_rW3", "L0_ffn_rb3", "L0_ffn_eW1", "L0_ffn_eb1", "L0_ffn_eW2", "L0_ffn_eb2"]


def kernel(**inputs):
    import numpy as _np
    import concourse.bacc as _bacc
    from concourse.bass_utils import run_bass_kernel_spmd as _run

    nc = _bacc.Bacc("TRN2", target_bir_lowering=False, num_devices=1)
    arrays, args = {}, {}
    for name in _INS:
        a = _np.ascontiguousarray(inputs[name])
        arrays[f"in_{name}"] = a
        args[name] = nc.dram_tensor(f"in_{name}", a.shape, mybir.dt.from_np(a.dtype), kind="ExternalInput").ap()
    result = nc.dram_tensor("result", (B, T, C), F32, kind="ExternalOutput").ap()
    build(nc, args, result)
    r = _run(nc, [arrays], core_ids=[0])
    return r.results[0]["result"]
```

```python
from contextlib import ExitStack

import concourse.bass as bass
from concourse import mybir

F32 = mybir.dt.float32
F32R = mybir.dt.float32r
BF16 = mybir.dt.bfloat16
I32 = mybir.dt.int32
ALU = mybir.AluOpType
ACT = mybir.ActivationFunctionType
AX = mybir.AxisListType.X

P = 128
B, TIN, C = 128, 125, 256
T = TIN + 1
TAPS = 32
NM = 32
CC = C // P
HID = 1024
HC = HID // P
E = 8
CAP = int(T / E * 1.25)
SL = E * CAP
HSL = SL // 2
EPS = 1e-5

GB = 4
NG = B // GB
GT = GB * T
PAIRS = B // 2
STEP = 4
TURNS = PAIRS // STEP
LPAD = 256

HANKEL = 64
HANKEL_SLOTS = 8

LOG2E = 1.4426950408889634
LN2_HI = 0.693145751953125
LN2_LO = 1.4286068203094172e-06
ROUND = 12582912.0
TWO_PI = 6.283185307179586
PI2_A = 6.28125
PI2_B = 0.0019350051879882812
PI2_C = 3.019915981956753e-07
PI_BELOW = 3.1415925


def wait(eng, sem, value):
    if isinstance(value, int) and value <= 0:
        return
    eng.wait_ge(sem, value)


def wait_apart(eng, sem, value, passed):
    wait(eng, sem, value)
    if not isinstance(value, int):
        eng.sem_inc(passed, 1)


class Chain:

    def __init__(self, eng, sem, base=0):
        self.eng, self.sem, self.base, self.n = eng, sem, base, 0

    def step(self, ins):
        ins.then_inc(self.sem, 1)
        self.n += 1
        self.eng.wait_ge(self.sem, self.base + self.n)


def split(chain, eng, hi, lo, src):
    chain.step(eng.tensor_copy(hi, src))
    chain.step(eng.tensor_tensor(lo, src, hi.bitcast(F32), ALU.subtract))


def matmul3(pe, out, w_hi, w_lo, x_hi, x_lo, start, stop):
    pe.matmul(out, w_hi, x_hi, start=start, stop=False)
    pe.matmul(out, w_hi, x_lo, start=False, stop=False)
    return pe.matmul(out, w_lo, x_hi, start=False, stop=stop)


def exp_steps(ch, dve, x, t, k, r, p, scale_bits):
    ch.step(dve.tensor_scalar(t, x, LOG2E, ROUND, ALU.mult, ALU.add))
    ch.step(dve.tensor_scalar(k, t, -ROUND, None, ALU.add))
    ch.step(dve.tensor_scalar(k, k, 127.0, -126.0, ALU.min, ALU.max))
    ch.step(dve.scalar_tensor_tensor(r, k, -LN2_HI, x, ALU.mult, ALU.add))
    ch.step(dve.scalar_tensor_tensor(r, k, -LN2_LO, r, ALU.mult, ALU.add))
    ch.step(dve.tensor_scalar(p, r, 1.0 / 5040.0, None, ALU.mult))
    for fact in (720.0, 120.0, 24.0, 6.0, 2.0, 1.0):
        ch.step(dve.scalar_tensor_tensor(p, p, 1.0 / fact, r, ALU.add, ALU.mult))
    ch.step(dve.tensor_scalar(scale_bits, k, 127.0, 8388608.0, ALU.add, ALU.mult))
    ch.step(dve.scalar_tensor_tensor(p, p, 1.0, scale_bits.bitcast(F32), ALU.add, ALU.mult))


def rstd_steps(ch, dve, var_in, var, y, t):
    ch.step(dve.tensor_scalar(var, var_in, EPS, None, ALU.add))
    ch.step(dve.tensor_scalar(y.bitcast(I32), var.bitcast(I32), -0.5, 1597463007.0, ALU.mult, ALU.add))
    for _ in range(3):
        ch.step(dve.tensor_tensor(t, y, y, ALU.mult))
        ch.step(dve.scalar_tensor_tensor(t, t, -0.5, var, ALU.mult, ALU.mult))
        ch.step(dve.scalar_tensor_tensor(y, t, 1.5, y, ALU.add, ALU.mult))


RSTD_STEPS = 2 + 3 * 3


def load_hankel(eng, scratch, hankel, i, s):
    n = HANKEL // HANKEL_SLOTS
    rows = bass.AP(scratch["kern"].tensor, (i * HANKEL + s * n) * LPAD, [[1, T], [LPAD, n], [1, P]])
    eng.dma_start(hankel["rows"][:, s * n:(s + 1) * n, :], rows).then_inc(hankel["loaded"][s], 16)


def phase_tokens(nc, A, scratch, xn, hankel):
    h1_dram, kern_dram, taps_dram = scratch["h1"], scratch["kern"], scratch["taps"]
    with ExitStack() as ctx:
        def sb(name, shape, dt=F32):
            return ctx.enter_context(nc.sbuf_tensor(name, shape, dt))

        def sem(name):
            return ctx.enter_context(nc.semaphore(name))

        ident = sb("a_ident", [P, P])
        ones = sb("a_ones", [P, P])
        tap_row = sb("tap_row", [1, LPAD])
        tap_all = sb("tap_all", [P, TAPS])
        tap_sum = sb("tap_sum", [P, 1])
        conv_rev = sb("conv_rev", [TIN, T])
        conv = sb("conv", [TIN, T])
        wv = sb("wv", [P, CC, C])
        wo = sb("wo", [P, CC, C])
        woT = sb("woT", [P, CC, C])
        bv = sb("bv", [P, CC])
        bv_sum = sb("bv_sum", [P, CC])
        bv_rows = sb("bv_rows", [P, CC, T])
        bo_row = sb("bo_row", [1, C])
        PART = 32
        sel_f32 = sb("sel_f32", [2 * PART, T])
        sel = sb("sel", [2 * PART, T], F32R)
        bias = sb("bias", [2 * PART, 2, C], F32R)
        w_hi = sb("w_hi", [P, CC, C], F32R)
        w_lo = sb("w_lo", [P, CC, C], F32R)

        x_in = sb("x_in", [TIN, STEP, 2, C])
        s_hi = sb("s_hi", [P, STEP, 2 * CC * T], F32R)
        s_lo = sb("s_lo", [P, STEP, 2 * CC * T], F32R)
        h1 = xn
        stats = sb("stats", [T, 2 * STEP, 6])
        mv = sb("mv", [T, 2 * STEP, 2])
        var = sb("var", [T, 2 * STEP])
        rstd = sb("rstd", [T, 2 * STEP])
        newton = sb("newton", [T, 2 * STEP])
        shift = sb("shift", [T, 2 * STEP])

        far_space = ExitStack()

        def far(name, shape, dt=F32):
            return far_space.enter_context(nc.sbuf_tensor(name, shape, dt, side="right"))

        logs = far("logs", [P, 2 + CC * NM])
        exps = far("exps", [P, 2 + CC * NM])
        a_im = far("a_im", [P, CC, NM])
        c_in = far("c_in", [P, CC, NM, 2])
        d_skip = far("d_skip", [P, CC])
        s0 = far("s0", [P, 2 + CC * NM])
        s1 = far("s1", [P, 2 + CC * NM])
        s2 = far("s2", [P, 2 + CC * NM])
        s3 = far("s3", [P, 2 + CC * NM], I32)
        g = {n: far("g_" + n, [P, CC, NM]) for n in
             ("are", "xr", "yi", "mag", "sin", "cos", "zr", "zi", "den", "ir", "ii", "cr", "ci", "t", "u")}
        NA, NB = 8, 16
        vr = far("vr", [P, CC, NB, NM])
        vi = far("vi", [P, CC, NB, NM])
        ur = far("ur", [P, CC, NA, NM])
        ui = far("ui", [P, CC, NA, NM])
        pr = [far(f"pr{n}", [P, CC, NM]) for n in range(2)]
        pi = [far(f"pi{n}", [P, CC, NM]) for n in range(2)]
        q0 = far("q0", [P, CC, NB // 2, NM])
        AH = NA // 4
        prod = far("prod", [P, AH, NB, NM])
        prod2 = far("prod2", [P, AH, NB, NM])
        kern = wo

        far_space.close()
        hankel["rows"] = hankel["space"].enter_context(nc.sbuf_tensor("rows_in", [T, HANKEL, P], F32, side="right"))

        ps_s = [ctx.enter_context(nc.psum_tensor(f"ps_s{n}", [P, 512], F32)) for n in range(STEP)]
        ps_h = [ctx.enter_context(nc.psum_tensor(f"ps_h{n}", [P, 512], F32)) for n in range(STEP)]
        ps_w, ps_b = ps_h[0:CC], ps_h[CC]

        consts_made = sem("consts_made")
        taps_in = sem("taps_in")
        taps_out = sem("taps_out")
        conv_in = sem("conv_in")
        weights_in = sem("weights_in")
        modes_in = sem("modes_in")
        woT_done = sem("woT_done")
        woT_copied = sem("woT_copied")
        w_done = sem("w_done")
        setup = sem("a_setup")
        setup_pool = sem("a_setup_pool")
        weights_ready = sem("weights_ready")
        angles_ready = sem("angles_ready")
        sines_ready = sem("sines_ready")
        modes_ready = sem("modes_ready")
        kern_out = sem("kern_out")
        x_loaded = [sem(f"x_loaded{k}") for k in range(STEP)]
        h1_stored = [sem(f"h1_stored{k}") for k in range(STEP)]
        conv_done = sem("conv_done")
        s_hi_ready = sem("s_hi_ready")
        s_lo_ready = sem("s_lo_ready")
        proj_done = sem("proj_done")
        h1_ready = sem("h1_ready")
        stats_done = sem("stats_done")
        aggr_done = sem("aggr_done")
        rstd_chain = sem("rstd_chain")
        norm_ready = sem("norm_ready")
        norm_done = sem("norm_done")
        sel_made = sem("sel_made")
        passed_act = sem("a_passed_act")
        passed_dve = sem("a_passed_dve")

        def load_x(sp, u, k):
            for t in (slice(0, 112), slice(112, TIN)):
                sp.dma_start(x_in[t, k], A["x"][bass.ds(2 * u, 2), t].rearrange("b t c -> t b c"))\
                  .then_inc(x_loaded[k], 16)

        block = ctx.enter_context(nc.Block())

        @block.sync
        def _(sp):
            sp.dma_start(wo[:], A["L0_tok_Wo"].rearrange("(k p) n -> p k n", p=P)).then_inc(weights_in, 16)
            sp.dma_start(wv[:], A["L0_tok_Wv"].rearrange("(k p) n -> p k n", p=P)).then_inc(weights_in, 16)
            sp.dma_start(bo_row[:], A["L0_tok_bo"].rearrange("(a n) -> a n", a=1)).then_inc(weights_in, 16)
            sp.dma_start(tap_all[:], bass.AP(A["L0_tok_decay_w"].tensor, 0, [[0, P], [1, TAPS]]))\
              .then_inc(weights_in, 16)
            for k in range(STEP):
                load_x(sp, k, k)

            def turn(i, load=True, store=True):
                if load:
                    for k in range(STEP):
                        wait(sp, conv_done, i * STEP + k + 1)
                        load_x(sp, (i + 1) * STEP + k, k)
                if store:
                    for k in range(STEP):
                        v = (i - 1) * STEP + k
                        wait(sp, h1_ready, v + 1)
                        sp.dma_start(h1_dram[:, bass.ds(2 * v, 2), :], h1[:, bass.ds(2 * v, 2), :])\
                          .then_inc(h1_stored[k], 16)

            turn(0, store=False)
            with sp.Fori(1, TURNS - 1) as i:
                turn(i)
            turn(TURNS - 1, load=False)
            sp.wait_ge(kern_out, 16)
            for s in range(2):
                load_hankel(sp, scratch, hankel, 0, s)
            turn(TURNS, load=False)
            for s in range(2, HANKEL_SLOTS):
                load_hankel(sp, scratch, hankel, 0, s)
            for k in range(STEP):
                sp.wait_ge(h1_stored[k], 16 * TURNS)

        @block.gpsimd
        def _(pool):
            pool.memset(tap_row[:], 0.0).then_inc(consts_made, 1)
            pool.memset(ident[:], 0.0).then_inc(setup_pool, 1)
            pool.memset(ones[:], 1.0).then_inc(consts_made, 1)
            pool.memset(sel_f32[:], 0.0).then_inc(sel_made, 1)
            pool.wait_ge(setup_pool, 1)
            pool.affine_select(out=ident[:], in_=ident[:], compare_op=ALU.not_equal, fill=1.0, base=0,
                               pattern=[[-1, P]], channel_multiplier=1).then_inc(consts_made, 1)
            pool.wait_ge(consts_made, 3)
            for n in range(2):
                pool.wait_ge(sel_made, n + 1)
                pool.memset(sel_f32[PART * n:PART * n + 1, :], 1.0).then_inc(sel_made, 1)
            pool.wait_ge(sel_made, 3)
            pool.wait_ge(woT_done, 1)
            pool.memset(kern[:], 0.0).then_inc(setup_pool, 1)
            ch = Chain(pool, setup_pool, 2)
            pool.wait_ge(setup_pool, 2)
            pool.wait_ge(modes_ready, 1)

            def cmul(outr, outi, xr, xi, yr, yi, tmp):
                ch.step(pool.tensor_tensor(outr, xr, yr, ALU.mult))
                ch.step(pool.tensor_tensor(tmp, xi, yi, ALU.mult))
                ch.step(pool.tensor_tensor(outr, outr, tmp, ALU.subtract))
                ch.step(pool.tensor_tensor(outi, xr, yi, ALU.mult))
                ch.step(pool.tensor_tensor(tmp, xi, yr, ALU.mult))
                ch.step(pool.tensor_tensor(outi, outi, tmp, ALU.add))

            def wide(x, m):
                return x[:].rearrange("p g (o n) -> p g o n", o=1).to_broadcast((P, CC, m, NM))

            ch.step(pool.memset(vr[:, :, NB - 1, :], 1.0))
            ch.step(pool.memset(vi[:, :, NB - 1, :], 0.0))
            zr, zi = g["zr"], g["zi"]
            m, at = 1, 0
            while m < NB:
                lo, mid = NB - 2 * m, NB - m
                if m == 1:
                    ch.step(pool.tensor_copy(vr[:, :, lo, :], zr[:]))
                    ch.step(pool.tensor_copy(vi[:, :, lo, :], zi[:]))
                else:
                    cmul(vr[:, :, lo:mid, :], vi[:, :, lo:mid, :], vr[:, :, mid:NB, :], vi[:, :, mid:NB, :],
                         wide(zr, m), wide(zi, m), q0[:, :, 0:m, :])
                cmul(pr[at][:], pi[at][:], zr[:], zi[:], zr[:], zi[:], q0[:, :, 0, :])
                zr, zi, at, m = pr[at], pi[at], 1 - at, 2 * m
            ch.step(pool.tensor_copy(ur[:, :, NA - 1, :], g["cr"][:]))
            ch.step(pool.tensor_copy(ui[:, :, NA - 1, :], g["ci"][:]))
            m = 1
            while m < NA:
                lo, mid = NA - 2 * m, NA - m
                cmul(ur[:, :, lo:mid, :], ui[:, :, lo:mid, :], ur[:, :, mid:NA, :], ui[:, :, mid:NA, :],
                     wide(zr, m), wide(zi, m), q0[:, :, 0:m, :])
                if 2 * m < NA:
                    cmul(pr[at][:], pi[at][:], zr[:], zi[:], zr[:], zi[:], q0[:, :, 0, :])
                    zr, zi, at = pr[at], pi[at], 1 - at
                m *= 2
            for c in range(CC):
                for a in range(0, NA, AH):
                    def u_of(x):
                        return x[:, c, a:a + AH, :].rearrange("p a (o n) -> p a o n", o=1)\
                                                   .to_broadcast((P, AH, NB, NM))

                    def v_of(x):
                        return x[:, c, :, :].rearrange("p (o b) n -> p o b n", o=1).to_broadcast((P, AH, NB, NM))

                    ch.step(pool.tensor_tensor(prod[:], u_of(ur), v_of(vr), ALU.mult))
                    ch.step(pool.tensor_tensor(prod2[:], u_of(ui), v_of(vi), ALU.mult))
                    ch.step(pool.tensor_tensor(prod[:], prod[:], prod2[:], ALU.subtract))
                    n = NM // 2
                    while n > 1:
                        ch.step(pool.tensor_tensor(prod[:, :, :, 0:n], prod[:, :, :, 0:n], prod[:, :, :, n:2 * n],
                                                   ALU.add))
                        n //= 2
                    ch.step(pool.tensor_tensor(
                        kern[:, c, NB * a:NB * (a + AH)].rearrange("p (a b) -> p a b", a=AH),
                        prod[:, :, :, 0], prod[:, :, :, 1], ALU.add))
            for c in range(CC):
                last = pool.tensor_tensor(kern[:, c, 127:128], kern[:, c, 127:128], d_skip[:, c:c + 1], ALU.add)
                ch.step(last)
            pool.dma_start(kern_dram.rearrange("(c p) l -> p c l", p=P)[:, :, 0:T + P],
                           kern[:, :, P - T:2 * P]).then_inc(kern_out, 16)

        @block.scalar
        def _(act):
            act.dma_start(bv[:], A["L0_tok_bv"].rearrange("(c p) -> p c", p=P),
                          allow_slow_non_contiguous=True).then_inc(weights_in, 16)
            act.wait_ge(consts_made, 1)
            act.dma_start(tap_row[0:1, TIN - TAPS:TIN], A["L0_tok_decay_w"].rearrange("(a n) -> a n", a=1))\
               .then_inc(taps_in, 16)
            act.wait_ge(taps_in, 16)
            act.dma_start(taps_dram, tap_row[:]).then_inc(taps_out, 16)
            act.wait_ge(taps_out, 16)
            act.dma_start(conv_rev[:], bass.AP(taps_dram.tensor, 0, [[1, TIN], [1, T]])).then_inc(conv_in, 16)
            act.dma_start(logs[:, 0:2], A["L0_attn_log_dt"].rearrange("(c p) -> p c", p=P),
                          allow_slow_non_contiguous=True).then_inc(modes_in, 16)
            act.dma_start(logs[:, 2:2 + CC * NM].rearrange("p (c n) -> p c n", c=CC),
                          A["L0_attn_log_A_real"].rearrange("(c p) n -> p c n", p=P)).then_inc(modes_in, 16)
            act.dma_start(a_im[:], A["L0_attn_A_imag"].rearrange("(c p) n -> p c n", p=P)).then_inc(modes_in, 16)
            act.dma_start(c_in[:], A["L0_attn_C"].rearrange("(c p) n r -> p c n r", p=P)).then_inc(modes_in, 16)
            act.dma_start(d_skip[:], A["L0_attn_D"].rearrange("(c p) -> p c", p=P),
                          allow_slow_non_contiguous=True).then_inc(modes_in, 16)

            def normalise(i, k):
                if k == 0:
                    wait_apart(act, norm_ready, i + 1, passed_act)
                for j in range(2):
                    n = 2 * k + j
                    b = xn[:, bass.ds(2 * (i * STEP + k) + j, 1), :].rearrange("p o c -> p (o c)")
                    act.activation(b, b, ACT.Identity, bias=shift[:, n:n + 1], scale=rstd[:, n:n + 1])\
                       .then_inc(norm_done, 1)

            def turn(i, conv=True, proj=True, norm=True):
                if conv:
                    for k in range(STEP):
                        u = i * STEP + k
                        act.wait_ge(conv_done, u + 1)
                        wait(act, proj_done, u - STEP + 1)
                        act.activation(s_hi[:, k], ps_s[k][:, 0:2 * CC * T], ACT.Copy).then_inc(s_hi_ready, 1)
                for k in range(STEP + 1):
                    if norm and k < STEP:
                        wait_apart(act, h1_stored[k], 16 * (i - 1), passed_act)
                    if proj and k < STEP:
                        v = (i - 1) * STEP + k
                        wait_apart(act, proj_done, v + 1, passed_act)
                        act.copy(h1[:, bass.ds(2 * v, 2), :], ps_h[k][0:T, :].rearrange("p (b c) -> p b c", b=2))\
                           .then_inc(h1_ready, 1)
                    if norm and k > 0:
                        normalise(i - 2, k - 1)

            turn(0, proj=False, norm=False)
            act.wait_ge(angles_ready, 1)
            act.activation(g["sin"][:], g["yi"][:], ACT.Sin).then_inc(sines_ready, 1)
            act.activation(g["cos"][:], g["t"][:], ACT.Sin).then_inc(sines_ready, 1)
            turn(1, norm=False)
            with act.Fori(2, TURNS) as i:
                turn(i)
            turn(TURNS, conv=False)
            turn(TURNS + 1, conv=False, proj=False)

        @block.vector
        def _(dve):
            ch = Chain(dve, setup)
            dve.wait_ge(weights_in, 80)
            ch.step(dve.reduce_sum(tap_sum[:], tap_all[:], AX))
            ch.step(dve.tensor_scalar(bv_sum[:], bv[:], tap_sum[:, 0:1], None, ALU.mult))
            dve.wait_ge(consts_made, 3)
            for c in range(CC):
                ch.step(dve.tensor_scalar(bv_rows[:, c, :], ones[:, 0:T], bv_sum[:, c:c + 1], None, ALU.mult))
            dve.wait_ge(woT_done, 1)
            for c in range(CC):
                dve.tensor_copy(woT[:, c, :], ps_w[c][:, 0:C]).then_inc(woT_copied, 1)
            dve.wait_ge(conv_in, 16)
            dve.tensor_copy(conv[:], conv_rev[:, ::-1]).then_inc(weights_ready, 1)
            dve.wait_ge(w_done, 1)
            for c in range(CC):
                split(ch, dve, w_hi[:, c, :], w_lo[:, c, :], ps_w[c][:, 0:C])
            dve.wait_ge(sel_made, 3)
            dve.tensor_copy(sel[:], sel_f32[:])
            for j in range(2):
                ch.step(dve.tensor_copy(bias[:, j], ps_b[0:2 * PART, 0:C]))
            for j in range(2):
                low = slice(PART, 2 * PART)
                ins = dve.tensor_tensor(bias[low, j], ps_b[low, 0:C], bias[low, j].bitcast(F32), ALU.subtract)
            ins.then_inc(weights_ready, 1)
            m = {n: x[:].rearrange("p c n -> p (c n)") for n, x in g.items()}
            n_modes = CC * NM

            def angles():
                dve.wait_ge(modes_in, 80)
                exp_steps(ch, dve, logs[:], s0[:], s1[:], s2[:], exps[:], s3[:])
                for c in range(CC):
                    ch.step(dve.tensor_scalar(g["are"][:, c, :], exps[:, 2 + c * NM:2 + (c + 1) * NM], -1.0, None, ALU.mult))
                    ch.step(dve.tensor_scalar(g["xr"][:, c, :], g["are"][:, c, :], exps[:, c:c + 1], None, ALU.mult))
                    ch.step(dve.tensor_scalar(g["yi"][:, c, :], a_im[:, c, :], exps[:, c:c + 1], None, ALU.mult))
                ch.step(dve.tensor_scalar(m["t"], m["yi"], 1.0 / TWO_PI, ROUND, ALU.mult, ALU.add))
                ch.step(dve.tensor_scalar(m["t"], m["t"], -ROUND, None, ALU.add))
                for part in (PI2_A, PI2_B, PI2_C):
                    ch.step(dve.scalar_tensor_tensor(m["yi"], m["t"], -part, m["yi"], ALU.mult, ALU.add))
                ch.step(dve.tensor_scalar(m["yi"], m["yi"], PI_BELOW, -PI_BELOW, ALU.min, ALU.max))
                ch.step(dve.tensor_scalar(m["u"], m["yi"], -1.0, None, ALU.mult))
                ch.step(dve.tensor_tensor(m["u"], m["u"], m["yi"], ALU.max))
                ch.step(dve.tensor_scalar(m["t"], m["u"], -1.0, TWO_PI / 4, ALU.mult, ALU.add))
                ch.step(dve.tensor_copy(m["u"], m["t"]))
                dve.sem_inc(angles_ready, 1)

            def modes():
                n = n_modes
                exp_steps(ch, dve, m["xr"], s0[:, 0:n], s1[:, 0:n], s2[:, 0:n], m["mag"], s3[:, 0:n])
                im = a_im[:].rearrange("p c n -> p (c n)")
                ch.step(dve.tensor_tensor(m["den"], m["are"], m["are"], ALU.mult))
                ch.step(dve.tensor_tensor(m["u"], im, im, ALU.mult))
                ch.step(dve.tensor_tensor(m["den"], m["den"], m["u"], ALU.add))
                ch.step(dve.reciprocal(m["u"], m["den"]))
                ch.step(dve.tensor_tensor(m["ir"], m["are"], m["u"], ALU.mult))
                ch.step(dve.scalar_tensor_tensor(m["ii"], im, -1.0, m["u"], ALU.mult, ALU.mult))
                dve.wait_ge(sines_ready, 2)
                ch.step(dve.tensor_tensor(m["zr"], m["mag"], m["cos"], ALU.mult))
                ch.step(dve.tensor_tensor(m["zi"], m["mag"], m["sin"], ALU.mult))
                ch.step(dve.tensor_scalar(m["mag"], m["zr"], -1.0, None, ALU.add))
                ch.step(dve.tensor_tensor(m["den"], m["mag"], m["ir"], ALU.mult))
                ch.step(dve.tensor_tensor(m["t"], m["zi"], m["ii"], ALU.mult))
                ch.step(dve.tensor_tensor(m["den"], m["den"], m["t"], ALU.subtract))
                ch.step(dve.tensor_tensor(m["u"], m["mag"], m["ii"], ALU.mult))
                ch.step(dve.tensor_tensor(m["t"], m["zi"], m["ir"], ALU.mult))
                ch.step(dve.tensor_tensor(m["u"], m["u"], m["t"], ALU.add))
                c_re = c_in[:].rearrange("p c n r -> p (c n) r")[:, :, 0]
                c_im = c_in[:].rearrange("p c n r -> p (c n) r")[:, :, 1]
                ch.step(dve.tensor_tensor(m["cr"], m["den"], c_re, ALU.mult))
                ch.step(dve.tensor_tensor(m["t"], m["u"], c_im, ALU.mult))
                ch.step(dve.tensor_tensor(m["cr"], m["cr"], m["t"], ALU.subtract))
                ch.step(dve.tensor_scalar(m["cr"], m["cr"], 2.0, None, ALU.mult))
                ch.step(dve.tensor_tensor(m["ci"], m["den"], c_im, ALU.mult))
                ch.step(dve.tensor_tensor(m["t"], m["u"], c_re, ALU.mult))
                ch.step(dve.tensor_tensor(m["ci"], m["ci"], m["t"], ALU.add))
                dve.tensor_scalar(m["ci"], m["ci"], 2.0, None, ALU.mult).then_inc(modes_ready, 1)

            def turn(i, conv=True, proj=True):
                if conv:
                    for k in range(STEP):
                        u = i * STEP + k
                        dve.wait_ge(s_hi_ready, u + 1)
                        dve.tensor_tensor(s_lo[:, k], ps_s[k][:, 0:2 * CC * T], s_hi[:, k].bitcast(F32),
                                          ALU.subtract).then_inc(s_lo_ready, 1)
                if proj:
                    for k in range(STEP):
                        v = (i - 1) * STEP + k
                        wait_apart(dve, h1_ready, v + 1, passed_dve)
                        for j in range(2):
                            b = h1[:, bass.ds(2 * v + j, 1), :].rearrange("p o c -> p (o c)")
                            dve.bn_stats(stats[:, 2 * k + j, :], b).then_inc(stats_done, 1)
                    v = (i - 1) * STEP
                    wait_apart(dve, stats_done, 2 * (v + STEP), passed_dve)
                    for n in range(2 * STEP):
                        dve.bn_aggr(mv[:, n, :], stats[:, n, :]).then_inc(aggr_done, 1)
                    dve.wait_ge(aggr_done, 2 * (v + STEP))
                    wait(dve, norm_done, 2 * v)
                    ch = Chain(dve, rstd_chain, (i - 1) * RSTD_STEPS)
                    rstd_steps(ch, dve, mv[:, :, 1], var[:], rstd[:], newton[:])
                    dve.scalar_tensor_tensor(shift[:], mv[:, :, 0], -1.0, rstd[:], ALU.mult, ALU.mult)\
                       .then_inc(norm_ready, 1)

            turn(0, proj=False)
            angles()
            turn(1)
            modes()
            with dve.Fori(2, TURNS) as i:
                turn(i)
            turn(TURNS, conv=False)

        @block.tensor
        def _(pe):
            pe.wait_ge(consts_made, 3)
            pe.wait_ge(weights_in, 80)
            for m in range(CC):
                for e in range(CC):
                    last = pe.transpose(ps_w[m][:, e * P:(e + 1) * P], wo[:, e, m * P:(m + 1) * P], ident[:])
            last.then_inc(woT_done, 1)
            pe.wait_ge(woT_copied, 2)
            for m in range(CC):
                pe.matmul(ps_b[0:T, 0:C], bv_rows[:, m, :], woT[:, m, :], start=(m == 0), stop=False)
            pe.matmul(ps_b[0:T, 0:C], ones[0:1, 0:T], bo_row[:], start=False, stop=True)
            for d in range(CC):
                for m in range(CC):
                    last = pe.matmul(ps_w[d][:, 0:C], wv[:, m, d * P:(d + 1) * P], woT[:, m, :],
                                     start=(m == 0), stop=(m == CC - 1))
            last.then_inc(w_done, 1)
            pe.wait_ge(weights_ready, 2)

            def turn(i, conv_=True, proj=True):
                if conv_:
                    for k in range(STEP):
                        u = i * STEP + k
                        pe.wait_ge(x_loaded[k], 32 * (i + 1))
                        wait(pe, s_lo_ready, u - STEP + 1)
                        for j in range(2):
                            for c in range(CC):
                                n = (j * CC + c) * T
                                last = pe.matmul(ps_s[k][:, n:n + T], x_in[:, k, j, c * P:(c + 1) * P], conv[:],
                                                 start=True, stop=True)
                        last.then_inc(conv_done, 1)
                if proj:
                    for k in range(STEP):
                        v = (i - 1) * STEP + k
                        wait(pe, s_lo_ready, v + 1)
                        wait(pe, h1_ready, v - STEP + 1)
                        pe.matmul(ps_h[k][0:T, :], sel[:], bias[:].rearrange("p b c -> p (b c)"), start=True, stop=False)
                        for j in range(2):
                            for c in range(CC):
                                n = (j * CC + c) * T
                                last = matmul3(pe, ps_h[k][0:T, j * C:(j + 1) * C], s_hi[:, k, n:n + T],
                                               s_lo[:, k, n:n + T], w_hi[:, c, :], w_lo[:, c, :], False,
                                               j == 1 and c == CC - 1)
                        last.then_inc(proj_done, 1)

            turn(0, proj=False)
            turn(1)
            with pe.Fori(2, TURNS) as i:
                turn(i)
            turn(TURNS, conv_=False)


def phase_states(nc, A, scratch, xn, hankel, raw1):
    CH = 4
    UNITS = 16
    BANKS = 8
    TURNS_B = C // (CH * UNITS)
    LD = 2
    SLOTS = UNITS // LD
    assert UNITS * CH == HANKEL and SLOTS == HANKEL_SLOTS
    y_dram, rows_in, toep_loaded = scratch["y"], hankel["rows"], hankel["loaded"]
    with ExitStack() as ctx:
        toep = ctx.enter_context(nc.sbuf_tensor("toep", [T, UNITS * CH, T], F32))
        ps = [ctx.enter_context(nc.psum_tensor(f"ps_y{n}", [P, CH, P], F32)) for n in range(BANKS)]
        toep_ready = ctx.enter_context(nc.semaphore("toep_ready"))
        y_done = ctx.enter_context(nc.semaphore("y_done"))
        y_ready = ctx.enter_context(nc.semaphore("y_ready"))
        y_stored = ctx.enter_context(nc.semaphore("y_stored"))
        raw_in = ctx.enter_context(nc.semaphore("raw_in"))
        passed_dve = ctx.enter_context(nc.semaphore("b_passed_dve"))
        block = ctx.enter_context(nc.Block())

        @block.sync
        def _(sp):
            def turn(i):
                for s in range(SLOTS):
                    wait(sp, toep_ready, (i - 1) * SLOTS + s + 1)
                    load_hankel(sp, scratch, hankel, i, s)

            with sp.Fori(1, TURNS_B) as i:
                turn(i)
            sp.dma_start(raw1[:], A["L0_ffn_rW1"].rearrange("(k p) n -> p k n", p=P)).then_inc(raw_in, 16)
            sp.wait_ge(raw_in, 16)
            sp.wait_ge(y_stored, 64)

        @block.vector
        def _(dve):
            def turn(i):
                for s in range(SLOTS):
                    dve.wait_ge(toep_loaded[s], 16 * (i + 1))
                    wait_apart(dve, y_done, (i - 1) * UNITS + (s + 1) * LD, passed_dve)
                    h = slice(s * LD * CH, (s + 1) * LD * CH)
                    dve.tensor_copy(toep[:, h, :], rows_in[:, h, T - 1::-1]).then_inc(toep_ready, 1)

            turn(0)
            with dve.Fori(1, TURNS_B) as i:
                turn(i)

        @block.tensor
        def _(pe):
            def turn(i):
                for n in range(UNITS):
                    if n % LD == 0:
                        pe.wait_ge(toep_ready, i * SLOTS + n // LD + 1)
                    wait(pe, y_ready, i * UNITS + n - BANKS + 1)
                    for c in range(CH):
                        h = (i * UNITS + n) * CH + c
                        channel = xn[:, :, bass.ds(h, 1)].rearrange("p b o -> p (b o)")
                        last = pe.matmul(ps[n % BANKS][0:T, c, :], toep[:, n * CH + c, :], channel, start=True, stop=True)
                    last.then_inc(y_done, 1)

            turn(0)
            with pe.Fori(1, TURNS_B) as i:
                turn(i)

        @block.scalar
        def _(act):
            def turn(i):
                for n in range(UNITS):
                    h = (i * UNITS + n) * CH
                    act.wait_ge(y_done, i * UNITS + n + 1)
                    act.copy(xn[:, :, bass.ds(h, CH)], ps[n % BANKS][0:T].rearrange("p h b -> p b h")).then_inc(y_ready, 1)

            turn(0)
            with act.Fori(1, TURNS_B // 2) as i:
                turn(i)
            act.wait_ge(y_ready, C // CH // 2)
            for n in range(4):
                b = slice(n * B // 4, (n + 1) * B // 4)
                act.dma_start(y_dram[:, b, 0:P], xn[:, b, 0:P]).then_inc(y_stored, 16)
            with act.Fori(TURNS_B // 2, TURNS_B) as i:
                turn(i)


def phase_router(nc, A, scratch, w, raw, y_left, place, gate, d):
    h1_dram, y_dram, h2_dram, rows_dram = scratch["h1"], scratch["y"], scratch["h2"], scratch["rows"]
    NT = HC
    RELU = 4
    MM = 4
    with ExitStack() as ctx:
        def sb(name, shape, dt=F32, side="left"):
            return ctx.enter_context(nc.sbuf_tensor(name, shape, dt, side=side))

        def sem(name):
            return ctx.enter_context(nc.semaphore(name))

        a1_hi = sb("a1_hi", [P, HC, GT], F32R)
        a1_lo = sb("a1_lo", [P, HC, GT], F32R)
        w["w2_hi"] = sb("w2_hi", [P, HC, HID], F32R)
        w["w2_lo"] = sb("w2_lo", [P, HC, HID], F32R)
        x2_part = [sb(f"x2_part{n}", [T, GB, C], BF16) for n in range(3)]
        x2_rest = sb("x2_rest", [T, GB, C])
        rows = sb("rows", [P, CC, E, GB, CAP])
        onehot = sb("onehot", [T, GB * E, CAP], BF16)
        logT = sb("logT", [2 * E, GT])
        logit = sb("logit", [T, GB, E])
        ex = sb("ex", [T, GB, E])
        prob = sb("prob", [T, GB, E])
        first = sb("first", [T, GB, E])
        rest = sb("rest", [T, GB, E])
        chosen = sb("chosen", [T, GB, E])
        chosen_bf = sb("chosen_bf", [T, GB * E], BF16)
        m1 = sb("m1", [T, GB])
        m2 = sb("m2", [T, GB])
        w["w1_hi"] = sb("w1_hi", [P, CC, HID], F32R)
        w["w1_lo"] = sb("w1_lo", [P, CC, HID], F32R)
        raw3 = sb("raw3", [P, HC, E])
        h1 = sb("c_h1", [T, GB, C])
        y = sb("c_y", [T, GB, C])
        h2 = sb("c_h2", [T, GB, C])
        x2 = sb("c_x2", [T, GB, C])
        stats = sb("c_stats", [T, GB, 6])
        mv = sb("c_mv", [T, GB, 2])
        var = sb("c_var", [T, GB])
        rstd = sb("c_rstd", [T, GB])
        newton = sb("c_newton", [T, GB])
        shift = sb("c_shift", [T, GB])
        xT_hi = sb("xT_hi", [P, CC, GT], F32R)
        xT_lo = sb("xT_lo", [P, CC, GT], F32R)
        a2_hi = sb("a2_hi", [P, HC, GT], F32R, side="right")
        a2_lo = sb("a2_lo", [P, HC, GT], F32R, side="right")
        w["w3"] = sb("w3", [P, HC, 2 * E], F32R, side="right")
        relu = sb("relu", [P, RELU, GT], side="right")
        key = sb("key", [T, GB, E], side="right")
        w["rb1"], w["rb2"], w["rb3"] = (sb(n, [P, size], side="right") for n, size in (("rb1", HC), ("rb2", HC), ("rb3", E)))

        ps_m = [ctx.enter_context(nc.psum_tensor(f"ps_m{n}", [P, 512], F32)) for n in range(MM)]
        ps_x = [ctx.enter_context(nc.psum_tensor(f"ps_x{n}", [P, 512], F32)) for n in range(3)]
        ps_l = ps_x[2]
        ps_r = ctx.enter_context(nc.psum_tensor("ps_r", [P, 512], F32))
        logit_ps = ps_r[0:T, 0:GB * 2 * E].rearrange("p (b e) -> p b e", b=GB)
        pos_ps = ps_r[0:T, GB * 2 * E:GB * 3 * E]

        h1_in = sem("c_h1_in")
        y_in = sem("c_y_in")
        h2_ready = sem("c_h2_ready")
        h2_stored = sem("c_h2_stored")
        stats_done = sem("c_stats_done")
        aggr_done = sem("c_aggr_done")
        prep_chain = sem("prep_chain")
        norm_ready = sem("c_norm_ready")
        norm_done = sem("c_norm_done")
        part0_ready = sem("part0_ready")
        rest_ready = sem("rest_ready")
        part1_ready = sem("part1_ready")
        part2_ready = sem("part2_ready")
        xT_done = sem("xT_done")
        xT_hi_ready = sem("xT_hi_ready")
        xT_ready = sem("xT_ready")
        tile_done = sem("tile_done")
        relu_done = sem("relu_done")
        hi_ready = sem("hi_ready")
        lo_ready = sem("lo_ready")
        logT_done = sem("logT_done")
        logT_copied = sem("logT_copied")
        logit_done = sem("logit_done")
        route_chain = sem("route_chain")
        exp_ready = sem("exp_ready")
        exp_done = sem("exp_done")
        chosen_ready = sem("chosen_ready")
        place_ready = sem("place_ready")
        pos_done = sem("pos_done")
        onehot_ready = sem("onehot_ready")
        rows_done = sem("rows_done")
        rows_copied = sem("rows_copied")
        rows_stored = sem("rows_stored")
        passed_dve = sem("c_passed_dve")
        passed_pe = sem("c_passed_pe")
        small_in = sem("small_in")
        raw2_in = [sem(f"raw2_in{k}") for k in range(HC)]
        hi_done = sem("router_hi_done")
        w1_ready = sem("w1_ready")
        w2_ready = sem("w2_ready")
        w3_ready = sem("w3_ready")
        made = sem("router_consts")
        consts_ready = sem("router_consts_ready")
        block = ctx.enter_context(nc.Block())

        LEFT = [slice(0, 4), slice(4, 16), slice(112, B), slice(16, 48), slice(48, 80), slice(80, 112)]
        left_stored = [sem(f"left_stored{n}") for n in range(len(LEFT))]

        def left_gone(eng, upto):
            for n in range(upto + 1):
                eng.wait_ge(left_stored[n], 16)

        TILES = 2 * NT
        ROUTE_STEPS = 19
        PIECES = GB * CC

        def bank_of(piece):
            n = piece % 3 * SL
            return ps_x[piece // 3][:, n:n + SL]

        def w2_low(eng, k):
            eng.wait_ge(hi_done, k + 2)
            eng.tensor_tensor(w["w2_lo"][:, k], raw["w2"][:, k], w["w2_hi"][:, k].bitcast(F32), ALU.subtract)\
               .then_inc(w2_ready, 1)

        def groups(eng, turn, before, after):
            before()
            turn(0, route=False)
            turn(1)
            with eng.Fori(2, NG - 1) as g:
                turn(g)
            turn(NG - 1, prep=False)
            after()

        @block.sync
        def _(sp):
            def load(g):
                wait(sp, h2_ready, g)
                sp.dma_start(h1[:], h1_dram[:, bass.ds(g * GB, GB), :]).then_inc(h1_in, 16)
                sp.dma_start(y[:], y_dram[:, bass.ds(g * GB, GB), :]).then_inc(y_in, 16)

            def store_h2(g):
                wait(sp, h2_ready, g + 1)
                sp.dma_start(h2_dram[:, bass.ds(g * GB, GB), :], h2[:]).then_inc(h2_stored, 16)

            def store_rows(g):
                wait(sp, rows_copied, PIECES * (g + 1))
                sp.dma_start(rows_dram[:, :, bass.ds(g * GB * CAP, GB * CAP)],
                             rows[:].rearrange("p c e b s -> p (c e) (b s)")).then_inc(rows_stored, 16)

            def store_left(n):
                sp.dma_start(y_dram[:, LEFT[n], P:C], y_left[:, LEFT[n], P:C]).then_inc(left_stored[n], 16)

            sp.dma_start(h1[:], h1_dram[:, 0:GB, :]).then_inc(h1_in, 16)
            store_left(0)
            store_left(1)
            sp.wait_ge(left_stored[0], 16)
            sp.dma_start(y[:], y_dram[:, 0:GB, :]).then_inc(y_in, 16)
            sp.dma_start(raw3[:], A["L0_ffn_rW3"].rearrange("(k p) n -> p k n", p=P)).then_inc(small_in, 16)
            for name, dst in (("L0_ffn_rb1", w["rb1"]), ("L0_ffn_rb2", w["rb2"])):
                sp.dma_start(dst[:], A[name].rearrange("(k p) -> p k", p=P),
                             allow_slow_non_contiguous=True).then_inc(small_in, 16)
            sp.dma_start(w["rb3"][:], bass.AP(A["L0_ffn_rb3"].tensor, 0, [[0, P], [1, E]])).then_inc(small_in, 16)
            for n in range(2, len(LEFT)):
                store_left(n)
            for k in range(HC):
                sp.dma_start(raw["w2"][:, k], A["L0_ffn_rW2"][k * P:(k + 1) * P]).then_inc(raw2_in[k], 16)
            left_gone(sp, len(LEFT) - 1)
            store_h2(0)
            load(1)
            store_h2(1)
            load(2)

            def turn(g):
                store_rows(g - 1)
                store_h2(g + 1)
                load(g + 2)

            turn(1)
            with sp.Fori(2, NG - 2) as g:
                turn(g)
            store_rows(NG - 3)
            store_h2(NG - 1)
            store_rows(NG - 2)
            sp.wait_ge(h2_stored, 16 * NG)
            sp.wait_ge(rest_ready, NG)
            sp.wait_ge(tile_done, (NG - 1) * TILES + NT)
            sp.dma_start(d["w1_raw"][:], A["L0_ffn_eW1"][0].rearrange("(k p) n -> p k n", p=P)).then_inc(d["first_in"], 16)
            sp.dma_start(d["w2_raw"][:], A["L0_ffn_eW2"][0].rearrange("(k p) n -> p k n", p=P)).then_inc(d["first_in"], 16)
            sp.wait_ge(rows_stored, 16 * (NG - 1))

            def load_rows(at):
                src = rows_dram.rearrange("p (c e) n -> p c e n", c=CC)[:, :, 0, at]
                return sp.dma_start(d["rows"][:, :, at], src)

            load_rows(slice(0, (B - GB) * CAP)).then_inc(d["first_in"], 16)
            store_rows(NG - 1)
            sp.wait_ge(rows_stored, 16 * NG)
            load_rows(slice((B - GB) * CAP, B * CAP)).then_inc(d["first_rows_in"], 16)
            sp.wait_ge(d["first_in"], 48)

        @block.gpsimd
        def _(pool):
            left_gone(pool, 1)
            pool.memset(w["ident"][:], 0.0).then_inc(made, 1)
            pool.memset(w["earlier"][:], 1.0).then_inc(made, 1)
            pool.wait_ge(made, 1)
            pool.affine_select(out=w["ident"][:], in_=w["ident"][:], compare_op=ALU.not_equal, fill=1.0, base=0,
                               pattern=[[-1, P]], channel_multiplier=1).then_inc(consts_ready, 1)
            pool.wait_ge(made, 2)
            pool.affine_select(out=w["earlier"][:], in_=w["earlier"][:], compare_op=ALU.is_gt, fill=0.0, base=0,
                               pattern=[[1, T]], channel_multiplier=-1).then_inc(consts_ready, 1)
            pool.iota(w["rank"][:], pattern=[[0, GB], [-1, E]], base=E, channel_multiplier=0,
                      allow_small_or_imprecise_dtypes=True).then_inc(consts_ready, 1)
            pool.iota(w["slot_no"][:], pattern=[[0, GB * E], [1, CAP]], base=0, channel_multiplier=0,
                      allow_small_or_imprecise_dtypes=True).then_inc(consts_ready, 1)
            left_gone(pool, 5)
            for k in range(0, 6, 2):
                w2_low(pool, k)

        @block.scalar
        def _(act):
            def norm(g):
                wait(act, norm_ready, g + 1)
                wait(act, rest_ready, g)
                wait(act, xT_done, g)
                for b in range(GB):
                    act.activation(x2[:, b], h2[:, b], ACT.Identity, bias=shift[:, b:b + 1], scale=rstd[:, b:b + 1])\
                       .then_inc(norm_done, 1)

            def copy_xT(g):
                wait(act, xT_done, g + 1)
                for c in range(CC):
                    act.copy(xT_hi[:, c], ps_x[c][:, 0:GT]).then_inc(xT_hi_ready, 1)

            def relus(g, layer, tiles):
                bias = w["rb1"] if layer == 0 else w["rb2"]
                for t in tiles:
                    n = g * TILES + layer * NT + t
                    act.wait_ge(tile_done, n + 1)
                    wait(act, lo_ready, n - RELU + 1)
                    act.activation(relu[:, t % RELU], ps_m[t % MM][:, 0:GT], ACT.Relu,
                                   bias=bias[:, t:t + 1]).then_inc(relu_done, 1)

            def copy_logT(g):
                wait(act, logT_done, g + 1)
                act.copy(logT[:], ps_l[0:2 * E, 0:GT]).then_inc(logT_copied, 1)

            def exps(g):
                wait(act, exp_ready, g + 1)
                act.activation(ex[:], logit[:], ACT.Exp).then_inc(exp_done, 1)

            def copy_rows(g):
                wait(act, rows_done, g + 1)
                wait(act, rows_stored, 16 * g)
                for n in range(PIECES):
                    act.copy(rows[:, n // GB, :, n % GB, :], bank_of(n).rearrange("p (e s) -> p e s", e=E))\
                       .then_inc(rows_copied, 1)

            def part0(g):
                wait(act, rows_done, g)
                wait(act, norm_done, GB * (g + 1))
                act.copy(x2_part[0][:], x2[:]).then_inc(part0_ready, 1)

            def part1(g):
                wait(act, rest_ready, g + 1)
                act.copy(x2_part[1][:], x2_rest[:]).then_inc(part1_ready, 1)

            def turn(g, route=True, prep=True):
                if route:
                    relus(g, 0, range(NT))
                    copy_logT(g - 1)
                else:
                    relus(g, 0, range(4))
                    left_gone(act, 4)
                    w2_high(range(2))
                    relus(g, 0, [4, 5])
                    w2_high([2, 3])
                    relus(g, 0, [6, 7])
                    w2_high(range(4, HC))
                    act.wait_ge(w2_ready, HC)
                    act.copy(w["w3"][:, :, 0:E], raw3[:]).then_inc(hi_done, 1)
                    left_gone(act, 5)
                relus(g, 1, [0])
                if route:
                    exps(g - 1)
                relus(g, 1, [1, 2, 3])
                if route:
                    copy_rows(g - 1)
                part0(g)
                relus(g, 1, [4])
                if prep:
                    norm(g + 1)
                part1(g)
                relus(g, 1, [5])
                if prep:
                    copy_xT(g + 1)
                relus(g, 1, [6, 7])

            def w2_high(chunks):
                for k in chunks:
                    act.wait_ge(raw2_in[k], 16)
                    act.copy(w["w2_hi"][:, k], raw["w2"][:, k]).then_inc(hi_done, 1)

            def before():
                left_gone(act, 2)
                act.copy(w["w1_hi"][:], raw["w1"][:]).then_inc(hi_done, 1)
                norm(0)
                copy_xT(0)
                act.wait_ge(small_in, 64)
                act.wait_ge(w1_ready, 1)

            def after():
                copy_logT(NG - 1)
                exps(NG - 1)
                copy_rows(NG - 1)

            groups(act, turn, before, after)

        @block.vector
        def _(dve):
            def stats_of(g):
                wait(dve, h1_in, 16 * (g + 1))
                wait(dve, y_in, 16 * (g + 1))
                wait(dve, h2_stored, 16 * g)
                wait(dve, norm_done, GB * g)
                dve.tensor_tensor(h2[:], h1[:], y[:], ALU.add).then_inc(h2_ready, 1)
                wait(dve, h2_ready, g + 1)
                for b in range(GB):
                    dve.bn_stats(stats[:, b, :], h2[:, b]).then_inc(stats_done, 1)
                wait_apart(dve, stats_done, GB * (g + 1), passed_dve)
                for b in range(GB):
                    dve.bn_aggr(mv[:, b, :], stats[:, b, :]).then_inc(aggr_done, 1)
                wait(dve, aggr_done, GB * (g + 1))
                ch = Chain(dve, prep_chain, g * RSTD_STEPS)
                rstd_steps(ch, dve, mv[:, :, 1], var[:], rstd[:], newton[:])
                dve.scalar_tensor_tensor(shift[:], mv[:, :, 0], -1.0, rstd[:], ALU.mult, ALU.mult)\
                   .then_inc(norm_ready, 1)

            def split_xT(g):
                wait(dve, xT_hi_ready, CC * (g + 1))
                for c in range(CC):
                    dve.tensor_tensor(xT_lo[:, c], ps_x[c][:, 0:GT], xT_hi[:, c].bitcast(F32), ALU.subtract)\
                       .then_inc(xT_ready, 1)

            def splits(g, layer, tiles):
                hi, lo = (a1_hi, a1_lo) if layer == 0 else (a2_hi, a2_lo)
                for t in tiles:
                    n = g * TILES + layer * NT + t
                    dve.wait_ge(relu_done, n + 1)
                    if layer == 1 and t == 0:
                        wait(dve, logT_done, g)
                    dve.tensor_copy(hi[:, t], relu[:, t % RELU]).then_inc(hi_ready, 1)
                    dve.wait_ge(hi_ready, n + 1)
                    dve.tensor_tensor(lo[:, t], relu[:, t % RELU], hi[:, t].bitcast(F32), ALU.subtract)\
                       .then_inc(lo_ready, 1)

            def rest_of_x2(g):
                wait(dve, part0_ready, g + 1)
                wait(dve, part2_ready, g)
                dve.tensor_tensor(x2_rest[:], x2[:], x2_part[0][:], ALU.subtract).then_inc(rest_ready, 1)

            def part2(g):
                wait(dve, part1_ready, g + 1)
                dve.tensor_tensor(x2_part[2][:], x2_rest[:], x2_part[1][:], ALU.subtract).then_inc(part2_ready, 1)

            def over_e(x):
                return x[:].rearrange("p (b o) -> p b o", o=1).to_broadcast((T, GB, E))

            def best(ch, scores, mask):
                ch.step(dve.tensor_reduce(m1[:], scores, AX, ALU.max))
                ch.step(dve.tensor_tensor(key[:], scores, over_e(m1), ALU.is_equal))
                ch.step(dve.tensor_tensor(key[:], key[:], w["rank"][0:T], ALU.mult))
                ch.step(dve.tensor_reduce(m2[:], key[:], AX, ALU.max))
                ch.step(dve.tensor_tensor(mask, key[:], over_e(m2), ALU.is_equal))

            def choose(g):
                ch = Chain(dve, route_chain, g * ROUTE_STEPS)
                wait(dve, logit_done, g + 1)
                bias = w["rb3"][0:T, :].rearrange("p (o e) -> p o e", o=1).to_broadcast((T, GB, E))
                ch.step(dve.tensor_tensor(logit[:], logit_ps[:, :, 0:E], bias, ALU.add))
                ch.step(dve.tensor_tensor(logit[:], logit_ps[:, :, E:2 * E], logit[:], ALU.add))
                ch.step(dve.tensor_reduce(m1[:], logit[:], AX, ALU.max))
                dve.tensor_tensor(logit[:], logit[:], over_e(m1), ALU.subtract).then_inc(exp_ready, 1)
                wait(dve, exp_done, g + 1)
                ch.step(dve.reduce_sum(m2[:], ex[:], AX))
                ch.step(dve.reciprocal(m1[:], m2[:]))
                ch.step(dve.tensor_tensor(prob[:], ex[:], over_e(m1), ALU.mult))
                best(ch, prob[:], first[:])
                ch.step(dve.scalar_tensor_tensor(rest[:], first[:], -2.0, prob[:], ALU.mult, ALU.add))
                best(ch, rest[:], chosen[:])
                ch.step(dve.tensor_tensor(chosen[:], chosen[:], first[:], ALU.add))
                dve.tensor_copy(chosen_bf[:], chosen[:].rearrange("p b e -> p (b e)")).then_inc(chosen_ready, 1)
                dve.tensor_tensor(gate[:, bass.ds(g * GB * E, GB * E)].rearrange("p (b e) -> p b e", b=GB),
                                  prob[:], chosen[:], ALU.mult)
                assert ch.n == ROUTE_STEPS - 1

            def slots(g):
                at = place[:, bass.ds(g * GB * E, GB * E)]
                wait(dve, pos_done, g + 1)
                dve.tensor_scalar(key[:], chosen[:], -1000.0, 1000.0, ALU.mult, ALU.add).then_inc(route_chain, 1)
                dve.wait_ge(route_chain, (g + 1) * ROUTE_STEPS)
                dve.tensor_tensor(at, pos_ps, key[:].rearrange("p b e -> p (b e)"), ALU.add)\
                   .then_inc(place_ready, 1)
                wait(dve, place_ready, g + 1)
                wait(dve, rows_done, g)
                dve.tensor_tensor(onehot[:], w["slot_no"][0:T],
                                  at.rearrange("p (n o) -> p n o", o=1).to_broadcast((T, GB * E, CAP)),
                                  ALU.is_equal).then_inc(onehot_ready, 1)

            def turn(g, route=True, prep=True):
                if not route:
                    left_gone(dve, 3)
                splits(g, 0, range(NT))
                if not route:
                    left_gone(dve, 5)
                    for k in (1, 3, 5, 6, 7):
                        w2_low(dve, k)
                    dve.wait_ge(w2_ready, HC)
                    dve.wait_ge(hi_done, HC + 2)
                    dve.tensor_tensor(w["w3"][:, :, E:2 * E], raw3[:], w["w3"][:, :, 0:E].bitcast(F32), ALU.subtract)\
                       .then_inc(w3_ready, 1)
                    dve.wait_ge(consts_ready, 4)
                splits(g, 1, [0])
                if route:
                    choose(g - 1)
                splits(g, 1, [1])
                if prep:
                    stats_of(g + 1)
                splits(g, 1, [2])
                if route:
                    slots(g - 1)
                splits(g, 1, [3])
                rest_of_x2(g)
                splits(g, 1, [4])
                part2(g)
                splits(g, 1, [5])
                if prep:
                    split_xT(g + 1)
                splits(g, 1, [6, 7])

            def before():
                stats_of(0)
                dve.wait_ge(hi_done, 1)
                dve.tensor_tensor(w["w1_lo"][:], raw["w1"][:], w["w1_hi"][:].bitcast(F32), ALU.subtract)\
                   .then_inc(w1_ready, 1)
                split_xT(0)

            def after():
                choose(NG - 1)
                slots(NG - 1)

            groups(dve, turn, before, after)

        @block.tensor
        def _(pe):
            def transpose_x2(g):
                wait(pe, norm_done, GB * (g + 1))
                wait(pe, rows_copied, PIECES * (g - 1))
                wait(pe, xT_ready, CC * g)
                for c in range(CC):
                    for b in range(GB):
                        last = pe.transpose(ps_x[c][:, b * T:(b + 1) * T], x2[:, b, c * P:(c + 1) * P],
                                            w["ident"][0:T, 0:T])
                last.then_inc(xT_done, 1)

            def layer(g, n_layer, tiles):
                w_hi, w_lo = (w["w1_hi"], w["w1_lo"]) if n_layer == 0 else (w["w2_hi"], w["w2_lo"])
                x_hi, x_lo = (xT_hi, xT_lo) if n_layer == 0 else (a1_hi, a1_lo)
                chunks = CC if n_layer == 0 else HC
                for t in tiles:
                    n = g * TILES + n_layer * NT + t
                    if n_layer == 0 and t == 0:
                        wait(pe, xT_ready, CC * (g + 1))
                    wait(pe, relu_done, n - MM + 1)
                    for k in range(chunks):
                        if n_layer == 1 and t == 0:
                            wait(pe, lo_ready, g * TILES + k + 1)
                        o = slice(t * P, (t + 1) * P)
                        last = matmul3(pe, ps_m[t % MM][:, 0:GT], w_hi[:, k, o], w_lo[:, k, o], x_hi[:, k], x_lo[:, k],
                                       k == 0, k == chunks - 1)
                    last.then_inc(tile_done, 1)

            def logits(g):
                if isinstance(g, int) and g == 0:
                    pe.wait_ge(w3_ready, 1)
                wait(pe, lo_ready, (g + 1) * TILES)
                wait(pe, rows_copied, PIECES * g)
                for k in range(HC):
                    pe.matmul(ps_l[0:2 * E, 0:GT], w["w3"][:, k, :], a2_hi[:, k], start=(k == 0), stop=False)
                    last = pe.matmul(ps_l[0:E, 0:GT], w["w3"][:, k, 0:E], a2_lo[:, k], start=False, stop=(k == HC - 1))
                last.then_inc(logT_done, 1)

            def transpose_logits(g):
                wait(pe, logT_copied, g + 1)
                wait_apart(pe, onehot_ready, g, passed_pe)
                for b in range(GB):
                    last = pe.transpose(ps_r[0:T, b * 2 * E:(b + 1) * 2 * E], logT[:, b * T:(b + 1) * T],
                                        w["ident"][0:2 * E, 0:2 * E])
                last.then_inc(logit_done, 1)

            def positions(g):
                wait(pe, chosen_ready, g + 1)
                pe.matmul(pos_ps, w["earlier"][:], chosen_bf[:], start=True, stop=True).then_inc(pos_done, 1)

            def gather(g):
                wait(pe, onehot_ready, g + 1)
                wait(pe, part2_ready, g + 1)
                for n in range(PIECES):
                    c, b = n // GB, n % GB
                    hot = onehot[:, b * E:(b + 1) * E, :].rearrange("p e s -> p (e s)")
                    for part in range(3):
                        last = pe.matmul(bank_of(n), x2_part[part][:, b, c * P:(c + 1) * P], hot, start=(part == 0),
                                         stop=(part == 2))
                last.then_inc(rows_done, 1)

            def turn(g, route=True, prep=True):
                layer(g, 0, range(NT))
                if route:
                    logits(g - 1)
                else:
                    pe.wait_ge(w2_ready, HC)
                    pe.wait_ge(consts_ready, 4)
                layer(g, 1, [0])
                if route:
                    transpose_logits(g - 1)
                layer(g, 1, [1, 2])
                if route:
                    positions(g - 1)
                layer(g, 1, [3])
                if route:
                    gather(g - 1)
                layer(g, 1, [4, 5])
                if prep:
                    transpose_x2(g + 1)
                layer(g, 1, [6, 7])

            def before():
                pe.wait_ge(consts_ready, 1)
                transpose_x2(0)
                pe.wait_ge(w1_ready, 1)

            def after():
                logits(NG - 1)
                transpose_logits(NG - 1)
                positions(NG - 1)
                gather(NG - 1)

            groups(pe, turn, before, after)


SPT = 4
RELU_D = 4


def expert_buffers(nc, ctx):
    def sb(name, shape, dt=F32):
        return ctx.enter_context(nc.sbuf_tensor(name, shape, dt))

    n = SPT * B
    return {
        "w1_hi": [sb(f"d_w1_hi{q}", [P, CC, HID], F32R) for q in range(2)],
        "w1_lo": [sb(f"d_w1_lo{q}", [P, CC, HID], F32R) for q in range(2)],
        "w2_hi": [sb(f"d_w2_hi{q}", [P, HC, C], F32R) for q in range(2)],
        "w2_lo": [sb(f"d_w2_lo{q}", [P, HC, C], F32R) for q in range(2)],
        "a_hi": [sb(f"d_a_hi{q}", [P, HC, n], F32R) for q in range(2)],
        "out": sb("d_out", [P, SPT, C]),
        "x_hi": [sb(f"d_x_hi{q}", [P, CC, n], F32R) for q in range(2)],
        "b2": sb("d_b2", [P, 2, C]),
        "b1_rows": sb("b1_rows", [E * HC, P]),
        "b1": sb("d_b1", [P, E * HC]),
        "x_lo": [sb(f"d_x_lo{q}", [P, CC, n], F32R) for q in range(2)],
        "w1_raw": sb("w1_raw", [P, CC, HID]),
        "w2_raw": sb("w2_raw", [P, HC, C]),
        "rows": sb("d_rows", [P, CC, B * CAP]),
        "a_lo": [sb(f"d_a_lo{q}", [P, HC, n], F32R) for q in range(2)],
        "relu": sb("d_relu", [P, RELU_D, n]),
    }


def phase_experts(nc, A, scratch, w, d):
    rows_dram, out_dram = scratch["rows"], scratch["slots"]
    TPE = -(-CAP // SPT)
    MM = 4
    RELU = RELU_D
    N = SPT * B
    assert B == P and N == 512

    def slots_of(j):
        return min(SPT, CAP - j * SPT)

    with ExitStack() as ctx:
        def sb(name, shape, dt=F32):
            return ctx.enter_context(nc.sbuf_tensor(name, shape, dt))

        def sem(name):
            return ctx.enter_context(nc.semaphore(name))

        w1_raw, w2_raw, rows = d["w1_raw"], d["w2_raw"], d["rows"]
        w1_hi, w1_lo, w2_hi, w2_lo = d["w1_hi"], d["w1_lo"], d["w2_hi"], d["w2_lo"]
        x_hi, x_lo, a_hi, a_lo, relu, out = d["x_hi"], d["x_lo"], d["a_hi"], d["a_lo"], d["relu"], d["out"]
        b1_rows, b1, b2 = d["b1_rows"], d["b1"], d["b2"]
        ps_m = [ctx.enter_context(nc.psum_tensor(f"ps_d{n}", [P, 512], F32)) for n in range(MM)]
        ps_o = [ctx.enter_context(nc.psum_tensor(f"ps_o{n}", [P, 512], F32)) for n in range(SPT)]

        b1_in = sem("b1_in")
        b1_done = sem("b1_done")
        b1_ready = sem("b1_ready")
        w_in = sem("d_w_in")
        b2_in = [sem(f"b2_in{n}") for n in range(2)]
        first_rows_in, rows_in = d["first_rows_in"], sem("d_rows_in")
        w_hi_done = sem("w_hi_done")
        w_ready = sem("d_w_ready")
        x_hi_done = sem("x_hi_done")
        x_ready = sem("d_x_ready")
        tile_done = sem("d_tile_done")
        relu_done = sem("d_relu_done")
        hi_ready = sem("d_hi_ready")
        lo_ready = sem("d_lo_ready")
        out_done = sem("d_out_done")
        out_ready = sem("d_out_ready")
        passed_act = sem("d_passed_act")
        passed_pool = sem("d_passed_pool")
        first_hi = sem("d_first_hi")
        out_stored = [sem(f"d_out_stored{n}") for n in range(SPT)]
        block = ctx.enter_context(nc.Block())

        def in_turns(eng, turn):
            turn(0, first=True)
            with eng.Fori(1, E // 2 - 1) as i:
                turn(i)
            turn(E // 2 - 1, last=True)

        def first_tile(c):
            return rows[:, c].rearrange("p (b s) -> p s b", s=CAP)[:, 0:SPT, :]

        def before(e, j):
            return (e, j - 1) if j else (e - 1, TPE - 1)

        @block.sync
        def _(sp):
            def load_w(e):
                wait(sp, w_ready, 2 * e)
                sp.dma_start(w1_raw[:], A["L0_ffn_eW1"][bass.ds(e, 1)].rearrange("e (k p) n -> p (e k) n", p=P))\
                  .then_inc(w_in, 16)
                sp.dma_start(w2_raw[:], A["L0_ffn_eW2"][bass.ds(e, 1)].rearrange("e (k p) n -> p (e k) n", p=P))\
                  .then_inc(w_in, 16)

            def load_b2(e, q):
                sp.dma_start(b2[:, q], A["L0_ffn_eb2"][bass.ds(e, 1)].to_broadcast((P, C))).then_inc(b2_in[q], 16)

            def load_rows(e):
                wait(sp, x_ready, TPE * e)
                sp.dma_start(rows[:], rows_dram.rearrange("p (c e) n -> p c e n", c=CC)[:, :, bass.ds(e, 1), :]
                             .rearrange("p c o n -> p c (o n)")).then_inc(rows_in, 16)

            def store(e, j):
                for r in range(slots_of(j)):
                    wait(sp, out_ready, e * CAP + j * SPT + r + 1)
                    sp.dma_start(out_dram[bass.ds(e * CAP + j * SPT + r, 1)].rearrange("o b c -> b (o c)"), out[:, r])\
                      .then_inc(out_stored[r], 16)

            sp.dma_start(b1_rows[:], A["L0_ffn_eb1"].rearrange("e (k p) -> (e k) p", p=P)).then_inc(b1_in, 16)

            def turn(i, first=False, last=False):
                for q in range(2):
                    e = 2 * i + q
                    for j in range(TPE):
                        if j == 0:
                            wait(sp, out_ready, (e - 1) * CAP)
                            load_b2(e, q)
                            if not (last and q == 1):
                                load_w(e + 1)
                        if not (first and q == 0 and j == 0):
                            store(*before(e, j))
                        if j == 3 and not (last and q == 1):
                            load_rows(e + 1)

            in_turns(sp, turn)
            store(E - 1, TPE - 1)
            for r in range(SPT):
                sp.wait_ge(out_stored[r], 16 * E * (TPE if r < slots_of(TPE - 1) else TPE - 1))

        @block.gpsimd
        def _(pool):
            def split_w(e, q):
                wait(pool, w_in, 32 * e)
                wait_apart(pool, out_done, (e - 1) * CAP, passed_pool)
                pool.tensor_copy(w1_hi[q][:], w1_raw[:]).then_inc(w_hi_done, 1)
                pool.tensor_copy(w2_hi[q][:], w2_raw[:]).then_inc(w_hi_done, 1)
                wait(pool, w_hi_done, 2 * e)
                pool.tensor_tensor(w1_lo[q][:], w1_raw[:], w1_hi[q][:].bitcast(F32), ALU.subtract).then_inc(w_ready, 1)
                pool.tensor_tensor(w2_lo[q][:], w2_raw[:], w2_hi[q][:].bitcast(F32), ALU.subtract).then_inc(w_ready, 1)

            def split_x(e, j, q):
                n = slots_of(j)
                if j == 0:
                    wait(pool, rows_in, 16 * e)
                elif isinstance(e, int) and e == 0 and j == 1:
                    pool.wait_ge(x_ready, 1)
                wait_apart(pool, tile_done, HC * (e * TPE + j - 1), passed_pool)
                s = (q * TPE + j) % 2
                for c in range(CC):
                    src = rows[:, c].rearrange("p (b s) -> p s b", s=CAP)[:, j * SPT:j * SPT + n, :]
                    hi = x_hi[s][:, c, 0:n * B].rearrange("p (s b) -> p s b", s=n)
                    pool.tensor_copy(hi, src).then_inc(x_hi_done, 1)
                wait(pool, x_hi_done, CC * (e * TPE + j))
                for c in range(CC):
                    src = rows[:, c].rearrange("p (b s) -> p s b", s=CAP)[:, j * SPT:j * SPT + n, :]
                    hi = x_hi[s][:, c, 0:n * B].rearrange("p (s b) -> p s b", s=n)
                    lo = x_lo[s][:, c, 0:n * B].rearrange("p (s b) -> p s b", s=n)
                    ins = pool.tensor_tensor(lo, src, hi.bitcast(F32), ALU.subtract)
                ins.then_inc(x_ready, 1)

            def turn(i, first=False, last=False):
                for q in range(2):
                    for j in range(TPE):
                        if not (first and q == 0 and j == 0):
                            split_x(2 * i + q, j, q)
                        if j == 2 and not (last and q == 1):
                            split_w(2 * i + q + 1, 1 - q)

            in_turns(pool, turn)

        @block.scalar
        def _(act):
            for c in range(CC):
                act.copy(w1_hi[0][:, c], w1_raw[:, c]).then_inc(first_hi, 1)
            act.wait_ge(first_rows_in, 16)
            for c in range(CC):
                act.copy(x_hi[0][:, c].rearrange("p (s b) -> p s b", s=SPT), first_tile(c)).then_inc(first_hi, 1)
            act.wait_ge(b1_done, 1)
            act.copy(b1[:], ps_m[0][:, 0:E * HC]).then_inc(b1_ready, 1)
            act.copy(w2_hi[0][:], w2_raw[:]).then_inc(first_hi, 1)
            act.wait_ge(b1_ready, 1)

            def turn(i, first=False, last=False):
                for q in range(2):
                    for j in range(TPE):
                        e, n = 2 * i + q, slots_of(j) * B
                        for t in range(HC):
                            m = (e * TPE + j) * HC + t
                            act.wait_ge(tile_done, m + 1)
                            wait_apart(act, lo_ready, m - RELU + 1, passed_act)
                            act.activation(relu[:, t % RELU, 0:n], ps_m[t % MM][:, 0:n], ACT.Relu,
                                           bias=b1[:, bass.ds(e * HC + t, 1)]).then_inc(relu_done, 1)

            in_turns(act, turn)

        @block.vector
        def _(dve):
            def splits(e, j, q):
                n, s = slots_of(j) * B, (q * TPE + j) % 2
                for t in range(HC):
                    m = (e * TPE + j) * HC + t
                    dve.wait_ge(relu_done, m + 1)
                    dve.tensor_copy(a_hi[s][:, t, 0:n], relu[:, t % RELU, 0:n]).then_inc(hi_ready, 1)
                    dve.wait_ge(hi_ready, m + 1)
                    dve.tensor_tensor(a_lo[s][:, t, 0:n], relu[:, t % RELU, 0:n], a_hi[s][:, t, 0:n].bitcast(F32),
                                      ALU.subtract).then_inc(lo_ready, 1)

            def add_bias(e, j, q):
                if j == 0:
                    wait(dve, b2_in[q], 16 * (e // 2 + 1) if isinstance(e, int) else 8 * (e - q) + 16)
                for r in range(slots_of(j)):
                    wait(dve, out_done, e * CAP + j * SPT + r + 1)
                    wait(dve, out_stored[r], 16 * (e * (TPE if r < slots_of(TPE - 1) else TPE - 1) + j))
                    dve.tensor_tensor(out[:, r], ps_o[r][:, 0:C], b2[:, q], ALU.add).then_inc(out_ready, 1)

            def turn(i, first=False, last=False):
                for q in range(2):
                    for j in range(TPE):
                        e = 2 * i + q
                        splits(e, j, q)
                        if not (first and q == 0 and j == 0):
                            add_bias(*before(e, j), q if j else 1 - q)

            for c in range(CC):
                dve.wait_ge(first_hi, c + 1)
                ins = dve.tensor_tensor(w1_lo[0][:, c], w1_raw[:, c], w1_hi[0][:, c].bitcast(F32), ALU.subtract)
            ins.then_inc(w_ready, 1)
            for c in range(CC):
                dve.wait_ge(first_hi, CC + c + 1)
                ins = dve.tensor_tensor(x_lo[0][:, c].rearrange("p (s b) -> p s b", s=SPT), first_tile(c),
                                        x_hi[0][:, c].rearrange("p (s b) -> p s b", s=SPT).bitcast(F32), ALU.subtract)
            ins.then_inc(x_ready, 1)
            dve.wait_ge(first_hi, 2 * CC + 1)
            dve.tensor_tensor(w2_lo[0][:], w2_raw[:], w2_hi[0][:].bitcast(F32), ALU.subtract).then_inc(w_ready, 1)
            in_turns(dve, turn)
            add_bias(E - 1, TPE - 1, 1)

        @block.tensor
        def _(pe):
            pe.wait_ge(b1_in, 16)
            pe.transpose(ps_m[0][:, 0:E * HC], b1_rows[:], w["ident"][0:E * HC, 0:E * HC]).then_inc(b1_done, 1)
            pe.wait_ge(b1_ready, 1)

            def layer1(e, j, q):
                n, s = slots_of(j) * B, (q * TPE + j) % 2
                wait(pe, x_ready, e * TPE + j + 1)
                if j == 0:
                    wait(pe, w_ready, 1 if isinstance(e, int) and e == 0 else 2 * (e + 1))
                for t in range(HC):
                    m = (e * TPE + j) * HC + t
                    wait(pe, relu_done, m - MM + 1)
                    for k in range(CC):
                        o = slice(t * P, (t + 1) * P)
                        last = matmul3(pe, ps_m[t % MM][:, 0:n], w1_hi[q][:, k, o], w1_lo[q][:, k, o],
                                       x_hi[s][:, k, 0:n], x_lo[s][:, k, 0:n], k == 0, k == CC - 1)
                    last.then_inc(tile_done, 1)

            def layer2(e, j, q):
                s = (q * TPE + j) % 2
                wait(pe, lo_ready, (e * TPE + j + 1) * HC)
                if isinstance(e, int) and e == 0 and j == 0:
                    pe.wait_ge(w_ready, 2)
                for r in range(slots_of(j)):
                    here = e * CAP + j * SPT + r
                    past = here - SPT if j or r >= slots_of(TPE - 1) else here - slots_of(TPE - 1)
                    if j == 0 and r >= slots_of(TPE - 1):
                        past = here - slots_of(TPE - 1) - SPT
                    wait(pe, out_ready, past + 1)
                    rows_at = slice(r * B, (r + 1) * B)
                    for k in range(HC):
                        last = matmul3(pe, ps_o[r][:, 0:C], a_hi[s][:, k, rows_at], a_lo[s][:, k, rows_at],
                                       w2_hi[q][:, k], w2_lo[q][:, k], k == 0, k == HC - 1)
                    last.then_inc(out_done, 1)

            def turn(i, first=False, last=False):
                for q in range(2):
                    for j in range(TPE):
                        e = 2 * i + q
                        layer1(e, j, q)
                        if not (first and q == 0 and j == 0):
                            layer2(*before(e, j), q if j else 1 - q)

            in_turns(pe, turn)
            layer2(E - 1, TPE - 1, 1)


def phase_combine(nc, scratch, w, place, gate, result):
    h2_dram, slots_dram = scratch["h2"], scratch["slots"]
    STEP_E = 4
    TURNS_E = NG // STEP_E
    with ExitStack() as ctx:
        def sb(name, shape, dt=F32):
            return ctx.enter_context(nc.sbuf_tensor(name, shape, dt))

        def sem(name):
            return ctx.enter_context(nc.semaphore(name))

        hot = sb("e_hot", [T, STEP_E, GB * E, CAP])
        mix = sb("e_mix", [T, STEP_E, GB * E, CAP])
        mixT = sb("e_mixT", [HSL, STEP_E, 2, GT])
        slots = sb("e_slots", [HSL, STEP_E, 2, GB * C])
        h2 = sb("e_h2", [T, STEP_E, GB, C])
        out = sb("e_out", [T, STEP_E, GB, C])
        ps_t = [[ctx.enter_context(nc.psum_tensor(f"ps_t{n}{h}", [P, 512], F32)) for h in range(2)] for n in range(2)]
        ps_c = [[ctx.enter_context(nc.psum_tensor(f"ps_c{n}{h}", [P, 512], F32)) for h in range(2)] for n in range(2)]
        slots_in = [sem(f"slots_in{n}") for n in range(STEP_E)]
        h2_in = [sem(f"e_h2_in{n}") for n in range(STEP_E)]
        out_stored = [sem(f"e_out_stored{n}") for n in range(STEP_E)]
        hot_done = sem("hot_done")
        mix_ready = sem("mix_ready")
        mixT_done = sem("mixT_done")
        mixT_ready = sem("mixT_ready")
        sum_done = sem("sum_done")
        out_ready = sem("e_out_ready")
        block = ctx.enter_context(nc.Block())

        def in_turns(eng, turn):
            turn(0, mixing=False)
            turn(1)
            with eng.Fori(2, TURNS_E) as i:
                turn(i)
            turn(TURNS_E, mix=False)

        @block.sync
        def _(sp):
            def load(g, k):
                for h in range(2):
                    for r in (slice(0, 64), slice(64, HSL)):
                        rows = slots_dram[h * HSL + r.start:h * HSL + r.stop, bass.ds(g * GB, GB), :]
                        sp.dma_start(slots[r, k, h], rows.rearrange("s b c -> s (b c)")).then_inc(slots_in[k], 16)
                sp.dma_start(h2[:, k], h2_dram[:, bass.ds(g * GB, GB), :]).then_inc(h2_in[k], 16)

            for k in range(STEP_E):
                load(k, k)

            def turn(i, load_next=True):
                for k in range(STEP_E):
                    g = i * STEP_E + k
                    wait(sp, out_ready, 2 * (g + 1))
                    sp.dma_start(result[bass.ds(g * GB, GB)].rearrange("b t c -> t b c"), out[:, k])\
                      .then_inc(out_stored[k], 16)
                    if load_next:
                        load(g + STEP_E, k)

            with sp.Fori(0, TURNS_E - 1) as i:
                turn(i)
            turn(TURNS_E - 1, load_next=False)
            for k in range(STEP_E):
                sp.wait_ge(out_stored[k], 16 * TURNS_E)

        @block.gpsimd
        def _(pool):
            def turn(i):
                for k in range(STEP_E):
                    g = i * STEP_E + k
                    span = bass.ds(g * GB * E, GB * E)
                    wait(pool, mixT_done, g - STEP_E + 1)
                    over = (T, GB * E, CAP)
                    wait(pool, hot_done, g + 1)
                    pool.tensor_tensor(mix[:, k], hot[:, k],
                                       gate[:, span].rearrange("p (n o) -> p n o", o=1).to_broadcast(over),
                                       ALU.mult).then_inc(mix_ready, 1)

            turn(0)
            with pool.Fori(1, TURNS_E) as i:
                turn(i)

        @block.tensor
        def _(pe):
            def turn(i, mix=True, mixing=True):
                for k in range(STEP_E):
                    if mix:
                        g = i * STEP_E + k
                        wait(pe, mix_ready, g + 1)
                        wait(pe, mixT_ready, 2 * (g - 1))
                        for h in range(2):
                            for b in range(GB):
                                at = mix_at(k, b, h)
                                last = pe.transpose(ps_t[k % 2][h][0:HSL, b * T:(b + 1) * T], at, w["ident"][0:T, 0:T])
                        last.then_inc(mixT_done, 1)
                    if mixing:
                        g = (i - 1) * STEP_E + k
                        wait(pe, mixT_ready, 2 * (g + 1))
                        wait(pe, slots_in[k], 64 * i)
                        wait(pe, out_ready, 2 * (g - 1))
                        for b in range(GB):
                            for h in range(2):
                                last = pe.matmul(ps_c[k % 2][b // 2][0:T, b % 2 * C:(b % 2 + 1) * C],
                                                 mixT[:, k, h, b * T:(b + 1) * T], slots[:, k, h, b * C:(b + 1) * C],
                                                 start=(h == 0), stop=(h == 1))
                        last.then_inc(sum_done, 1)

            def mix_at(k, b, h):
                return mix[:, k, b * E + h * E // 2:b * E + (h + 1) * E // 2, :].rearrange("p e s -> p (e s)")

            in_turns(pe, turn)

        @block.scalar
        def _(act):
            def turn(i):
                for k in range(STEP_E):
                    g = i * STEP_E + k
                    wait(act, mixT_done, g + 1)
                    wait(act, sum_done, g - STEP_E + 1)
                    for h in range(2):
                        act.copy(mixT[:, k, h], ps_t[k % 2][h][0:HSL, 0:GT]).then_inc(mixT_ready, 1)

            turn(0)
            with act.Fori(1, TURNS_E) as i:
                turn(i)

        @block.vector
        def _(dve):
            def hot_of(g, k):
                wait(dve, mix_ready, g - STEP_E + 1)
                at = place[:, bass.ds(g * GB * E, GB * E)].rearrange("p (n o) -> p n o", o=1)
                dve.tensor_tensor(hot[:, k], w["slot_no"][0:T], at.to_broadcast((T, GB * E, CAP)),
                                  ALU.is_equal).then_inc(hot_done, 1)

            def turn(i, mix=True, mixing=True, ahead=True):
                for k in range(STEP_E):
                    if mix and (ahead or k + 2 < STEP_E):
                        hot_of(i * STEP_E + k + 2, (k + 2) % STEP_E)
                    if mixing:
                        g = (i - 1) * STEP_E + k
                        dve.wait_ge(sum_done, g + 1)
                        wait(dve, h2_in[k], 16 * i)
                        wait(dve, out_stored[k], 16 * (i - 1))
                        for n in range(2):
                            dve.tensor_tensor(out[:, k, 2 * n:2 * n + 2],
                                              ps_c[k % 2][n][0:T, :].rearrange("p (b c) -> p b c", b=2),
                                              h2[:, k, 2 * n:2 * n + 2], ALU.add).then_inc(out_ready, 1)

            hot_of(0, 0)
            hot_of(1, 1)
            turn(0, mixing=False)
            turn(1)
            with dve.Fori(2, TURNS_E - 1) as i:
                turn(i)
            turn(TURNS_E - 1, ahead=False)
            turn(TURNS_E, mix=False)


def build(nc, A, result):
    scratch = {
        "taps": nc.dram_tensor("taps_scratch", (1, LPAD), F32).ap(),
        "kern": nc.dram_tensor("kern_scratch", (C, LPAD), F32).ap(),
        "h1": nc.dram_tensor("h1_scratch", (T, B, C), F32).ap(),
        "y": nc.dram_tensor("y_scratch", (T, B, C), F32).ap(),
        "h2": nc.dram_tensor("h2_scratch", (T, B, C), F32).ap(),
        "rows": nc.dram_tensor("rows_scratch", (P, CC * E, B * CAP), F32).ap(),
        "slots": nc.dram_tensor("slots_scratch", (SL, B, C), F32).ap(),
    }
    with ExitStack() as ctx:
        def sb(name, shape, dt=F32):
            return ctx.enter_context(nc.sbuf_tensor(name, shape, dt))

        far_space = ExitStack()
        hankel = {"space": far_space, "loaded": [ctx.enter_context(nc.semaphore(f"toep_loaded{n}"))
                                                 for n in range(HANKEL_SLOTS)]}
        with nc.sbuf_tensor("xn", [T, B, C], F32) as xn:
            phase_tokens(nc, A, scratch, xn, hankel)
            raw1 = far_space.enter_context(nc.sbuf_tensor("raw_w1", [P, CC, HID], F32, side="right"))
            phase_states(nc, A, scratch, xn, hankel, raw1)
        far_space.close()
        with nc.sbuf_tensor("raw_w2", [P, HC, HID], F32, side="right") as raw2:
            raw = {"w1": raw1, "w2": raw2}
        place = sb("place", [T, B * E])
        gate = sb("gate", [T, B * E])
        w = {"ident": sb("ident", [P, P]), "earlier": sb("earlier", [T, T], BF16),
             "slot_no": sb("slot_no", [P, GB * E, CAP]), "rank": sb("rank", [P, GB, E])}
        with ExitStack() as space:
            d = expert_buffers(nc, space)
        d |= {n: ctx.enter_context(nc.semaphore(f"d_{n}")) for n in ("first_in", "first_rows_in")}
        phase_router(nc, A, scratch, w, raw, xn, place, gate, d)
        phase_experts(nc, A, scratch, w, d)
        phase_combine(nc, scratch, w, place, gate, result)


_INS = ["x", "L0_tok_Wv", "L0_tok_bv", "L0_tok_Wo", "L0_tok_bo", "L0_tok_decay_w", "L0_attn_log_dt",
        "L0_attn_log_A_real", "L0_attn_A_imag", "L0_attn_C", "L0_attn_D", "L0_ffn_rW1", "L0_ffn_rb1", "L0_ffn_rW2",
        "L0_ffn_rb2", "L0_ffn_rW3", "L0_ffn_rb3", "L0_ffn_eW1", "L0_ffn_eb1", "L0_ffn_eW2", "L0_ffn_eb2"]


def kernel(**inputs):
    import numpy as _np
    import concourse.bacc as _bacc
    from concourse.bass_utils import run_bass_kernel_spmd as _run

    nc = _bacc.Bacc("TRN2", target_bir_lowering=False, num_devices=1)
    arrays, args = {}, {}
    for name in _INS:
        a = _np.ascontiguousarray(inputs[name])
        arrays[f"in_{name}"] = a
        args[name] = nc.dram_tensor(f"in_{name}", a.shape, mybir.dt.from_np(a.dtype), kind="ExternalInput").ap()
    result = nc.dram_tensor("result", (B, T, C), F32, kind="ExternalOutput").ap()
    build(nc, args, result)
    r = _run(nc, [arrays], core_ids=[0])
    return r.results[0]["result"]
```
